# Optimizing a Trainium2 kernel written in Bass

```python
import numpy as np
import jax
import jax.numpy as jnp

def _softmax(x, axis=-1):
    return jax.nn.softmax(x, axis=axis)

def _gelu(x):
    return jax.nn.gelu(x, approximate=True)

def _silu(x):
    return jax.nn.silu(x)

def _sigmoid(x):
    return jax.nn.sigmoid(x)

def _layernorm(x, axis=-1, eps=1e-05):
    m = jnp.mean(x, axis=axis, keepdims=True)
    v = jnp.var(x, axis=axis, keepdims=True)
    return (x - m) / jnp.sqrt(v + eps)

def _scatter_add(tgt, idx, src, axis=0):
    return tgt.at[idx].add(src)

def _segment_sum(src, seg, n):
    return jax.ops.segment_sum(src, seg, n)
kernel_name = 'mk_early_fusion_d2_tok_img1024_r4_685913'

def setup_inputs(seed: int=0):
    np.random.seed(seed)
    _w = jnp.asarray

    def _rec_inputs():
        import jax
        import jax.numpy as jnp
        _rk = jax.random.key(seed)
        x = -0.00016672 + 0.999947 * jax.random.normal(jax.random.fold_in(_rk, 1), (16, 3, 96, 96), jnp.float32)
        txt = 0.434251 + 1.14597 * jax.random.normal(jax.random.fold_in(_rk, 2), (16, 128, 256), jnp.float32)
        return (x, txt)
    x, txt = _rec_inputs()

    def _L0_tok_setup():
        import jax, jax.numpy as jnp
        import numpy as np
        DIM = 256
        IMG = 96
        P = 16
        C = 3
        TEMP = 10000.0
        EPS = 1e-05
        PATCH_DIM = C * P * P
        HP = IMG // P

        def layernorm(x, gamma, beta):
            mu = jnp.mean(x, axis=-1, keepdims=True)
            var = jnp.var(x, axis=-1, keepdims=True)
            return (x - mu) * jax.lax.rsqrt(var + EPS) * gamma + beta

        def posemb_sincos_2d(h, w, dim, dtype):
            y, x = jnp.meshgrid(jnp.arange(h), jnp.arange(w), indexing='ij')
            omega = jnp.arange(dim // 4, dtype=jnp.float32) / (dim // 4 - 1)
            omega = 1.0 / TEMP ** omega
            y = y.reshape(-1)[:, None] * omega[None, :]
            x = x.reshape(-1)[:, None] * omega[None, :]
            pe = jnp.concatenate((jnp.sin(x), jnp.cos(x), jnp.sin(y), jnp.cos(y)), axis=1)
            return pe.astype(dtype)
        key = jax.random.key(seed)
        ks = jax.random.split(key, 8)
        B = 64
        img = jax.random.normal(ks[0], (B, C, IMG, IMG), dtype=jnp.float32)
        cls_token = jax.random.normal(ks[1], (1, 1, DIM), dtype=jnp.float32)
        cls_pos_embedding = jax.random.normal(ks[2], (1, 1, DIM), dtype=jnp.float32)
        ln1_g = jnp.ones((PATCH_DIM,), jnp.float32)
        ln1_b = jnp.zeros((PATCH_DIM,), jnp.float32)
        W = jax.random.normal(ks[3], (PATCH_DIM, DIM), dtype=jnp.float32) / np.sqrt(PATCH_DIM)
        bias = jnp.zeros((DIM,), jnp.float32)
        ln2_g = jnp.ones((DIM,), jnp.float32)
        ln2_b = jnp.zeros((DIM,), jnp.float32)
        return {'img': img, 'cls_token': cls_token, 'cls_pos_embedding': cls_pos_embedding, 'ln1_g': ln1_g, 'ln1_b': ln1_b, 'W': W, 'bias': bias, 'ln2_g': ln2_g, 'ln2_b': ln2_b}
    _L0_tok_all = _L0_tok_setup()
    _L0_tok_in = {k: v for k, v in _L0_tok_all.items() if k in ('cls_token', 'cls_pos_embedding', 'ln1_g', 'ln1_b', 'W', 'bias', 'ln2_g', 'ln2_b')}
    del _L0_tok_all

    def _L0_attn_setup():
        import jax, jax.numpy as jnp
        import numpy as np
        D_MODEL = 256
        STATE_DIM = 16
        BATCH = 32
        SEQ = 512

        def _selective_scan(delta, A, B, C):

            def step(state, inp):
                delta_t, B_t, C_t = inp
                state = jnp.exp(A * delta_t) * state + B_t
                y = jnp.sum(state * C_t, axis=-1)
                return (state, y)
            b = delta.shape[0]
            init = jnp.zeros((b, A.shape[0]), dtype=delta.dtype)
            xs = (jnp.swapaxes(delta, 0, 1), jnp.swapaxes(B, 0, 1), jnp.swapaxes(C, 0, 1))
            _, ys = jax.lax.scan(step, init, xs)
            return jnp.swapaxes(ys, 0, 1)
        key = jax.random.key(seed)
        k_x, k_win, k_bin, k_wout, k_bout = jax.random.split(key, 5)
        proj_dim = 2 * D_MODEL + 3 * STATE_DIM
        x = jax.random.normal(k_x, (BATCH, SEQ, D_MODEL), dtype=jnp.float32)
        W_in = jax.random.normal(k_win, (D_MODEL, proj_dim), dtype=jnp.float32) * 0.02
        b_in = jnp.zeros((proj_dim,), dtype=jnp.float32)
        W_out = jax.random.normal(k_wout, (D_MODEL, D_MODEL), dtype=jnp.float32) * 0.02
        b_out = jnp.zeros((D_MODEL,), dtype=jnp.float32)
        A_log = -jnp.log(jnp.arange(1, STATE_DIM + 1, dtype=jnp.float32))
        return {'x': x, 'W_in': W_in, 'b_in': b_in, 'A_log': A_log, 'W_out': W_out, 'b_out': b_out}
    _L0_attn_all = _L0_attn_setup()
    _L0_attn_in = {k: v for k, v in _L0_attn_all.items() if k in ('W_in', 'b_in', 'A_log', 'W_out', 'b_out')}
    del _L0_attn_all

    def _L0_ffn_setup():
        import jax, jax.numpy as jnp
        import numpy as np
        D_MODEL = 256
        FFN_DIM = 512
        NUM_EXPERTS = 8
        NUM_GROUPS = 4
        EXPERTS_PER_GROUP = NUM_EXPERTS // NUM_GROUPS
        TOP_K = 2
        GROUPS_TOP_K = 1
        EPS = 1e-09

        def _topk_normalized(scores, k):
            vals, idx = jax.lax.top_k(scores, k)
            vals = vals / (jnp.sum(vals, axis=-1, keepdims=True) + EPS)
            return (vals, idx)
        key = jax.random.key(seed)
        ks = jax.random.split(key, 6)
        B, S = (2, 256)
        x = jax.random.normal(ks[0], (B, S, D_MODEL), dtype=jnp.float32)
        sd = 0.02
        macro_w = jax.random.normal(ks[1], (D_MODEL, NUM_GROUPS), dtype=jnp.float32) * sd
        micro_w = jax.random.normal(ks[2], (NUM_GROUPS, D_MODEL, EXPERTS_PER_GROUP), dtype=jnp.float32) * sd
        gate_w = jax.random.normal(ks[3], (NUM_EXPERTS, D_MODEL, FFN_DIM), dtype=jnp.float32) * sd
        up_w = jax.random.normal(ks[4], (NUM_EXPERTS, D_MODEL, FFN_DIM), dtype=jnp.float32) * sd
        down_w = jax.random.normal(ks[5], (NUM_EXPERTS, FFN_DIM, D_MODEL), dtype=jnp.float32) * sd
        return {'x': x, 'macro_w': macro_w, 'micro_w': micro_w, 'gate_w': gate_w, 'up_w': up_w, 'down_w': down_w}
    _L0_ffn_all = _L0_ffn_setup()
    _L0_ffn_in = {k: v for k, v in _L0_ffn_all.items() if k in ('macro_w', 'micro_w', 'gate_w', 'up_w', 'down_w')}
    del _L0_ffn_all

    def _L1_attn_setup():
        import jax, jax.numpy as jnp
        import numpy as np
        THETA = 10000.0

        def _rope(t):
            T, d = (t.shape[-2], t.shape[-1])
            freqs = 1.0 / THETA ** (jnp.arange(0, d, 2, dtype=jnp.float32) / d)
            ang = jnp.arange(T, dtype=jnp.float32)[:, None] * freqs[None, :]
            ang = jnp.repeat(ang, 2, axis=-1)
            cos, sin = (jnp.cos(ang), jnp.sin(ang))
            x = t.reshape(t.shape[:-1] + (d // 2, 2))
            x1, x2 = (x[..., 0], x[..., 1])
            rot = jnp.stack([-x2, x1], axis=-1).reshape(t.shape)
            return t * cos + rot * sin
        key = jax.random.key(seed)
        ks = jax.random.split(key, 5)
        B, T, C = (4, 512, 256)
        s = 0.02
        return {'x': jax.random.normal(ks[0], (B, T, C), dtype=jnp.float32), 'Wq': jax.random.normal(ks[1], (C, C), dtype=jnp.float32) * s, 'bq': jnp.zeros((C,), dtype=jnp.float32), 'Wk': jax.random.normal(ks[2], (C, C), dtype=jnp.float32) * s, 'bk': jnp.zeros((C,), dtype=jnp.float32), 'Wv': jax.random.normal(ks[3], (C, C), dtype=jnp.float32) * s, 'bv': jnp.zeros((C,), dtype=jnp.float32), 'Wf': jax.random.normal(ks[4], (C, C), dtype=jnp.float32) * s, 'bf': jnp.zeros((C,), dtype=jnp.float32)}
    _L1_attn_all = _L1_attn_setup()
    _L1_attn_in = {k: v for k, v in _L1_attn_all.items() if k in ('Wq', 'bq', 'Wk', 'bk', 'Wv', 'bv', 'Wf', 'bf')}
    del _L1_attn_all

    def _L1_ffn_setup():
        import jax, jax.numpy as jnp
        import numpy as np
        B, S, D, H, E, K = (4, 512, 256, 1024, 4, 2)
        key = jax.random.key(seed)
        ks = jax.random.split(key, 7)
        s1 = 1.0 / np.sqrt(D)
        s2 = 1.0 / np.sqrt(H)
        return {'x': jax.random.normal(ks[0], (B, S, D), jnp.float32), 'w1': jax.random.uniform(ks[1], (E, D, H), jnp.float32, -s1, s1), 'b1': jax.random.uniform(ks[2], (E, H), jnp.float32, -s1, s1), 'w2': jax.random.uniform(ks[3], (E, H, D), jnp.float32, -s2, s2), 'b2': jax.random.uniform(ks[4], (E, D), jnp.float32, -s2, s2), 'wr': jax.random.uniform(ks[5], (D, E), jnp.float32, -s1, s1), 'br': jax.random.uniform(ks[6], (E,), jnp.float32, -s1, s1)}
    _L1_ffn_all = _L1_ffn_setup()
    _L1_ffn_in = {k: v for k, v in _L1_ffn_all.items() if k in ('w1', 'b1', 'w2', 'b2', 'wr', 'br')}
    del _L1_ffn_all
    return {'x': x, 'txt': txt, 'L0_tok_cls_token': _L0_tok_in['cls_token'], 'L0_tok_cls_pos_embedding': _L0_tok_in['cls_pos_embedding'], 'L0_tok_ln1_g': _L0_tok_in['ln1_g'], 'L0_tok_ln1_b': _L0_tok_in['ln1_b'], 'L0_tok_W': _L0_tok_in['W'], 'L0_tok_bias': _L0_tok_in['bias'], 'L0_tok_ln2_g': _L0_tok_in['ln2_g'], 'L0_tok_ln2_b': _L0_tok_in['ln2_b'], 'L0_attn_W_in': _L0_attn_in['W_in'], 'L0_attn_b_in': _L0_attn_in['b_in'], 'L0_attn_A_log': _L0_attn_in['A_log'], 'L0_attn_W_out': _L0_attn_in['W_out'], 'L0_attn_b_out': _L0_attn_in['b_out'], 'L0_ffn_macro_w': _L0_ffn_in['macro_w'], 'L0_ffn_micro_w': _L0_ffn_in['micro_w'], 'L0_ffn_gate_w': _L0_ffn_in['gate_w'], 'L0_ffn_up_w': _L0_ffn_in['up_w'], 'L0_ffn_down_w': _L0_ffn_in['down_w'], 'L1_attn_Wq': _L1_attn_in['Wq'], 'L1_attn_bq': _L1_attn_in['bq'], 'L1_attn_Wk': _L1_attn_in['Wk'], 'L1_attn_bk': _L1_attn_in['bk'], 'L1_attn_Wv': _L1_attn_in['Wv'], 'L1_attn_bv': _L1_attn_in['bv'], 'L1_attn_Wf': _L1_attn_in['Wf'], 'L1_attn_bf': _L1_attn_in['bf'], 'L1_ffn_w1': _L1_ffn_in['w1'], 'L1_ffn_b1': _L1_ffn_in['b1'], 'L1_ffn_w2': _L1_ffn_in['w2'], 'L1_ffn_b2': _L1_ffn_in['b2'], 'L1_ffn_wr': _L1_ffn_in['wr'], 'L1_ffn_br': _L1_ffn_in['br']}

def reference(x, txt, L0_tok_cls_token, L0_tok_cls_pos_embedding, L0_tok_ln1_g, L0_tok_ln1_b, L0_tok_W, L0_tok_bias, L0_tok_ln2_g, L0_tok_ln2_b, L0_attn_W_in, L0_attn_b_in, L0_attn_A_log, L0_attn_W_out, L0_attn_b_out, L0_ffn_macro_w, L0_ffn_micro_w, L0_ffn_gate_w, L0_ffn_up_w, L0_ffn_down_w, L1_attn_Wq, L1_attn_bq, L1_attn_Wk, L1_attn_bk, L1_attn_Wv, L1_attn_bv, L1_attn_Wf, L1_attn_bf, L1_ffn_w1, L1_ffn_b1, L1_ffn_w2, L1_ffn_b2, L1_ffn_wr, L1_ffn_br):
    import jax
    import jax.numpy as jnp

    def _L0_tok_ref(img, cls_token, cls_pos_embedding, ln1_g, ln1_b, W, bias, ln2_g, ln2_b):
        import jax, jax.numpy as jnp
        import numpy as np
        DIM = 256
        IMG = 96
        P = 16
        C = 3
        TEMP = 10000.0
        EPS = 1e-05
        PATCH_DIM = C * P * P
        HP = IMG // P

        def layernorm(x, gamma, beta):
            mu = jnp.mean(x, axis=-1, keepdims=True)
            var = jnp.var(x, axis=-1, keepdims=True)
            return (x - mu) * jax.lax.rsqrt(var + EPS) * gamma + beta

        def posemb_sincos_2d(h, w, dim, dtype):
            y, x = jnp.meshgrid(jnp.arange(h), jnp.arange(w), indexing='ij')
            omega = jnp.arange(dim // 4, dtype=jnp.float32) / (dim // 4 - 1)
            omega = 1.0 / TEMP ** omega
            y = y.reshape(-1)[:, None] * omega[None, :]
            x = x.reshape(-1)[:, None] * omega[None, :]
            pe = jnp.concatenate((jnp.sin(x), jnp.cos(x), jnp.sin(y), jnp.cos(y)), axis=1)
            return pe.astype(dtype)
        b = img.shape[0]
        x = img.reshape(b, C, HP, P, HP, P)
        x = jnp.transpose(x, (0, 2, 4, 3, 5, 1))
        x = x.reshape(b, HP, HP, PATCH_DIM)
        x = layernorm(x, ln1_g, ln1_b)
        x = jnp.einsum('bhwp,pd->bhwd', x, W) + bias
        x = layernorm(x, ln2_g, ln2_b)
        pe = posemb_sincos_2d(HP, HP, DIM, x.dtype)
        x = x.reshape(b, HP * HP, DIM) + pe[None]
        cls_tokens = jnp.broadcast_to(cls_token + cls_pos_embedding, (b, 1, DIM))
        return jnp.concatenate((cls_tokens, x), axis=1)

    def _L0_attn_ref(x, W_in, b_in, A_log, W_out, b_out):
        import jax, jax.numpy as jnp
        import numpy as np
        D_MODEL = 256
        STATE_DIM = 16
        BATCH = 32
        SEQ = 512

        def _selective_scan(delta, A, B, C):

            def step(state, inp):
                delta_t, B_t, C_t = inp
                state = jnp.exp(A * delta_t) * state + B_t
                y = jnp.sum(state * C_t, axis=-1)
                return (state, y)
            b = delta.shape[0]
            init = jnp.zeros((b, A.shape[0]), dtype=delta.dtype)
            xs = (jnp.swapaxes(delta, 0, 1), jnp.swapaxes(B, 0, 1), jnp.swapaxes(C, 0, 1))
            _, ys = jax.lax.scan(step, init, xs)
            return jnp.swapaxes(ys, 0, 1)
        xz = jnp.einsum('bsd,dp->bsp', x, W_in) + b_in
        d, n = (D_MODEL, STATE_DIM)
        xm = xz[..., :d]
        z = xz[..., d:2 * d]
        Bm = xz[..., 2 * d:2 * d + n]
        Cm = xz[..., 2 * d + n:2 * d + 2 * n]
        delta = jax.nn.softplus(xz[..., 2 * d + 2 * n:])
        A = -jnp.exp(A_log)
        y = _selective_scan(delta, A, Bm, Cm)
        y = y[..., None] * jax.nn.gelu(z, approximate=False)
        return jnp.einsum('bsd,de->bse', y, W_out) + b_out

    def _L0_ffn_ref(x, macro_w, micro_w, gate_w, up_w, down_w):
        import jax, jax.numpy as jnp
        import numpy as np
        D_MODEL = 256
        FFN_DIM = 512
        NUM_EXPERTS = 8
        NUM_GROUPS = 4
        EXPERTS_PER_GROUP = NUM_EXPERTS // NUM_GROUPS
        TOP_K = 2
        GROUPS_TOP_K = 1
        EPS = 1e-09

        def _topk_normalized(scores, k):
            vals, idx = jax.lax.top_k(scores, k)
            vals = vals / (jnp.sum(vals, axis=-1, keepdims=True) + EPS)
            return (vals, idx)
        B, S, D = x.shape
        T = B * S
        xf = x.reshape(T, D)
        macro_scores = jax.nn.sigmoid(xf @ macro_w)
        mv, mi = _topk_normalized(macro_scores, GROUPS_TOP_K)
        macro_full = jnp.sum(jax.nn.one_hot(mi, NUM_GROUPS, dtype=xf.dtype) * mv[..., None], axis=1)
        micro_scores = jax.nn.sigmoid(jnp.einsum('td,gde->tge', xf, micro_w))
        uv, ui = _topk_normalized(micro_scores, TOP_K)
        micro_full = jnp.sum(jax.nn.one_hot(ui, EXPERTS_PER_GROUP, dtype=xf.dtype) * uv[..., None], axis=2)
        w = (macro_full[:, :, None] * micro_full).reshape(T, NUM_EXPERTS)
        gate = jax.nn.silu(jnp.einsum('td,edf->tef', xf, gate_w))
        up = jnp.einsum('td,edf->tef', xf, up_w)
        h = gate * up
        out = jnp.einsum('te,tef,efd->td', w, h, down_w)
        return out.reshape(B, S, D)

    def _L1_attn_ref(x, Wq, bq, Wk, bk, Wv, bv, Wf, bf):
        import jax, jax.numpy as jnp
        import numpy as np
        THETA = 10000.0

        def _rope(t):
            T, d = (t.shape[-2], t.shape[-1])
            freqs = 1.0 / THETA ** (jnp.arange(0, d, 2, dtype=jnp.float32) / d)
            ang = jnp.arange(T, dtype=jnp.float32)[:, None] * freqs[None, :]
            ang = jnp.repeat(ang, 2, axis=-1)
            cos, sin = (jnp.cos(ang), jnp.sin(ang))
            x = t.reshape(t.shape[:-1] + (d // 2, 2))
            x1, x2 = (x[..., 0], x[..., 1])
            rot = jnp.stack([-x2, x1], axis=-1).reshape(t.shape)
            return t * cos + rot * sin
        B, T, C = x.shape
        Q = _rope(x @ Wq.T + bq)
        K = _rope(x @ Wk.T + bk)
        V = x @ Wv.T + bv
        A = jnp.einsum('btd,bsd->bts', Q, K) / jnp.sqrt(jnp.float32(C))
        causal = jnp.tril(jnp.ones((T, T), dtype=bool))
        A = jnp.where(causal, A, -jnp.inf)
        A = jax.nn.softmax(A, axis=-1)
        out = jnp.einsum('bts,bsd->btd', A, V)
        return out @ Wf.T + bf

    def _L1_ffn_ref(x, w1, b1, w2, b2, wr, br):
        import jax, jax.numpy as jnp
        import numpy as np
        B, S, D, H, E, K = (4, 512, 256, 1024, 4, 2)
        Bx, Sx, Dx = x.shape
        xf = x.reshape(-1, Dx)
        logits = xf @ wr + br
        topk_vals, topk_idx = jax.lax.top_k(logits, K)
        gates = jax.nn.softmax(topk_vals, axis=-1)
        h = jax.nn.gelu(jnp.einsum('nd,edh->enh', xf, w1) + b1[:, None, :], approximate=False)
        y = jnp.einsum('enh,ehd->end', h, w2) + b2[:, None, :]
        c = jnp.einsum('eh,ehd->ed', jax.nn.gelu(b1, approximate=False), w2) + b2
        c_sum = c.sum(axis=0)
        yt = jnp.transpose(y, (1, 0, 2))
        y_sel = jnp.take_along_axis(yt, topk_idx[:, :, None], axis=1)
        c_sel = c[topk_idx]
        out = jnp.einsum('nk,nkd->nd', gates, y_sel - c_sel + c_sum[None, None, :])
        return out.reshape(Bx, Sx, Dx)
    h = _L0_tok_ref(x, L0_tok_cls_token, L0_tok_cls_pos_embedding, L0_tok_ln1_g, L0_tok_ln1_b, L0_tok_W, L0_tok_bias, L0_tok_ln2_g, L0_tok_ln2_b)
    h = jnp.concatenate([h, txt], axis=1)
    h = h + _L0_attn_ref(_layernorm(h, axis=-1), L0_attn_W_in, L0_attn_b_in, L0_attn_A_log, L0_attn_W_out, L0_attn_b_out)
    h = h + _L0_ffn_ref(_layernorm(h, axis=-1), L0_ffn_macro_w, L0_ffn_micro_w, L0_ffn_gate_w, L0_ffn_up_w, L0_ffn_down_w)
    h = h + _L1_attn_ref(_layernorm(h, axis=-1), L1_attn_Wq, L1_attn_bq, L1_attn_Wk, L1_attn_bk, L1_attn_Wv, L1_attn_bv, L1_attn_Wf, L1_attn_bf)
    h = h + _L1_ffn_ref(_layernorm(h, axis=-1), L1_ffn_w1, L1_ffn_b1, L1_ffn_w2, L1_ffn_b2, L1_ffn_wr, L1_ffn_br)
    return h

_drawn_inputs = setup_inputs


def setup_inputs(seed=0):
    import zlib

    import numpy as np

    out = dict(_drawn_inputs(seed))
    spreads = {'L0_tok_ln1_g': (1.0, 0.2),
     'L0_tok_ln1_b': (0.0, 0.1),
     'L0_tok_bias': (0.0, 0.1),
     'L0_tok_ln2_g': (1.0, 0.2),
     'L0_tok_ln2_b': (0.0, 0.1),
     'L0_attn_b_in': (0.0, 0.1),
     'L0_attn_b_out': (0.0, 0.1),
     'L1_attn_bq': (0.0, 0.8),
     'L1_attn_bk': (0.0, 2.0),
     'L1_attn_bv': (0.0, 0.285),
     'L1_attn_bf': (0.0, 0.1)}
    factors = {'L0_ffn_macro_w': 4.081,
     'L0_ffn_micro_w': 8.0,
     'L0_ffn_gate_w': 3.52,
     'L0_ffn_up_w': 3.506,
     'L0_ffn_down_w': 3.558,
     'L1_attn_Wq': 8.0,
     'L1_attn_Wk': 8.0,
     'L1_ffn_b1': 3.332,
     'L1_ffn_br': 2.876,
     'L1_ffn_b2': 2.692}
    for name, (base, spread) in spreads.items():
        noise = np.random.default_rng([zlib.crc32(name.encode()), seed]).standard_normal(out[name].shape)
        drawn = base * np.exp(spread * noise) if base else spread * noise
        out[name] = jnp.asarray(drawn.astype(out[name].dtype))
    for name, factor in factors.items():
        out[name] = (out[name] * factor).astype(out[name].dtype)
    return out
```

```python
from contextlib import ExitStack

import numpy as np

import concourse.bass as bass
from concourse import mybir

F32 = mybir.dt.float32
BF16 = mybir.dt.bfloat16
F16 = mybir.dt.float16
I32 = mybir.dt.int32
U32 = mybir.dt.uint32
ALU = mybir.AluOpType
ACT = mybir.ActivationFunctionType
AX = mybir.AxisListType.X
AXS = [mybir.AxisListType.X, mybir.AxisListType.XY]

P = 128
BATCH, TEXT, D = 16, 128, 256
GRID, PATCH, CH = 6, 16, 3
IMG = GRID * GRID + 1
SEQ = IMG + TEXT
PDIM = PATCH * PATCH * CH
PC = PDIM // P
KC = D // P
PER = 3
IT = -(-BATCH // PER)
IROWS = PER * IMG
IPAD = 112
LAST = BATCH - PER * (IT - 1)
NT = BATCH + IT
PB = IT * PER
NS = 16
SG = 3
SB = PB // SG
EPS = 1e-5
G0, E0, F0 = 4, 2, 512
SLOT0 = (BATCH * SEQ + G0 * (P - 1)) // P
W0N = 2 * KC * F0 + (F0 // P) * D
E1, F1, TOPK = 4, 1024, 2
SLOT1 = (TOPK * BATCH * SEQ + E1 * (P - 1)) // P
HF = F1 // F0
W1N = KC * F1 + (F1 // P) * D
W1W = E1 * W1N
PAY0 = D + E0 + 1
PAY1 = D + 2 * E1
TOKENS = NT * P
DUMP = 2 * TOKENS
RUNS = [(0, 6, P), (6, 6, P), (12, 4, P), (BATCH, IT - 1, IROWS), (NT - 1, 1, LAST * IMG)]
CW = 1024
NFULL = -(-BATCH * SEQ // P)
NCST = 2 * P + NT + 4 * NT + 4 * NFULL + SLOT1 + NT
NCOL = 22
NWS = KC * (96 + D + D + 12)
STOP = 5
SCALE = float(D) ** -0.5
NATT = 4 * KC * D + 3 * SEQ + P + SEQ
NSM1 = 4 * KC + (F1 // P) * E1 + E1 + D
AHEAD = 2
SAT = 17.0


def ceil_even(n):
    return n + n % 2


class Region:

    def __init__(self, t, words, at=0):
        self.t, self.words, self.at = t, words, at

    def take(self, shape, dt=F32):
        n = int(np.prod(shape))
        words = n if dt not in (BF16, F16) else ceil_even(n) // 2
        assert self.at + words <= self.words, (self.at, words, self.words)
        ap = self.t[:, self.at:self.at + words]
        self.at += ceil_even(words)
        if dt != F32:
            ap = ap.bitcast(dt)
        if len(shape) == 1:
            return ap
        names = "abcdef"[:len(shape)]
        kw = {c: s for c, s in zip(names[1:], shape[1:])}
        return ap.rearrange(f"p ({' '.join(names)}) -> p {' '.join(names)}", **kw)


class Chain:

    def __init__(self, eng, sem):
        self.eng, self.sem, self.n, self.loop = eng, sem, 0, None

    def link(self, ins):
        ins.then_inc(self.sem, 1)
        if self.loop is None:
            self.n += 1
            self.eng.wait_ge(self.sem, self.n)
        else:
            self.loop[1] += 1
            self.eng.wait_ge(self.sem, self.loop[0] * self.loop[2] + (self.n + self.loop[1]))

    def begin(self, i, per):
        self.loop = [i, 0, per]

    def end(self, trips):
        assert self.loop[1] == self.loop[2], self.loop
        self.n += trips * self.loop[2]
        self.loop = None


Y_BANKS = (6, 7, 0)


def token_tiles(eng, body, pair_of=None):
    with eng.Fori(0, BATCH // 2) as i:
        if pair_of is not None:
            pair_of[0] = i
        body(2 * i, P, 0)
        body(2 * i + 1, P, 1)
    with eng.Fori(0, (IT - 2) // 2) as j:
        body(BATCH + 2 * j, IROWS, 0)
        body(BATCH + 1 + 2 * j, IROWS, 1)
    body(NT - 2, IROWS, 0)
    body(NT - 1, LAST * IMG, 1)


def pipelined(eng, n, body):
    pairs = (n - 3) // 2
    body(0, 0, 0)
    body(1, 1, 0)
    with eng.Fori(1, 1 + pairs) as j:
        body(2 * j, 0, j)
        body(2 * j + 1, 1, j)
    for i in range(2 + 2 * pairs, n):
        body(i, i % 2, i // 2)


def known(i, value):
    return isinstance(i, int) and i == value


def batch_cols(view, t, rows):
    if rows == P:
        return view[:, :, bass.ds(t * SEQ + IMG, TEXT)]
    nb = rows // IMG
    part = view[:, :, bass.ds((t - BATCH) * (PER * SEQ), PER * SEQ)]
    return part.rearrange("p k (b s) -> p k b s", s=SEQ)[:, :, 0:nb, 0:IMG]


def wait_from(eng, sem, value):
    if isinstance(value, int) and value <= 0:
        return
    eng.wait_ge(sem, value)


def build(nc, txt, patches, wtok, cols, rows_a, consts, pe_table, wsmall, w0, wattn, rows_f, w1, wsmall1,
          b1rows, out, stop=99):
    with ExitStack() as ctx:
        def sb(name, shape, dt=F32):
            return ctx.enter_context(nc.sbuf_tensor(name, shape, dt))

        def sem(name):
            return ctx.enter_context(nc.semaphore(name))

        h = sb("h", [P, NT, D])
        XW, YW = G0 * E0 * W0N, 16900
        X = sb("X", [P, XW])
        Y = sb("Y", [P, YW])
        stage = sb("stage", [P, 2, CW])
        cst = sb("cst", [P, NCST])
        ccols = sb("ccols", [P, NCOL])
        wsm = sb("wsm", [P, NWS])
        upper = sb("upper", [P, P], BF16)
        onesb = sb("onesb", [P, P], BF16)
        onesf = sb("onesf", [P, P])
        stats = sb("stats", [P, NT, 2, 6])
        mv = sb("mv", [P, NT, 2])
        rs4 = sb("rs4", [P, 4, NT])
        var, std, rstd, newt = (rs4[:, i, :] for i in range(4))
        yv = sb("yv", [P, NT])
        ra = sb("ra", [P, 12, NT])
        rb = sb("rb", [P, 12, NT])
        rc = sb("rc", [P, 12, NT])
        oh = sb("oh", [P, TOPK, 4, NT])
        ohb = sb("ohb", [P, 4, NT], BF16)
        raf = ra.rearrange("p g t -> p (g t)")
        sm = sb("sm", [P, 32])
        hscale = sb("hscale", [P, 4])
        amax = sb("amax", [P, 4])
        gates = sb("gates", [P, TOPK, NT])
        posf = sb("posf", [P, TOPK, NT])
        pos = sb("pos", [P, TOPK, NT], U32)
        slotf = sb("slotf", [P, SLOT1])
        slote = sb("slote", [P, SLOT1], I32)
        PS = ctx.enter_context(nc.psum_tensor("PS", [P, 8, 512], F32))

        xs0 = nc.dram_tensor("xs0", [SLOT0 * P, PAY0], F32).ap()
        ys0 = nc.dram_tensor("ys0", [DUMP + 1, D], F32).ap()
        xs1 = nc.dram_tensor("xs1", [SLOT1 * P, PAY1], F32).ap()
        ys1 = nc.dram_tensor("ys1", [DUMP + 1, D], F32).ap()
        dest = sb("dest", [P, SLOT1], U32)

        k_ident = cst[:, 0:P]
        k_upper = cst[:, P:2 * P]
        at = 2 * P
        k_valid = cst[:, at:at + NT]; at += NT
        k_reset = cst[:, at:at + 4 * NT]; at += 4 * NT
        k_fill = cst[:, at:at + 4 * NFULL].rearrange("p (g k) -> p g k", g=4); at += 4 * NFULL
        k_slot = cst[:, at:at + SLOT1]; at += SLOT1
        k_place = cst[:, at:at + NT]
        c_g1, c_b1 = ccols[:, 0:6], ccols[:, 6:12]
        c_bz, c_bq, c_bk = ccols[:, 12:14], ccols[:, 14:16], ccols[:, 16:18]
        c_bcd, c_alog, c_nega = ccols[0:96, 18:19], ccols[0:96, 19:20], ccols[0:96, 20:21]
        rw = Region(wsm, NWS)
        wbcd = rw.take([KC, 96])
        wz = rw.take([KC, D])
        wout = rw.take([KC, D])
        wr0 = rw.take([KC, 12])

        ry = Region(Y, YW)
        pt = ry.take([IT, PDIM])
        rs = Region(Y, YW)
        GS = SB * SEQ
        sB, sC, sD, sA = (rs.take([GS]) for _ in range(4))
        assert rs.at <= ry.at
        wt = ry.take([PC, D])
        sS = Region(Y, YW, rs.at).take([GS])
        rows = ry.take([6, D])
        r_g2, r_b2, r_tb, r_cls, r_cpos, r_bout = (rows[:, i, :] for i in range(6))
        pay_at = ry.at
        xT = ry.take([KC, PB * SEQ])
        pay = Region(Y, YW, pay_at).take([NT, PAY0])
        pT = ry.take([2, PC, IPAD])
        xn = ry.take([2, D])
        x2T = xn.rearrange("p a (k r) -> p a k r", k=KC)
        gT = ry.take([2, KC, P])
        zt = ry.take([PAY1])
        petab = gT.rearrange("p a k n -> p (a k n)")[:, 0:D]
        rd = Region(Y, YW)
        xin = rd.take([2, PAY0])
        ybuf = rd.take([2, D])
        wall = rd.take([SLOT0, 2])
        xh = rd.take([2, KC, P], F16)
        xl = rd.take([2, KC, P], F16)
        sg = rd.take([2, F0])
        hh = rd.take([2, F0])
        hTh = rd.take([2, 4, P], F16)
        hTl = rd.take([2, 4, P], F16)
        back = rd.take([NT, D])
        rx = Region(X, XW)
        wq, wk, wv, wf = (rx.take([KC, D]) for _ in range(4))
        tab = X[:, 4 * KC * D:NATT]
        k_cos, k_sin, k_nsin = (tab[:, i * SEQ:(i + 1) * SEQ] for i in range(3))
        k_maskA, k_maskB = tab[:, 3 * SEQ:3 * SEQ + P], tab[:, 3 * SEQ + P:4 * SEQ + P]
        rx.at = ceil_even(NATT)
        rowsF = rx.take([2, D])
        xnF = rx.take([2, D])
        xTi = rx.take([KC, PB * IMG])
        xTb = rx.take([2, KC, SEQ])
        qkT = rx.take([2, 2, KC, SEQ])
        qT, kT = qkT[:, :, 0], qkT[:, :, 1]
        tcos = rx.take([2, KC, SEQ])
        tsin = rx.take([2, KC, SEQ])
        vb = rx.take([2, 2, D])
        sA1, sB1 = rx.take([P]), rx.take([SEQ])
        pA, pB = rx.take([P]), rx.take([SEQ])
        pT1, pT2 = rx.take([SEQ]), rx.take([SEQ - P])
        oTb = rx.take([KC, P])
        oTi = rx.take([KC, PB * IMG])
        nmax, smax, psum_, rsum = (rx.take([2]) for _ in range(4))
        rg = Region(X, XW)
        b1b = rg.take([E1 * F1])
        small1 = rg.take([NSM1])
        rs1 = Region(X, XW, rg.at - ceil_even(NSM1))
        wr1 = rs1.take([KC, 4])
        c_b1c = rs1.take([(F1 // P) * E1])
        c_br = rs1.take([E1])
        c_b2 = rs1.take([D])
        gb1 = rg.take([(F1 // P) * E1])
        gbh = rg.take([F1 // P, E1, 4], F16)
        gbl = rg.take([F1 // P, E1, 4], F16)
        cvec, rvec = rg.take([D]), rg.take([D])
        gT4 = Region(X, XW, rg.at).take([NT, P])
        back1 = rg.take([NT, D])
        pay1 = rg.take([NT, PAY1])
        back0 = pay1.rearrange("p t n -> p (t n)")[:, 0:NT * D].rearrange("p (t n) -> p t n", t=NT)
        wall1 = rg.take([SLOT1])
        x2G = rg.take([2, KC, P])
        x1in = rg.take([2, PAY1])
        y1buf = rg.take([2, D])
        x1h, x1l = rg.take([2, KC, P], F16), rg.take([2, KC, P], F16)
        mid1 = rg.take([2, F0])
        hh1 = rg.take([2, F0])
        h1Th, h1Tl = rg.take([2, 4, P], F16), rg.take([2, 4, P], F16)
        w1h = Y[:, 0:W1W // 2].bitcast(F16)
        w1l = Y[:, W1W // 2:W1W].bitcast(F16)
        w0h = X[:, 0:XW // 2].bitcast(F16)
        w0l = X[:, XW // 2:XW].bitcast(F16)

        text_loaded = sem("text_loaded")
        patches_loaded = sem("patches_loaded")
        small_loaded = sem("small_loaded")
        consts_ready = sem("consts_ready")
        zero_ready = sem("zero_ready")
        zeroed = sem("zeroed")
        zeroed1 = sem("zeroed1")
        pads_zeroed = sem("pads_zeroed")
        dve_done = sem("dve_done")
        act_done = sem("act_done")
        var_ready = sem("var_ready")
        std_ready = sem("std_ready")
        nega_ready = sem("nega_ready")
        patch_normed = sem("patch_normed")
        patch_tr = sem("patch_tr")
        patch_copied = sem("patch_copied")
        tokb_psum = sem("tokb_psum")
        wt_scaled = sem("wt_scaled")
        tok_psum = sem("tok_psum")
        tok_added = sem("tok_added")
        cls_ready = sem("cls_ready")
        tok_ready = sem("tok_ready")
        cls_placed = sem("cls_placed")
        xn_ready = sem("xn_ready")
        xn_tr = sem("xn_tr")
        xT_copied = sem("xT_copied")
        bcd_psum = sem("bcd_psum")
        bc_copied = sem("bc_copied")
        dl_copied = sem("dl_copied")
        abs_ready = sem("abs_ready")
        sp_ready = sem("sp_ready")
        delta_ready = sem("delta_ready")
        decay_ready = sem("decay_ready")
        sc_ready = sem("sc_ready")
        y_psum = sem("y_psum")
        z_psum = sem("z_psum")
        g_ready = sem("g_ready")
        o_psum = sem("o_psum")
        h_added = sem("h_added")
        hb_added = sem("hb_added")
        stage_full = [sem("stage_full0"), sem("stage_full1")]
        stage_free = sem("stage_free")
        w_high = sem("w_high")
        x2_copied = sem("x2_copied")
        stats_ready = sem("stats_ready")
        route_psum = sem("route_psum")
        logits_ready = sem("logits_ready")
        sig_ready = sem("sig_ready")
        choice_ready = sem("choice_ready")
        count_psum = sem("count_psum")
        pay_ready = sem("pay_ready")
        scattered = sem("scattered")
        x_in = [sem("x_in0"), sem("x_in1")]
        x_tr = sem("x_tr")
        x_w = sem("x_w")
        x_hi = sem("x_hi")
        x_lo = sem("x_lo")
        gate_psum = sem("gate_psum")
        up_psum = sem("up_psum")
        act_out = sem("act_out")
        h_ready = sem("h_ready")
        hT_psum = sem("hT_psum")
        hT_hi = sem("hT_hi")
        hT_lo = sem("hT_lo")
        y_done = sem("y_done")
        y_copied = sem("y_copied")
        y_out = [sem("y_out0"), sem("y_out1")]
        taken_back = [sem(f"taken_back{i}") for i in range(len(RUNS))]
        added_back = sem("added_back")
        out_written = sem("out_written")
        slots_ready = sem("slots_ready")
        amax_ready = sem("amax_ready")
        amax_row = sem("amax_row")
        amax_all = sem("amax_all")
        amax_psum = sem("amax_psum")
        scale_ready = sem("scale_ready")
        attn_loaded = sem("attn_loaded")
        xTi_copied = sem("xTi_copied")
        xTb_copied = sem("xTb_copied")
        xTb_image = sem("xTb_image")
        q_psum = sem("q_psum")
        k_psum = sem("k_psum")
        v_psum = sem("v_psum")
        rope_mul = sem("rope_mul")
        rope_done = sem("rope_done")
        v_copied = sem("v_copied")
        s_psum = sem("s_psum")
        s_max = sem("s_max")
        p_exp = sem("p_exp")
        p_normed = sem("p_normed")
        pt_psum = sem("pt_psum")
        pt_copied = sem("pt_copied")
        ot_psum = sem("ot_psum")
        ot_copied = sem("ot_copied")
        pr_psum = sem("pr_psum")
        bf_added = sem("bf_added")
        h3_added = sem("h3_added")
        experts1_loaded = sem("experts1_loaded")
        gb_ready = sem("gb_ready")
        gb_split = sem("gb_split")
        c_psum = sem("c_psum")
        c_ready = sem("c_ready")
        r_ready = sem("r_ready")
        gt_psum = sem("gt_psum")
        gt_copied = sem("gt_copied")
        gr_psum = sem("gr_psum")
        h4_added = sem("h4_added")
        biased = sem("biased")

        NSMALL = 6

        class Layer0:
            scale, unscale = hscale[:, 0:1], hscale[:, 1:2]
            tiles, before, experts = SLOT0, 0, G0
            rows_in, rows_out = xs0, ys0
            wh, wl, per_expert = w0h, w0l, E0 * W0N
            x, y, xhi, xlo, mid, act_, hi, lo = xin, ybuf, xh, xl, sg, hh, hTh, hTl

            def w_in(e, k, up):
                return e * W0N + (up * KC + k) * F0

            def w_out(e, c):
                return e * W0N + 2 * KC * F0 + c * D
            ups, y_banks = 2, (6, 6)

        class Layer1:
            scale, unscale = hscale[:, 2:3], hscale[:, 3:4]
            tiles, before, experts = SLOT1, SLOT0, E1
            rows_in, rows_out = xs1, ys1
            wh, wl, per_expert = w1h, w1l, W1N
            x, y, xhi, xlo, mid, act_, hi, lo = x1in, y1buf, x1h, x1l, mid1, hh1, h1Th, h1Tl

            def w_in(s, k, up):
                return (s * KC + k) * F0

            def w_out(s, c):
                return KC * F1 + (4 * s + c) * D
            ups, y_banks = 1, (6, 2)
        block = ctx.enter_context(nc.Block())

        def dump(sp):
            if stop == 1:
                sp.wait_ge(cls_placed, 48)
                sp.wait_ge(text_loaded, 16)
            if stop == 2:
                sp.wait_ge(hb_added, NT)
            if stop == 3:
                sp.wait_ge(added_back, len(RUNS))
            if stop == 4:
                sp.wait_ge(h3_added, NT)
                sp.wait_ge(stage_free, AHEAD + XW // CW + W1W // CW)
            n = store_out(sp)
            sp.wait_ge(out_written, 16 * n)

        def store_out(sp, n=0):
            for k, (t, tiles, r) in enumerate(RUNS):
                if stop > 4:
                    sp.wait_ge(added_back, len(RUNS) + 2 * (k + 1))
                if r == P:
                    sp.dma_start(out[t:t + tiles, IMG:SEQ, :].rearrange("b s d -> s b d"), h[:, t:t + tiles, :])\
                        .then_inc(out_written, 16)
                    n += 1
                    continue
                for b in range(PER * (t - BATCH), min(BATCH, PER * (t - BATCH + tiles))):
                    first = (b % PER) * IMG
                    sp.dma_start(out[b, 0:IMG, :], h[first:first + IMG, BATCH + b // PER, :]).then_inc(out_written, 16)
                    n += 1
            return n

        def act_dispatch(act, before, x2T_):
            def copies(t, slot, j):
                act.wait_ge(xn_tr, before[0] * NT + AHEAD + t + 1)
                nc.scalar.activation(x2T_[:, slot, :, :], PS[:, slot, 0:KC * P].rearrange("p (k r) -> p k r", k=KC),
                                     ACT.Copy).then_inc(x2_copied, 1)
            pipelined(act, NT, copies)

        def pe_route(pe, before, x2T_, pay_, weights, n):
            def product(t, slot):
                pe.wait_ge(x2_copied, before[1] * NT + t + 1)
                for k in range(KC):
                    ins = nc.tensor.matmul(PS[:, 6, bass.ds(t * n, n)], x2T_[:, slot, k, :], weights[:, k, :],
                                           start=(k == 0), stop=(k == KC - 1))
                ins.then_inc(route_psum, 1)

            for t in range(NT):
                pe.wait_ge(xn_ready, before[0] * NT + t + 1)
                for k in range(KC):
                    ins = nc.tensor.transpose(PS[:, t % 2, k * P:(k + 1) * P], pay_[:, t, k * P:(k + 1) * P], k_ident)
                ins.then_inc(xn_tr, 1)
                if t:
                    product(t - 1, (t - 1) % 2)
            product(NT - 1, (NT - 1) % 2)

        def pe_count(pe, done):
            pe.wait_ge(choice_ready, done + 1)
            flat = ohb.rearrange("p g t -> p (g t)")
            nc.tensor.matmul(PS[:, 7, 0:4 * NT], upper[:, :], flat, start=True, stop=True)
            nc.tensor.matmul(PS[:, 7, 128:128 + 4 * NT], onesb[:, :], flat, start=True, stop=True)\
                .then_inc(count_psum, 1)

        def dve_norm(dve, pay_):
            def norm(t, slot, j):
                nc.vector.tensor_scalar(pay_[:, bass.ds(t, 1), 0:D], h[:, bass.ds(t, 1), :], mv[:, bass.ds(t, 1), 0],
                                        rstd[:, bass.ds(t, 1)], ALU.subtract, ALU.mult).then_inc(xn_ready, 1)
            pipelined(dve, NT, norm)

        def moments_of_all(dve, chain, layer):
            dve.wait_ge(stats_ready, layer * NT)
            for t in range(NT):
                ins = nc.vector.bn_aggr(mv[:, t, :], stats[:, t, 0, :])
            chain.link(ins)

        def over(ap, n):
            return ap.unsqueeze(1).broadcast_to([P, n, NT])

        def first_max(chain, values, top, hot):
            chain.link(nc.vector.tensor_reduce(top, values.rearrange("p g t -> p t g"), AX, ALU.max))
            chain.link(nc.vector.tensor_tensor(hot, values, over(top, 4), ALU.is_equal))
            taken = newt
            chain.link(nc.vector.tensor_copy(taken, hot[:, 0, :]))
            for g in range(1, 4):
                chain.link(nc.vector.tensor_tensor(hot[:, g, :], hot[:, g, :], taken, ALU.is_gt))
                chain.link(nc.vector.tensor_tensor(taken, taken, hot[:, g, :], ALU.max))

        def sum_over(chain, out_, values):
            chain.link(nc.vector.tensor_reduce(out_, values.rearrange("p g t -> p t g"), AX, ALU.add))

        def positions(dve, chain, choices, tiles, done):
            hot = rc[:, 0:4, :]
            if choices == 2:
                chain.link(nc.vector.tensor_tensor(hot, oh[:, 0], oh[:, 1], ALU.add))
                chain.link(nc.vector.tensor_tensor(hot, hot, over(k_valid, 4), ALU.mult))
            else:
                chain.link(nc.vector.tensor_tensor(hot, oh[:, 0], over(k_valid, 4), ALU.mult))
            nc.vector.tensor_copy(ohb[:, :, :], hot).then_inc(choice_ready, 1)
            dve.wait_ge(count_psum, done + 1)
            before_, total, upto = rc[:, 0:4, :], rc[:, 4:8, :], rc[:, 8:12, :]
            flat = lambda ap: ap.rearrange("p g t -> p (g t)")
            nc.vector.tensor_copy(flat(before_), PS[:, 7, 0:4 * NT])
            chain.link(nc.vector.tensor_copy(flat(total), PS[:, 7, 128:128 + 4 * NT]))
            chain.link(nc.vector.tensor_tensor_scan(flat(upto), k_reset, flat(total), 0.0, ALU.mult, ALU.add))
            n_of = upto[:, :, NT - 1:NT].broadcast_to([P, 4, NFULL])
            full = raf[:, 0:4 * NFULL].rearrange("p (g k) -> p g k", g=4)
            chain.link(nc.vector.tensor_tensor(full, n_of, k_fill, ALU.is_gt))
            tl, st, sl = sm[:, 0:4], sm[:, 4:8], sm[:, 8:12]
            chain.link(nc.vector.tensor_reduce(tl, full, AX, ALU.add))
            chain.link(nc.vector.memset(st[:, 0:1], 0.0))
            for g in range(1, 4):
                chain.link(nc.vector.tensor_tensor(st[:, g:g + 1], st[:, g - 1:g], tl[:, g - 1:g], ALU.add))
            chain.link(nc.vector.tensor_scalar(sl, st, float(P), None, ALU.mult))
            chain.link(nc.vector.tensor_tensor(upto, upto, total, ALU.subtract))
            chain.link(nc.vector.tensor_tensor(before_, before_, upto, ALU.add))
            chain.link(nc.vector.tensor_tensor(before_, before_, sl.unsqueeze(2).broadcast_to([P, 4, NT]), ALU.add))
            for c in range(choices):
                chain.link(nc.vector.tensor_tensor(total, oh[:, c], before_, ALU.mult))
                sum_over(chain, posf[:, c, :], total)
            chain.link(nc.vector.tensor_copy(pos[:, 0:choices, :], posf[:, 0:choices, :]))
            sf = slotf[:, 0:tiles]
            chain.link(nc.vector.tensor_scalar(sf, k_slot[:, 0:tiles], st[:, 1:2], None, ALU.is_ge))
            for g in (2, 3):
                chain.link(nc.vector.scalar_tensor_tensor(out=sf, in0=k_slot[:, 0:tiles], scalar=st[:, g:g + 1],
                                                          in1=sf, op0=ALU.is_ge, op1=ALU.add))
            nc.vector.tensor_copy(slote[:, 0:tiles], sf).then_inc(slots_ready, 1)

        def dve_scale(dve, chain, weights, layer, bound):
            chain.link(nc.vector.tensor_reduce(amax[:, 0:1], weights, AXS[len(weights.shape) - 2], ALU.max,
                                               apply_absolute_value=True))
            bound(amax[:, 0:1])
            dve.sem_inc(amax_ready, 1)
            dve.wait_ge(amax_psum, 2 * layer + 1)
            nc.vector.tensor_reduce(amax[0:1, 1:2], PS[0:1, 3, 0:P], AX, ALU.max).then_inc(amax_row, 1)
            dve.wait_ge(amax_psum, 2 * layer + 2)
            top, scale_, un = amax[:, 2:3], hscale[:, 2 * layer:2 * layer + 1], hscale[:, 2 * layer + 1:2 * layer + 2]
            chain.link(nc.vector.tensor_copy(top, PS[:, 3, 256:257]))
            if layer == 0:
                chain.link(nc.vector.tensor_tensor(top, top, top, ALU.mult))
                chain.link(nc.vector.tensor_scalar(un, top, float(D * D) / 2 ** 15, 1e-20, ALU.mult, ALU.max))
            else:
                chain.link(nc.vector.tensor_scalar(un, top, 1.0 / 2 ** 15, 1e-20, ALU.mult, ALU.max))
            chain.link(nc.vector.reciprocal(scale_, un))
            dve.sem_inc(scale_ready, 1)

        def pe_scale(pe, layer):
            pe.wait_ge(amax_ready, layer + 1)
            nc.tensor.transpose(PS[0:1, 3, 0:P], amax[:, 0:1], k_ident).then_inc(amax_psum, 1)
            pe.wait_ge(amax_row, layer + 1)
            nc.tensor.matmul(PS[:, 3, 256:257], onesf[0:1, :], amax[0:1, 1:2], start=True, stop=True).then_inc(amax_psum, 1)

        def ffn_loads(sp, L):
            def load(i, slot, j):
                if not (isinstance(i, int) and i < 2):
                    sp.wait_ge(x_tr, L.before + i - 1)
                    sp.wait_ge(x_w, L.before + i - 1)
                sp.dma_start(L.x[:, slot, :], L.rows_in[bass.ds(i * P, P), :])\
                    .then_inc(x_in[slot], 16)
            pipelined(sp, L.tiles, load)

        def ffn_pe(pe, L):
            def transpose_x(i, slot, j):
                pe.wait_ge(x_in[slot], 16 * (j + (L.before + 1) // 2 + 1))
                for k in range(KC):
                    ins = nc.tensor.transpose(PS[:, 7, k * P:(k + 1) * P], L.x[:, slot, k * P:(k + 1) * P], k_ident)
                ins.then_inc(x_tr, 1)

            def products_in(i, s, base, slot):
                if s == 0:
                    pe.wait_ge(x_lo, L.before + i + 1)
                for u in range(L.ups):
                    n = 0
                    for k in range(KC):
                        off = base + L.w_in(s, k, u)
                        for x_, w_ in ((L.xhi, L.wh), (L.xhi, L.wl), (L.xlo, L.wh)):
                            ins = nc.tensor.matmul(PS[:, 2 * u + s, 0:F0], x_[:, slot, k, :], w_[:, bass.ds(off, F0)],
                                                   start=(n == 0), stop=(n == 3 * KC - 1))
                            n += 1
                    ins.then_inc(up_psum if u else gate_psum, 1)

            def transpose_h(i, s):
                pe.wait_ge(h_ready, 2 * (L.before + i) + s + 1)
                for c in range(4):
                    ins = nc.tensor.transpose(PS[:, 4 + s, c * P:(c + 1) * P], L.act_[:, s, c * P:(c + 1) * P], k_ident)
                ins.then_inc(hT_psum, 1)

            def product_out(i, s, base, slot):
                pe.wait_ge(hT_lo, 2 * (L.before + i) + s + 1)
                if s == 0:
                    wait_from(pe, y_copied, L.before + i + 1 - len(set(L.y_banks)))
                for c in range(4):
                    off = base + L.w_out(s, c)
                    for n, (h_, w_) in enumerate(((L.hi, L.wh), (L.hi, L.wl), (L.lo, L.wh))):
                        ins = nc.tensor.matmul(PS[:, L.y_banks[slot], 0:D], h_[:, s, c, :], w_[:, bass.ds(off, D)],
                                               start=(s == 0 and c == 0 and n == 0), stop=(s == 1 and c == 3 and n == 2))
                if s == 1:
                    ins.then_inc(y_done, 1)

            def base_of(i):
                return pe.value_load(slote[0:1, bass.ds(i, 1)], min_val=0, max_val=L.experts - 1) * L.per_expert

            carried = [None, None]

            def tile(i, slot, j):
                base = base_of(i)
                if known(i, 0):
                    transpose_x(0, 0, 0)
                products_in(i, 0, base, slot)
                if not known(i, 0):
                    last = carried[0] if slot == 1 or isinstance(i, int) and carried[1] == i - 1 else base_of(i - 1)
                    transpose_h(i - 1, 1)
                if not known(i, L.tiles - 1):
                    transpose_x(i + 1, 1 - slot, j + slot)
                if not known(i, 0):
                    product_out(i - 1, 0, last, 1 - slot)
                products_in(i, 1, base, slot)
                transpose_h(i, 0)
                if not known(i, 0):
                    product_out(i - 1, 1, last, 1 - slot)
                carried[:] = [base, i if isinstance(i, int) else None]
            pipelined(pe, L.tiles, tile)
            n = L.tiles - 1
            base = base_of(n)
            product_out(n, 0, base, n % 2)
            transpose_h(n, 1)
            product_out(n, 1, base, n % 2)

        def ffn_act(act, L):
            def split_x(i, slot):
                act.wait_ge(x_tr, L.before + i + 1)
                nc.scalar.activation(L.xhi[:, slot].rearrange("p k r -> p (k r)"), PS[:, 7, 0:KC * P], ACT.Copy).then_inc(x_hi, 1)

            def nonlinear(i, s):
                step = 2 * (L.before + i) + s + 1
                if L is Layer0:
                    act.wait_ge(gate_psum, step)
                    nc.scalar.activation(L.mid[:, s, :], PS[:, s, 0:F0], ACT.Silu).then_inc(act_out, 1)
                else:
                    act.wait_ge(biased, 2 * i + s + 1)
                    nc.scalar.activation(L.act_[:, s, :], L.mid[:, s, :], ACT.Gelu).then_inc(h_ready, 1)

            def split_h(i, s):
                act.wait_ge(hT_psum, 2 * (L.before + i) + s + 1)
                nc.scalar.activation(L.hi[:, s, :, :].rearrange("p c r -> p (c r)"), PS[:, 4 + s, 0:F0], ACT.Copy,
                                     scale=L.scale)\
                    .then_inc(hT_hi, 1)

            def copy_y(i, slot, j):
                act.wait_ge(y_done, L.before + i + 1)
                if not (isinstance(j, int) and j == 0):
                    act.wait_ge(y_out[slot], 16 * ((L.before + 1) // 2 + j))
                nc.scalar.activation(L.y[:, slot, :], PS[:, L.y_banks[slot], 0:D], ACT.Copy,
                                     scale=L.unscale if L is Layer0 else wall1[:, bass.ds(i, 1)]).then_inc(y_copied, 1)

            def tile(i, slot, j):
                if known(i, 0):
                    split_x(0, 0)
                if L is Layer0:
                    nonlinear(i, 0)
                if not known(i, 0):
                    split_h(i - 1, 1)
                if L is not Layer0:
                    nonlinear(i, 0)
                if not known(i, L.tiles - 1):
                    split_x(i + 1, 1 - slot)
                if L is Layer0:
                    nonlinear(i, 1)
                split_h(i, 0)
                if L is not Layer0:
                    nonlinear(i, 1)
                if not known(i, 0):
                    copy_y(i - 1, 1 - slot, j + slot - 1)
            pipelined(act, L.tiles, tile)
            n = L.tiles - 1
            split_h(n, 1)
            copy_y(n, n % 2, n // 2)

        def ffn_pool(pool, L):
            for i in range(L.tiles):
                pool.wait_ge(x_w, L.before + i + 1)
                pool.wait_ge(y_copied, L.before + i + 1)
                if L.before + i:
                    last = 1 - i % 2
                    pool.wait_ge(y_out[last], 16 * ((L.before + 1 - last) // 2 + (i + 1 - last) // 2))
                nc.gpsimd.indirect_dma_start(out=L.rows_out, out_offset=bass.IndirectOffsetOnAxis(ap=dest[:, i:i + 1], axis=0),
                                             in_=L.y[:, i % 2, :], in_offset=None).then_inc(y_out[i % 2], 16)

        def take_back(sp, L, choice, buffer, tile0, n, r, done):
            rows_ = L.rows_out[choice * TOKENS + tile0 * P:choice * TOKENS + (tile0 + n) * P, :]
            sp.dma_start(buffer[0:r, tile0:tile0 + n, :], rows_.rearrange("(t p) n -> p t n", p=P)[0:r, :, :])\
                .then_inc(done, 16)

        def ffn_dve(dve, L):
            def split_x(i, slot, j, e):
                dve.wait_ge(x_hi, L.before + i + 1)
                nc.vector.tensor_tensor(L.xlo[:, slot].rearrange("p k r -> p (k r)"), PS[:, 7, 0:KC * P],
                                        L.xhi[:, slot].rearrange("p k r -> p (k r)"), ALU.subtract).then_inc(x_lo, 1)
                dve.wait_ge(x_in[slot], 16 * (j + (L.before + 1) // 2 + 1))
                if L is Layer0:
                    nc.vector.tensor_copy(wall[:, bass.ds(i, 1), :], L.x[:, slot:slot + 1, D:D + E0])
                    nc.vector.tensor_copy(dest[:, bass.ds(i, 1)], L.x[:, slot, D + E0:PAY0]).then_inc(x_w, 1)
                else:
                    nc.vector.tensor_scalar(wall1[:, bass.ds(i, 1)], L.x[:, slot, bass.ds(e + D, 1)], L.unscale, None, ALU.mult)
                    nc.vector.tensor_copy(dest[:, bass.ds(i, 1)], L.x[:, slot, bass.ds(e + (D + E1), 1)]).then_inc(x_w, 1)

            def combine(i, s, bias):
                step = 2 * (L.before + i) + s + 1
                if L is Layer0:
                    dve.wait_ge(x_w, i + 1)
                    dve.wait_ge(up_psum, step)
                    dve.wait_ge(act_out, step)
                    nc.vector.scalar_tensor_tensor(out=L.act_[:, s, :].unsqueeze(1), in0=PS[:, 2 + s, 0:F0].unsqueeze(1),
                                                   scalar=wall[:, bass.ds(i, 1), s], in1=L.mid[:, s, :].unsqueeze(1),
                                                   op0=ALU.mult, op1=ALU.mult).then_inc(h_ready, 1)
                else:
                    dve.wait_ge(gate_psum, step)
                    nc.vector.tensor_tensor(L.mid[:, s, :], PS[:, s, 0:F0], b1b[:, bass.ds(bias + s * F0, F0)],
                                            ALU.add).then_inc(biased, 1)

            def split_h(i, s):
                dve.wait_ge(hT_hi, 2 * (L.before + i) + s + 1)
                nc.vector.scalar_tensor_tensor(out=L.lo[:, s, :, :].rearrange("p c r -> p (c r)"), in0=PS[:, 4 + s, 0:F0],
                                               scalar=L.scale, in1=L.hi[:, s, :, :].rearrange("p c r -> p (c r)"),
                                               op0=ALU.mult, op1=ALU.subtract).then_inc(hT_lo, 1)

            def expert_of(i):
                if L is Layer0:
                    return None
                return dve.value_load(slote[0:1, bass.ds(i, 1)], min_val=0, max_val=E1 - 1)

            carried = [None, None]

            def tile(i, slot, j):
                e = carried[0] if slot == 1 or isinstance(i, int) and carried[1] == i else expert_of(i)
                if known(i, 0):
                    split_x(0, 0, 0, e)
                bias = None if L is Layer0 else e * F1
                combine(i, 0, bias)
                if not known(i, 0):
                    split_h(i - 1, 1)
                if not known(i, L.tiles - 1):
                    following = expert_of(i + 1)
                    split_x(i + 1, 1 - slot, j + slot, following)
                    carried[:] = [following, i + 1 if isinstance(i, int) else None]
                combine(i, 1, bias)
                split_h(i, 0)
            pipelined(dve, L.tiles, tile)
            split_h(L.tiles - 1, 1)

        def sp_rest(sp):
            sp.wait_ge(scattered, 16 * NT)
            ffn_loads(sp, Layer0)
            for k in range(2):
                sp.wait_ge(y_out[k], 16 * ((SLOT0 + 1 - k) // 2))
            for k, (t, n, r) in enumerate(RUNS):
                take_back(sp, Layer0, 0, back, t, n, r, taken_back[k])
            if stop > 3:
                sp_attention(sp)
            if stop > 4:
                sp_experts1(sp)

        def act_rest(act, roots):
            roots(4)
            act_dispatch(act, (1, 0), x2T)
            act.wait_ge(logits_ready, 1)
            nc.scalar.activation(rb[:, :, :], ra[:, :, :], ACT.Sigmoid).then_inc(sig_ready, 1)
            act.wait_ge(scale_ready, 1)
            ffn_act(act, Layer0)
            if stop > 3:
                act_attention(act, roots)
            if stop > 4:
                act_experts1(act, roots)

        def pe_rest(pe):
            pe_route(pe, (1, 0), x2T, pay, wr0, 12)
            pe_count(pe, 0)
            pe.wait_ge(stage_free, AHEAD + XW // CW)
            pe_scale(pe, 0)
            pe.wait_ge(slots_ready, 1)
            ffn_pe(pe, Layer0)
            if stop > 3:
                pe_attention(pe)
            if stop > 4:
                pe_experts1(pe)

        def tile_rows(t):
            return P if t < BATCH else IROWS if t < NT - 1 else LAST * IMG

        def pool_rest(pool):
            pool.wait_ge(zeroed, 16)
            pool.wait_ge(pay_ready, 1)
            for t in range(NT):
                r = tile_rows(t)
                nc.gpsimd.indirect_dma_start(out=xs0, out_offset=bass.IndirectOffsetOnAxis(ap=pos[0:r, 0, t:t + 1], axis=0),
                                             in_=pay[0:r, t, :], in_offset=None).then_inc(scattered, 16)
            ffn_pool(pool, Layer0)
            if stop > 3:
                pool_attention(pool)
            if stop > 4:
                pool_experts1(pool)

        def dve_rest(dve, chain, inverse_roots):
            moments_of_all(dve, chain, 1)
            inverse_roots()
            dve_norm(dve, pay)
            dve.wait_ge(route_psum, NT)
            nc.vector.tensor_copy(upper[:, :], k_upper)
            nc.vector.tensor_copy(ra[:, :, :], PS[:, 6, 0:12 * NT].rearrange("p (t g) -> p g t", g=12))\
                .then_inc(logits_ready, 1)
            dve.wait_ge(logits_ready, 1)
            top, score, a, b = rc[:, 8, :], rc[:, 9, :], rc[:, 10, :], rc[:, 11, :]
            chain.link(nc.vector.tensor_scalar(rc[:, 0:4, :], ra[:, 0:4, :], SAT, None, ALU.min))
            first_max(chain, rc[:, 0:4, :], top, oh[:, 0])
            dve.wait_ge(sig_ready, 1)
            chain.link(nc.vector.tensor_reduce(score, rb[:, 0:4, :].rearrange("p g t -> p t g"), AX, ALU.max))
            chain.link(nc.vector.tensor_scalar(a, score, 1e-9, None, ALU.add))
            chain.link(nc.vector.reciprocal(a, a))
            chain.link(nc.vector.tensor_tensor(score, score, a, ALU.mult))
            u = ra[:, 0:2, :]
            micro = rb[:, 4:12, :].rearrange("p (g e) t -> p e g t", e=E0)
            for e in range(E0):
                chain.link(nc.vector.tensor_tensor(rc[:, 0:4, :], micro[:, e], oh[:, 0], ALU.mult))
                sum_over(chain, u[:, e, :], rc[:, 0:4, :])
            chain.link(nc.vector.tensor_tensor(a, u[:, 0, :], u[:, 1, :], ALU.add))
            chain.link(nc.vector.tensor_scalar(a, a, 1e-9, None, ALU.add))
            chain.link(nc.vector.reciprocal(a, a))
            chain.link(nc.vector.tensor_tensor(a, a, score, ALU.mult))
            for e in range(E0):
                chain.link(nc.vector.tensor_tensor(pay[:, :, D + e], u[:, e, :], a, ALU.mult))
            chain.link(nc.vector.tensor_copy(pay[:, :, D + E0], k_place))
            positions(dve, chain, 1, SLOT0, 0)
            dve.sem_inc(pay_ready, 1)
            dve.wait_ge(stage_free, AHEAD + XW // CW)
            gate_up = w0h.rearrange("p (e n) -> p e n", e=G0 * E0)[:, :, 0:2 * KC * F0]
            dve_scale(dve, chain, gate_up, 0, lambda a_: None)
            ffn_dve(dve, Layer0)
            for k, (t, n, r) in enumerate(RUNS):
                dve.wait_ge(taken_back[k], 16)
                nc.vector.tensor_tensor(h[0:r, t:t + n, :], h[0:r, t:t + n, :], back[0:r, t:t + n, :], ALU.add)\
                    .then_inc(added_back, 1)
                dve.wait_ge(added_back, k + 1)
                for i in range(t, t + n):
                    nc.vector.bn_stats(stats[:, i, 0, :], h[:, i, :]).then_inc(stats_ready, 1)
            if stop > 3:
                dve_attention(dve, chain, inverse_roots)
            if stop > 4:
                dve_experts1(dve, chain, inverse_roots)

        NF = 2 * NT

        def sp_attention(sp):
            sp.wait_ge(y_done, SLOT0)
            sp.dma_start(X[:, 0:NATT], wattn).then_inc(attn_loaded, 16)
            sp.dma_start(rowsF.rearrange("p a n -> p (a n)"), rows_f.broadcast_to([P, 2 * D])).then_inc(attn_loaded, 16)
            first = XW // CW
            sp.wait_ge(added_back, len(RUNS))
            with sp.Fori(0, W1W // CW // 2) as n:
                for k in range(2):
                    sp.wait_ge(stage_free, first + 2 * n + (k + 1))
                    sp.dma_start(stage[:, k, :], w1[:, bass.ds((2 * n + k) * CW, CW)]).then_inc(stage_full[k], 16)

        def heads(eng, body):
            body(0, 0)
            body(1, 1)
            with eng.Fori(1, BATCH // 2 - 1) as j:
                body(2 * j, 0)
                body(2 * j + 1, 1)
            body(BATCH - 2, 0)
            body(BATCH - 1, 1)

        def pe_attention(pe):
            pe.wait_ge(attn_loaded, 32)
            for n in range(IT):
                pe.wait_ge(xn_ready, NF + n + 1)
                if n:
                    pe.wait_ge(xTi_copied, n)
                for k in range(KC):
                    ins = nc.tensor.transpose(PS[:, 7, k * P:(k + 1) * P], xnF[:, n % 2, k * P:(k + 1) * P], k_ident)
                ins.then_inc(xn_tr, 1)

            def text(b, slot):
                pe.wait_ge(xn_ready, NF + IT + b + 1)
                if known(b, 0):
                    pe.wait_ge(xTi_copied, IT)
                else:
                    pe.wait_ge(xTb_copied, b)
                for k in range(KC):
                    ins = nc.tensor.transpose(PS[:, 7, k * P:(k + 1) * P], xnF[:, slot, k * P:(k + 1) * P], k_ident)
                ins.then_inc(xn_tr, 1)

            def project(b, slot):
                pe.wait_ge(xTb_copied, b + 1)
                pe.wait_ge(xTb_image, b + 1)
                for bank, w_, done in ((0, wq, q_psum), (1, wk, k_psum)):
                    for m in range(KC):
                        for k in range(KC):
                            ins = nc.tensor.matmul(PS[:, bank, m * SEQ:(m + 1) * SEQ], w_[:, k, m * P:(m + 1) * P],
                                                   xTb[:, slot, k, :], start=(k == 0), stop=(k == KC - 1))
                    ins.then_inc(done, 1)
                wait_from(pe, v_copied, b)
                for a, (c0, c1) in enumerate(((0, P), (P, SEQ))):
                    for k in range(KC):
                        ins = nc.tensor.matmul(PS[0:c1 - c0, 2, a * D:(a + 1) * D], xTb[:, slot, k, c0:c1], wv[:, k, :],
                                               start=(k == 0), stop=(k == KC - 1))
                ins.then_inc(v_psum, 1)

            def scores(b, slot):
                pe.wait_ge(rope_done, b + 1)
                for o_, q0, q1, k1 in ((0, 0, P, P), (P, P, SEQ, SEQ)):
                    for m in range(KC):
                        ins = nc.tensor.matmul(PS[0:q1 - q0, 3, o_:o_ + k1], qT[:, slot, m, q0:q1], kT[:, slot, m, 0:k1],
                                               start=(m == 0), stop=(m == KC - 1))
                ins.then_inc(s_psum, 1)

            def transpose_p(b, slot):
                pe.wait_ge(p_normed, b + 1)
                nc.tensor.transpose(PS[:, 4, 0:P], pA, k_ident)
                nc.tensor.transpose(PS[:, 4, P:SEQ], pB[0:SEQ - P, 0:P], k_ident[0:SEQ - P, 0:SEQ - P])
                nc.tensor.transpose(PS[0:SEQ - P, 4, SEQ:2 * SEQ - P], pB[0:SEQ - P, P:SEQ],
                                    k_ident[0:SEQ - P, 0:SEQ - P]).then_inc(pt_psum, 1)

            def values(b, slot):
                pe.wait_ge(pt_copied, b + 1)
                pe.wait_ge(v_copied, b + 1)
                for m in range(KC):
                    nc.tensor.matmul(PS[:, 5, m * SEQ:(m + 1) * SEQ], vb[:, slot, 0, m * P:(m + 1) * P], pT1,
                                     start=True, stop=False)
                    ins = nc.tensor.matmul(PS[:, 5, m * SEQ + P:(m + 1) * SEQ], vb[0:SEQ - P, slot, 1, m * P:(m + 1) * P],
                                           pT2[0:SEQ - P, :], start=False, stop=True)
                ins.then_inc(ot_psum, 1)

            def out_text(b, slot):
                pe.wait_ge(ot_copied, 2 * b + 2)
                wait_from(pe, h3_added, b)
                for m in range(KC):
                    ins = nc.tensor.matmul(PS[:, 6, 0:D], oTb[:, m, :], wf[:, m, :], start=(m == 0), stop=(m == KC - 1))
                ins.then_inc(pr_psum, 1)

            text(0, 0)
            text(1, 1)
            project(0, 0)

            def batch(b, slot):
                scores(b, slot)
                if not known(b, BATCH - 1):
                    project(b + 1, 1 - slot)
                transpose_p(b, slot)
                if not known(b, 0):
                    out_text(b - 1, 1 - slot)
                if not (isinstance(b, int) and b >= BATCH - 2):
                    text(b + 2, slot)
                values(b, slot)
            heads(pe, batch)
            out_text(BATCH - 1, 1)
            for n in range(IT):
                r = tile_rows(BATCH + n)
                pe.wait_ge(h3_added, BATCH + n)
                for m in range(KC):
                    ins = nc.tensor.matmul(PS[0:r, 6, 0:D], oTi[:, m, n * IROWS:n * IROWS + r], wf[:, m, :],
                                           start=(m == 0), stop=(m == KC - 1))
                ins.then_inc(pr_psum, 1)

        def act_attention(act, roots):
            roots(5)
            for n in range(IT):
                act.wait_ge(xn_tr, AHEAD + NF + n + 1)
                nc.scalar.activation(xTi[:, :, n * IROWS:(n + 1) * IROWS],
                                     PS[:, 7, 0:KC * P].rearrange("p (k r) -> p k r", k=KC)[:, :, 0:IROWS],
                                     ACT.Copy).then_inc(xTi_copied, 1)

            def text(b, slot):
                act.wait_ge(xn_tr, AHEAD + NF + IT + b + 1)
                nc.scalar.activation(xTb[:, slot, :, IMG:SEQ], PS[:, 7, 0:KC * P].rearrange("p (k r) -> p k r", k=KC),
                                     ACT.Copy).then_inc(xTb_copied, 1)

            def exps(b):
                act.wait_ge(s_max, b + 1)
                nc.scalar.activation(pA, sA1, ACT.Exp, bias=nmax[:, 0:1], scale=SCALE, accum_out=psum_[:, 0:1])
                nc.scalar.activation(pB[0:SEQ - P, :], sB1[0:SEQ - P, :], ACT.Exp, bias=nmax[0:SEQ - P, 1:2], scale=SCALE,
                                     accum_out=psum_[0:SEQ - P, 1:2]).then_inc(p_exp, 1)

            def copy_pt(b):
                act.wait_ge(pt_psum, b + 1)
                nc.scalar.activation(pT1, PS[:, 4, 0:SEQ], ACT.Copy)
                nc.scalar.activation(pT2[0:SEQ - P, :], PS[0:SEQ - P, 4, SEQ:2 * SEQ - P], ACT.Copy).then_inc(pt_copied, 1)

            def copy_ot(b):
                act.wait_ge(ot_psum, b + 1)
                o_ = PS[:, 5, 0:KC * SEQ].rearrange("p (k r) -> p k r", k=KC)
                nc.scalar.activation(oTb, o_[:, :, IMG:SEQ], ACT.Copy).then_inc(ot_copied, 1)
                nc.scalar.activation(oTi[:, :, bass.ds(b * IMG, IMG)], o_[:, :, 0:IMG], ACT.Copy).then_inc(ot_copied, 1)

            def chunk(n, k, j):
                act.wait_ge(stage_full[k], 16 * (XW // CW // 2 + j + 1))
                nc.scalar.activation(w1h[:, bass.ds(n * CW, CW)], stage[:, k, :], ACT.Copy).then_inc(w_high, 1)

            text(0, 0)
            text(1, 1)

            def batch(b, slot):
                exps(b)
                copy_pt(b)
                if not (isinstance(b, int) and b >= BATCH - 2):
                    text(b + 2, slot)
                copy_ot(b)
                chunk(b, slot, b // 2 if isinstance(b, int) else None)
            def batches(b, slot):
                batch(b, slot)
            def run(b, slot, j):
                exps(b)
                copy_pt(b)
                if not (isinstance(b, int) and b >= BATCH - 2):
                    text(b + 2, slot)
                copy_ot(b)
                chunk(b, slot, j)
            run(0, 0, 0)
            run(1, 1, 0)
            with act.Fori(1, BATCH // 2 - 1) as j:
                run(2 * j, 0, j)
                run(2 * j + 1, 1, j)
            run(BATCH - 2, 0, BATCH // 2 - 1)
            run(BATCH - 1, 1, BATCH // 2 - 1)

        def pool_attention(pool):
            pool.wait_ge(attn_loaded, 32)
            pool.wait_ge(xTi_copied, IT)

            def image(b):
                pool.wait_ge(xn_tr, AHEAD + NF + IT + b + 1)
                nc.gpsimd.tensor_copy(xTb[:, b % 2, :, 0:IMG], xTi[:, :, b * IMG:(b + 1) * IMG]).then_inc(xTb_image, 1)

            def rope(b):
                pool.wait_ge(rope_mul, 2 * b + 2)
                nc.gpsimd.tensor_tensor(qkT[:, b % 2], tcos, tsin, ALU.add).then_inc(rope_done, 1)

            def bias(b):
                pool.wait_ge(xn_ready, NF + IT + b + 1)
                nc.gpsimd.tensor_tensor(h[:, b, :], h[:, b, :], rowsF[:, 1, :], ALU.add).then_inc(bf_added, 1)

            def low(n):
                k = n % 2
                pool.wait_ge(w_high, XW // CW + n + 1)
                nc.gpsimd.tensor_tensor(w1l[:, n * CW:(n + 1) * CW], stage[:, k, :], w1h[:, n * CW:(n + 1) * CW],
                                        ALU.subtract).then_inc(stage_free, 1)
            for n in range(IT):
                pool.wait_ge(xn_ready, NF + n + 1)
                nc.gpsimd.tensor_tensor(h[:, BATCH + n, :], h[:, BATCH + n, :], rowsF[:, 1, :], ALU.add)\
                    .then_inc(bf_added, 1)
            image(0)
            image(1)
            bias(0)
            bias(1)
            rope(0)
            for b in range(BATCH):
                if b < BATCH - 1:
                    rope(b + 1)
                if b < BATCH - 2:
                    image(b + 2)
                    bias(b + 2)
                low(b)

        def dve_attention(dve, chain, inverse_roots):
            moments_of_all(dve, chain, 2)
            inverse_roots()
            dve.wait_ge(y_done, SLOT0)

            def norm(n, t, slot):
                dve.wait_ge(xn_tr, NF + n + 1)
                nc.vector.tensor_scalar(xnF[:, slot:slot + 1, :], h[:, bass.ds(t, 1), :], mv[:, bass.ds(t, 1), 0],
                                        rstd[:, bass.ds(t, 1)], ALU.subtract, ALU.mult).then_inc(xn_ready, 1)
            for n in range(IT):
                norm(n, BATCH + n, n % 2)
            dve.wait_ge(attn_loaded, 32)

            def rope(b):
                for i, (bank, bias, done) in enumerate(((0, c_bq, q_psum), (1, c_bk, k_psum))):
                    dve.wait_ge(done, b + 1)
                    for m in range(KC):
                        nc.vector.scalar_tensor_tensor(out=tcos[:, i, m, :], in0=PS[:, bank, m * SEQ:(m + 1) * SEQ],
                                                       scalar=bias[:, m:m + 1], in1=k_cos, op0=ALU.add, op1=ALU.mult)
                        ins = nc.vector.scalar_tensor_tensor(
                            out=tsin[:, i, m, :], in0=PS[:, bank, (1 - m) * SEQ:(2 - m) * SEQ],
                            scalar=bias[:, 1 - m:2 - m], in1=k_sin if m else k_nsin, op0=ALU.add, op1=ALU.mult)
                    ins.then_inc(rope_mul, 1)

            def copy_v(b, slot):
                dve.wait_ge(v_psum, b + 1)
                nc.vector.tensor_tensor(vb[:, slot, 0, :], PS[:, 2, 0:D], rowsF[:, 0, :], ALU.add)
                nc.vector.tensor_tensor(vb[0:SEQ - P, slot, 1, :], PS[0:SEQ - P, 2, D:2 * D], rowsF[0:SEQ - P, 0, :],
                                        ALU.add).then_inc(v_copied, 1)

            def maxima(b):
                dve.wait_ge(s_psum, b + 1)
                nc.vector.tensor_tensor(sA1, PS[:, 3, 0:P], k_maskA, ALU.add)
                chain.link(nc.vector.tensor_tensor_reduce(sB1[0:SEQ - P, :], PS[0:SEQ - P, 3, P:P + SEQ],
                                                          k_maskB[0:SEQ - P, :], 1.0, -3e38, ALU.add, ALU.max,
                                                          smax[0:SEQ - P, 1:2]))
                chain.link(nc.vector.tensor_reduce(smax[:, 0:1], sA1, AX, ALU.max))
                nc.vector.tensor_scalar(nmax, smax, -SCALE, None, ALU.mult).then_inc(s_max, 1)

            def normalise_p(b):
                dve.wait_ge(p_exp, b + 1)
                chain.link(nc.vector.reciprocal(rsum, psum_))
                nc.vector.tensor_scalar(pA, pA, rsum[:, 0:1], None, ALU.mult)
                nc.vector.tensor_scalar(pB[0:SEQ - P, :], pB[0:SEQ - P, :], rsum[0:SEQ - P, 1:2], None, ALU.mult)\
                    .then_inc(p_normed, 1)

            def add_text(b):
                dve.wait_ge(bf_added, IT + b + 1)
                dve.wait_ge(pr_psum, b + 1)
                hb = h[:, bass.ds(b, 1), :]
                nc.vector.tensor_tensor(hb, PS[:, 6, 0:D].unsqueeze(1), hb, ALU.add).then_inc(h3_added, 1)
                dve.wait_ge(h3_added, b + 1)
                nc.vector.bn_stats(stats[:, bass.ds(b, 1), 0, :], hb).then_inc(stats_ready, 1)

            chain.link(nc.vector.memset(smax[:, :], 0.0))
            chain.link(nc.vector.memset(psum_[:, :], 1.0))
            norm(IT, 0, 0)
            norm(IT + 1, 1, 1)
            rope(0)
            copy_v(0, 0)

            def batch(b, slot):
                maxima(b)
                if not (isinstance(b, int) and b >= BATCH - 2):
                    norm(b + (IT + 2), b + 2, slot)
                normalise_p(b)
                if not known(b, BATCH - 1):
                    rope(b + 1)
                    copy_v(b + 1, 1 - slot)
                if not known(b, 0):
                    add_text(b - 1)
            body = batch
            body(0, 0)
            body(1, 1)
            with dve.Fori(1, BATCH // 2 - 1) as j:
                chain.begin(j - 1, 6)
                body(2 * j, 0)
                body(2 * j + 1, 1)
                chain.end(BATCH // 2 - 2)
            body(BATCH - 2, 0)
            body(BATCH - 1, 1)
            add_text(BATCH - 1)
            for n in range(IT):
                r = tile_rows(BATCH + n)
                dve.wait_ge(pr_psum, BATCH + n + 1)
                hb = h[0:r, BATCH + n, :]
                nc.vector.tensor_tensor(hb, PS[0:r, 6, 0:D], hb, ALU.add).then_inc(h3_added, 1)
                dve.wait_ge(h3_added, BATCH + n + 1)
                nc.vector.bn_stats(stats[:, BATCH + n, 0, :], h[:, BATCH + n, :]).then_inc(stats_ready, 1)

        def sp_experts1(sp):
            sp.wait_ge(h3_added, NT)
            sp.dma_start(b1b, b1rows.broadcast_to([P, E1 * F1])).then_inc(experts1_loaded, 16)
            sp.dma_start(small1, wsmall1).then_inc(experts1_loaded, 16)
            sp.wait_ge(scattered, 16 * 3 * NT)
            ffn_loads(sp, Layer1)
            for k in range(2):
                sp.wait_ge(y_out[k], 16 * ((SLOT0 + 1 - k) // 2 + (SLOT1 + 1 - k) // 2))
            for k, (t, n, r) in enumerate(RUNS):
                take_back(sp, Layer1, 0, back0, t, n, r, taken_back[k])
                take_back(sp, Layer1, 1, back1, t, n, r, taken_back[k])

        def act_experts1(act, roots):
            roots(6)
            act_dispatch(act, (3, 1), x2G)
            act.wait_ge(experts1_loaded, 32)
            nc.scalar.activation(gb1, c_b1c, ACT.Gelu).then_inc(gb_ready, 1)
            act.wait_ge(logits_ready, 3)
            nc.scalar.activation(rb[:, 0, :], rb[:, 1, :], ACT.Exp).then_inc(sig_ready, 1)
            for t in range(NT):
                act.wait_ge(gt_psum, t + 1)
                nc.scalar.activation(gT4[0:4, t, :], PS[0:4, t % 2, 0:P], ACT.Copy).then_inc(gt_copied, 1)
            act.wait_ge(scale_ready, 2)
            ffn_act(act, Layer1)

        def pe_experts1(pe):
            pe.wait_ge(experts1_loaded, 32)
            pe_route(pe, (3, 1), x2G, pay1, wr1, 4)
            pe.wait_ge(stage_free, AHEAD + XW // CW + W1W // CW)
            pe.wait_ge(gb_split, 1)
            n = 0
            for e in range(E1):
                for c in range(F1 // P):
                    off = e * W1N + KC * F1 + c * D
                    for g_, w_ in ((gbh, w1h), (gbh, w1l), (gbl, w1h)):
                        ins = nc.tensor.matmul(PS[0:4, 5, 0:D], g_[:, c, e, :], w_[:, off:off + D], start=(n == 0),
                                               stop=(n == 3 * E1 * (F1 // P) - 1))
                        n += 1
            ins.then_inc(c_psum, 1)
            pe.wait_ge(c_ready, 1)
            nc.tensor.matmul(PS[0:4, 4, 0:D], onesf[0:4, 0:4], cvec[0:4, :], start=True, stop=True).then_inc(c_psum, 1)
            pe_count(pe, 1)
            pe.wait_ge(r_ready, 1)
            for t in range(NT):
                if t >= 2:
                    pe.wait_ge(gt_copied, t - 1)
                nc.tensor.transpose(PS[0:4, t % 2, 0:P], rb[:, 4:8, t], k_ident).then_inc(gt_psum, 1)
                if t >= 1:
                    pe_gate_rows(pe, t - 1)
            pe_gate_rows(pe, NT - 1)
            pe.wait_ge(h4_added, NT)
            pe_scale(pe, 1)
            pe.wait_ge(slots_ready, 2)
            ffn_pe(pe, Layer1)

        def pe_gate_rows(pe, t):
            pe.wait_ge(gt_copied, t + 1)
            if t >= 2:
                pe.wait_ge(h4_added, t - 1)
            nc.tensor.matmul(PS[:, 2 + t % 2, 0:D], gT4[0:4, t, :], rvec[0:4, :], start=True, stop=True).then_inc(gr_psum, 1)

        def pool_experts1(pool):
            pool.wait_ge(zeroed1, 16)
            pool.wait_ge(pay_ready, 2)
            for t in range(NT):
                r = tile_rows(t)
                for c in range(TOPK):
                    nc.gpsimd.indirect_dma_start(
                        out=xs1, out_offset=bass.IndirectOffsetOnAxis(ap=pos[0:r, c, t:t + 1], axis=0),
                        in_=pay1[0:r, t, :], in_offset=None).then_inc(scattered, 16)
            ffn_pool(pool, Layer1)

        def dve_experts1(dve, chain, inverse_roots):
            moments_of_all(dve, chain, 3)
            inverse_roots()
            dve_norm(dve, pay1)
            dve.wait_ge(experts1_loaded, 32)
            chain.link(nc.vector.memset(gbh, 0.0))
            chain.link(nc.vector.memset(gbl, 0.0))
            dve.wait_ge(gb_ready, 1)
            for e in range(E1):
                ins = nc.vector.tensor_copy(gbh[:, :, e, e], gb1.rearrange("p (c e) -> p c e", e=E1)[:, :, e])
            chain.link(ins)
            for e in range(E1):
                ins = nc.vector.tensor_tensor(gbl[:, :, e, e], gb1.rearrange("p (c e) -> p c e", e=E1)[:, :, e],
                                              gbh[:, :, e, e], ALU.subtract)
            ins.then_inc(gb_split, 1)
            dve.wait_ge(route_psum, 2 * NT)
            lg, l2 = ra[:, 0:4, :], ra[:, 4:8, :]
            nc.vector.tensor_tensor(lg, PS[:, 6, 0:4 * NT].rearrange("p (t g) -> p g t", g=4),
                                    c_br.unsqueeze(2).broadcast_to([P, 4, NT]), ALU.add).then_inc(logits_ready, 1)
            dve.wait_ge(logits_ready, 2)
            v1, v2 = ra[:, 8, :], ra[:, 9, :]
            first_max(chain, lg, v1, oh[:, 0])
            chain.link(nc.vector.scalar_tensor_tensor(out=l2, in0=oh[:, 0], scalar=-1e30, in1=lg, op0=ALU.mult, op1=ALU.add))
            first_max(chain, l2, v2, oh[:, 1])
            nc.vector.tensor_tensor(rb[:, 1, :], v2, v1, ALU.subtract).then_inc(logits_ready, 1)
            dve.wait_ge(sig_ready, 2)
            ga, gb_ = gates[:, 0, :], gates[:, 1, :]
            chain.link(nc.vector.tensor_scalar(ra[:, 10, :], rb[:, 0, :], 1.0, None, ALU.add))
            chain.link(nc.vector.reciprocal(ga, ra[:, 10, :]))
            chain.link(nc.vector.tensor_tensor(gb_, ga, rb[:, 0, :], ALU.mult))
            chain.link(nc.vector.tensor_tensor(rb[:, 4:8, :], oh[:, 0], over(ga, 4), ALU.mult))
            chain.link(nc.vector.tensor_tensor(rb[:, 8:12, :], oh[:, 1], over(gb_, 4), ALU.mult))
            chain.link(nc.vector.tensor_tensor(rb[:, 4:8, :], rb[:, 4:8, :], rb[:, 8:12, :], ALU.add))
            dve.wait_ge(c_psum, 1)
            chain.link(nc.vector.tensor_tensor(cvec[0:4, :], PS[0:4, 5, 0:D], c_b2[0:4, :], ALU.add))
            dve.sem_inc(c_ready, 1)
            chain.link(nc.vector.tensor_tensor(rvec[0:4, :], c_b2[0:4, :], cvec[0:4, :], ALU.subtract))
            dve.wait_ge(c_psum, 2)
            chain.link(nc.vector.tensor_tensor(rvec[0:4, :], PS[0:4, 4, 0:D], rvec[0:4, :], ALU.add))
            chain.link(nc.vector.tensor_copy(pay1[:, :, D:D + E1], rb[:, 4:8, :].rearrange("p g t -> p t g")))
            places = rb[:, 8:12, :]
            chain.link(nc.vector.scalar_tensor_tensor(out=places, in0=oh[:, 1], scalar=float(TOKENS), in1=over(k_place, 4),
                                                      op0=ALU.mult, op1=ALU.add))
            chain.link(nc.vector.tensor_copy(pay1[:, :, D + E1:PAY1], places.rearrange("p g t -> p t g")))
            positions(dve, chain, TOPK, SLOT1, 1)
            dve.sem_inc(pay_ready, 1)
            dve.sem_inc(r_ready, 1)
            for t in range(NT):
                r = tile_rows(t)
                dve.wait_ge(gr_psum, t + 1)
                nc.vector.tensor_tensor(h[0:r, t, :], PS[0:r, 2 + t % 2, 0:D], h[0:r, t, :], ALU.add).then_inc(h4_added, 1)
            dve.wait_ge(h4_added, NT)
            def add_bias(a_):
                chain.link(nc.vector.tensor_reduce(amax[:, 3:4], c_b1c, AX, ALU.max, apply_absolute_value=True))
                chain.link(nc.vector.scalar_tensor_tensor(out=a_, in0=a_, scalar=float(D), in1=amax[:, 3:4],
                                                          op0=ALU.mult, op1=ALU.add))
            dve_scale(dve, chain, w1h.rearrange("p (e n) -> p e n", e=E1)[:, :, 0:KC * F1], 1, add_bias)
            ffn_dve(dve, Layer1)
            for k, (t, n, r) in enumerate(RUNS):
                dve.wait_ge(taken_back[k], 16 * 3)
                for c, part in enumerate((back0, back1)):
                    nc.vector.tensor_tensor(h[0:r, t:t + n, :], h[0:r, t:t + n, :], part[0:r, t:t + n, :], ALU.add)\
                        .then_inc(added_back, 1)
                    dve.wait_ge(added_back, len(RUNS) + 2 * k + c + 1)

        @block.sync
        def _(sp):
            sp.dma_start(pt[0:IPAD, :, :], patches.rearrange("j r f -> r j f")).then_inc(patches_loaded, 16)
            sp.dma_start(wt, wtok).then_inc(small_loaded, 16)
            sp.dma_start(ccols[:, 0:20], cols).then_inc(small_loaded, 16)
            sp.dma_start(rows.rearrange("p a n -> p (a n)"), rows_a.broadcast_to([P, 6 * D])).then_inc(small_loaded, 16)
            sp.dma_start(cst[:, :], consts).then_inc(small_loaded, 16)
            sp.dma_start(petab[0:IPAD, :], pe_table).then_inc(small_loaded, 16)
            sp.dma_start(wsm[:, :], wsmall).then_inc(small_loaded, 16)
            sp.dma_start(h[:, 0:BATCH, :], txt.rearrange("b s d -> s b d")).then_inc(text_loaded, 16)
            with sp.Fori(0, XW // CW // 2) as n:
                for k in range(2):
                    sp.wait_ge(stage_free, 2 * n + (k + 1))
                    sp.dma_start(stage[:, k, :], w0[:, bass.ds((2 * n + k) * CW, CW)]).then_inc(stage_full[k], 16)
            if stop <= 2:
                dump(sp)
                return
            sp.dma_start(xs1.rearrange("(a p) n -> p a n", p=P),
                         zt.unsqueeze(1).broadcast_to([P, SLOT1, PAY1])).then_inc(zeroed1, 16)
            sp_rest(sp)
            dump(sp)

        def split_chunks(pool, hi, lo, words, first):
            for n in range(first, first + words // CW):
                cols_ = slice((n - first) * CW, (n - first + 1) * CW)
                pool.wait_ge(w_high, n + 1)
                nc.gpsimd.tensor_tensor(lo[:, cols_], stage[:, n % 2, :], hi[:, cols_], ALU.subtract)\
                    .then_inc(stage_free, 1)

        @block.gpsimd
        def _(pool):
            nc.gpsimd.memset(zt[:, 0:PAY1 - E1], 0.0).then_inc(zero_ready, 1)
            nc.gpsimd.memset(zt[:, PAY1 - E1:PAY1], float(DUMP)).then_inc(zero_ready, 1)
            nc.gpsimd.memset(onesb[:, :], 1.0).then_inc(consts_ready, 1)
            nc.gpsimd.memset(onesf[:, :], 1.0).then_inc(consts_ready, 1)
            nc.gpsimd.memset(xT[:, :, BATCH * SEQ:], 0.0).then_inc(pads_zeroed, 1)
            pool.wait_ge(pads_zeroed, 1)
            nc.gpsimd.memset(h[96:P, BATCH:NT, :], 0.0).then_inc(pads_zeroed, 1)
            pool.wait_ge(pads_zeroed, 2)
            pool.sem_inc(stage_free, 2)
            split_chunks(pool, w0h, w0l, XW, 0)
            if stop > 2:
                pool_rest(pool)

        @block.scalar
        def _(act):
            chain = Chain(act, act_done)
            pair_of = [0]

            def roots(n):
                act.wait_ge(var_ready, n)
                nc.scalar.activation(std, var, ACT.Sqrt).then_inc(std_ready, 1)

            def high_half(high, n, k, j):
                act.wait_ge(stage_full[k], 16 * (j + 1))
                nc.scalar.activation(high[:, bass.ds(n * CW, CW)], stage[:, k, :], ACT.Copy).then_inc(w_high, 1)

            act.wait_ge(small_loaded, 16 * NSMALL)
            chain.link(nc.scalar.activation(c_nega, c_alog, ACT.Exp))
            nc.scalar.mul(c_nega, c_nega, -1.0).then_inc(nega_ready, 1)
            act.wait_ge(zero_ready, 2)
            act.dma_start(xs0.rearrange("(a p) n -> p a n", p=P),
                          zt[:, PAY1 - E1 + 1 - PAY0:PAY1 - E1 + 1].unsqueeze(1).broadcast_to([P, SLOT0, PAY0])).then_inc(zeroed, 16)
            roots(1)
            for j in range(IT):
                for half in range(2):
                    act.wait_ge(patch_tr, 2 * j + half + 1)
                    if j >= 2:
                        act.wait_ge(tok_psum, j - 1)
                    bank = PS[:, 1 + 2 * (j % 2) + half, 0:3 * IPAD].rearrange("p (c r) -> p c r", c=3)
                    nc.scalar.activation(pT[:, j % 2, 3 * half:3 * half + 3, :], bank, ACT.Copy)\
                        .then_inc(patch_copied, 1)
                high_half(w0h, j, j % 2, j // 2)
            roots(2)
            act.wait_ge(cls_ready, 1)
            act.wait_ge(tok_ready, 1)
            for b in range(PER):
                n = IT if b < LAST else IT - 1
                act.dma_start(h[b * IMG:b * IMG + 1, BATCH:BATCH + n, :],
                              r_cls[0:1, :].unsqueeze(1).broadcast_to([1, n, D])).then_inc(cls_placed, 16)

            act.sem_inc(xT_copied, AHEAD)
            roots(3)

            def copy_xT(t, rows, slot):
                act.wait_ge(xn_tr, t + 1 + AHEAD)
                src = PS[:, slot, 0:KC * P].rearrange("p (k r) -> p k r", k=KC)[:, :, 0:rows]
                if rows != P:
                    src = src.rearrange("p k (b s) -> p k b s", s=IMG)
                nc.scalar.activation(batch_cols(xT, t, rows), src, ACT.Copy).then_inc(xT_copied, 1)

            act.wait_ge(pads_zeroed, 2)
            token_tiles(act, copy_xT)
            for n in range(9):
                g, c = n // 3, (n % 3) * 2 * SEQ
                act.wait_ge(bcd_psum, n + 1)
                nc.scalar.activation(sD[32 * g:32 * g + 32, c:c + 2 * SEQ], PS[64:96, n % 2 + 2, 0:2 * SEQ],
                                     ACT.Identity, bias=c_bcd[64:96, :]).then_inc(dl_copied, 1)
            act.wait_ge(dl_copied, 9)
            chain.link(nc.scalar.activation(sA[0:96, :], sD[0:96, :], ACT.Abs))
            chain.link(nc.scalar.activation(sA[0:96, :], sA[0:96, :], ACT.Exp, scale=-1.0))
            nc.scalar.activation(sA[0:96, :], sA[0:96, :], ACT.Ln, bias=1.0).then_inc(sp_ready, 1)
            act.wait_ge(delta_ready, 1)
            nc.scalar.activation(sA[0:96, :], sD[0:96, :], ACT.Exp, scale=c_nega).then_inc(decay_ready, 1)

            def gelu_z(t, rows, slot):
                for m in range(KC):
                    act.wait_ge(z_psum, t + 1)
                    ins = nc.scalar.activation(gT[:, slot, m, 0:rows], PS[:, 2 + slot, m * P:m * P + rows], ACT.Gelu,
                                               bias=c_bz[:, m:m + 1])
                ins.then_inc(g_ready, 1)
                if rows == P:
                    high_half(w0h, t + IT, slot, pair_of[0] + IT // 2)
            token_tiles(act, gelu_z, pair_of)
            for n in range(BATCH + IT, XW // CW):
                high_half(w0h, n, n % 2, n // 2)
            if stop <= 2:
                return
            act_rest(act, roots)

        @block.tensor
        def _(pe):
            pe.wait_ge(small_loaded, 16 * NSMALL)
            for c in range(PC):
                ins = nc.tensor.matmul(PS[:, 0, 0:D], c_b1[:, c:c + 1].broadcast_to([P, P]), wt[:, c, :],
                                       start=(c == 0), stop=(c == PC - 1))
            ins.then_inc(tokb_psum, 1)

            def tok_matmul(j):
                pe.wait_ge(patch_copied, 2 * j + 2)
                if j == 0:
                    pe.wait_ge(wt_scaled, 1)
                if j >= 2:
                    pe.wait_ge(tok_added, j - 1)
                for c in range(PC):
                    ins = nc.tensor.matmul(PS[0:IPAD, 5 + j % 2, 0:D], pT[:, j % 2, c, :], wt[:, c, :],
                                           start=(c == 0), stop=(c == PC - 1))
                ins.then_inc(tok_psum, 1)

            for j in range(IT):
                pe.wait_ge(patch_normed, j + 1)
                if j >= 2:
                    pe.wait_ge(patch_copied, 2 * j - 2)
                for half in range(2):
                    for c in range(3):
                        ins = nc.tensor.transpose(PS[:, 1 + 2 * (j % 2) + half, c * IPAD:(c + 1) * IPAD],
                                                  pt[0:IPAD, j, (3 * half + c) * P:(3 * half + c + 1) * P],
                                                  k_ident[0:IPAD, 0:IPAD])
                    ins.then_inc(patch_tr, 1)
                if j >= 1:
                    tok_matmul(j - 1)
            tok_matmul(IT - 1)

            pe.sem_inc(xn_tr, AHEAD)

            def tr(t, rows, slot):
                pe.wait_ge(xn_ready, t + 1)
                pe.wait_ge(xT_copied, t + 1)
                for k in range(KC):
                    ins = nc.tensor.transpose(PS[:, slot, k * P:(k + 1) * P], xn[:, slot, k * P:(k + 1) * P], k_ident)
                ins.then_inc(xn_tr, 1)
            token_tiles(pe, tr)
            for n in range(PB // 2):
                if n == 0:
                    pe.wait_ge(xT_copied, NT + AHEAD)
                if n >= 2:
                    pe.wait_ge(bc_copied, n - 1)
                    pe.wait_ge(dl_copied, n - 1)
                for k in range(KC):
                    ins = nc.tensor.matmul(PS[0:96, 2 + n % 2, 0:2 * SEQ], wbcd[:, k, :],
                                           xT[:, k, 2 * n * SEQ:2 * (n + 1) * SEQ], start=(k == 0), stop=(k == KC - 1))
                ins.then_inc(bcd_psum, 1)

            def scan_sum():
                pe.wait_ge(sc_ready, 2)
                for t in range(NT):
                    b0 = t if t < BATCH else (t - BATCH) * PER
                    g, b = b0 // SB, b0 % SB
                    nb = min(PER, BATCH - b0)
                    rows_ = P if t < BATCH else nb * IMG
                    c = SB * IMG + b * TEXT if t < BATCH else b * IMG
                    part = sA[32 * g:32 * g + 32, c:c + rows_]
                    ins = nc.tensor.matmul(PS[0:rows_, Y_BANKS[g], t:t + 1], part, onesf[32 * g:32 * g + 32, 0:1],
                                           start=True, stop=True)
                ins.then_inc(y_psum, 1)

            def z_matmul(t, rows, slot):
                pe.wait_ge(h_added, t + 1)
                for m in range(KC):
                    out_ = PS[:, 2 + slot, m * P:m * P + rows]
                    if rows != P:
                        out_ = out_.rearrange("p (b s) -> p b s", s=IMG)
                    for k in range(KC):
                        rhs = batch_cols(xT, t, rows)[:, k]
                        ins = nc.tensor.matmul(out_, wz[:, k, m * P:(m + 1) * P], rhs, start=(k == 0),
                                               stop=(k == KC - 1))
                ins.then_inc(z_psum, 1)

            def o_matmul(t, rows, slot):
                pe.wait_ge(g_ready, t + 1)
                for k in range(KC):
                    ins = nc.tensor.matmul(PS[0:rows, 4 + slot, 0:D], gT[:, slot, k, 0:rows], wout[:, k, :],
                                           start=(k == 0), stop=(k == KC - 1))
                ins.then_inc(o_psum, 1)

            def zo(t, rows, slot):
                z_matmul(t, rows, slot)
                o_matmul(t, rows, slot)
            pe.wait_ge(bc_copied, 9)
            pe.wait_ge(dl_copied, 9)
            scan_sum()
            token_tiles(pe, zo)
            if stop <= 2:
                return
            pe_rest(pe)

        @block.vector
        def _(dve):
            chain = Chain(dve, dve_done)
            ln_count = [0]

            def moments(t, count=1):
                chain.link(nc.vector.bn_stats(stats[:, bass.ds(t, 1), 0, :], h[:, bass.ds(t, 1), :]))
                chain.link(nc.vector.bn_aggr(mv[:, bass.ds(t, 1), :], stats[:, bass.ds(t, 1), 0, :]))

            def inverse_roots():
                nc.vector.tensor_scalar(var, mv[:, :, 1], EPS, None, ALU.add).then_inc(var_ready, 1)
                ln_count[0] += 1
                dve.wait_ge(std_ready, ln_count[0])
                chain.link(nc.vector.reciprocal(rstd, std))
                chain.link(nc.vector.tensor_tensor(newt, rstd, rstd, ALU.mult))
                chain.link(nc.vector.tensor_tensor(newt, newt, var, ALU.mult))
                chain.link(nc.vector.tensor_scalar(newt, newt, -0.5, 1.5, ALU.mult, ALU.add))
                chain.link(nc.vector.tensor_tensor(rstd, rstd, newt, ALU.mult))

            chain.link(nc.vector.memset(mv[:, :, :], 0.0))
            dve.wait_ge(patches_loaded, 16)
            for j in range(IT):
                for half in range(2):
                    ins = nc.vector.bn_stats(stats[0:IPAD, j, half, :], pt[0:IPAD, j, half * 384:(half + 1) * 384])
            chain.link(ins)
            for j in range(IT):
                ins = nc.vector.bn_aggr(mv[0:IPAD, j, :], stats[0:IPAD, j, :, :].rearrange("p a b -> p (a b)"))
            chain.link(ins)
            inverse_roots()
            for j in range(IT):
                nc.vector.tensor_scalar(pt[0:IPAD, j, :], pt[0:IPAD, j, :], mv[0:IPAD, j, 0:1], rstd[0:IPAD, j:j + 1],
                                        ALU.subtract, ALU.mult).then_inc(patch_normed, 1)
            dve.wait_ge(tokb_psum, 1)
            chain.link(nc.vector.tensor_tensor(r_tb, PS[:, 0, 0:D], r_tb, ALU.add))
            for c in range(PC):
                ins = nc.vector.tensor_scalar(wt[:, c, :], wt[:, c, :], c_g1[:, c:c + 1], None, ALU.mult)
            ins.then_inc(wt_scaled, 1)
            nc.vector.tensor_tensor(r_cls[0:1, :], r_cls[0:1, :], r_cpos[0:1, :], ALU.add).then_inc(cls_ready, 1)
            chain.link(nc.vector.tensor_tensor(petab[0:IPAD, :], petab[0:IPAD, :], r_b2[0:IPAD, :], ALU.add))
            dve.wait_ge(pads_zeroed, 2)
            for j in range(IT):
                dve.wait_ge(tok_psum, j + 1)
                ins = nc.vector.tensor_tensor(h[0:IPAD, BATCH + j, :], PS[0:IPAD, 5 + j % 2, 0:D], r_tb[0:IPAD, :],
                                              ALU.add)
                ins.then_inc(tok_added, 1)
            dve.wait_ge(tok_added, IT)
            for j in range(IT):
                ins = nc.vector.bn_stats(stats[0:IPAD, j, 0, :], h[0:IPAD, BATCH + j, :])
            chain.link(ins)
            for j in range(IT):
                ins = nc.vector.bn_aggr(mv[0:IPAD, j, :], stats[0:IPAD, j, 0, :])
            chain.link(ins)
            inverse_roots()
            for j in range(IT):
                ins = nc.vector.tensor_scalar(h[0:IPAD, BATCH + j, :], h[0:IPAD, BATCH + j, :], mv[0:IPAD, j, 0:1],
                                              rstd[0:IPAD, j:j + 1], ALU.subtract, ALU.mult)
            chain.link(ins)
            image = h[0:IPAD, BATCH:NT, :]
            chain.link(nc.vector.tensor_tensor(image, image, r_g2[0:IPAD, :].unsqueeze(1).broadcast_to([IPAD, IT, D]),
                                               ALU.mult))
            nc.vector.tensor_tensor(image, image, petab[0:IPAD, :].unsqueeze(1).broadcast_to([IPAD, IT, D]),
                                    ALU.add).then_inc(tok_ready, 1)

            dve.wait_ge(text_loaded, 16)
            dve.wait_ge(cls_placed, 16 * PER)
            for t in range(NT):
                ins = nc.vector.bn_stats(stats[:, t, 0, :], h[:, t, :])
            chain.link(ins)
            for t in range(NT):
                ins = nc.vector.bn_aggr(mv[:, t, :], stats[:, t, 0, :])
            chain.link(ins)
            inverse_roots()

            def norm(t, rows, slot):
                dve.wait_ge(xn_tr, t + 1)
                nc.vector.tensor_scalar(xn[:, slot, :], h[:, bass.ds(t, 1), :], mv[:, bass.ds(t, 1), 0],
                                        rstd[:, bass.ds(t, 1)], ALU.subtract, ALU.mult).then_inc(xn_ready, 1)
            token_tiles(dve, norm)
            for n in range(9):
                g, c = n // 3, (n % 3) * 2 * SEQ
                dve.wait_ge(bcd_psum, n + 1)
                nc.vector.tensor_scalar(sB[32 * g:32 * g + 32, c:c + 2 * SEQ], PS[0:32, n % 2 + 2, 0:2 * SEQ],
                                        c_bcd[0:32, :], None, ALU.add)
                nc.vector.tensor_scalar(sC[32 * g:32 * g + 32, c:c + 2 * SEQ], PS[32:64, n % 2 + 2, 0:2 * SEQ],
                                        c_bcd[32:64, :], None, ALU.add).then_inc(bc_copied, 1)
            dve.wait_ge(bc_copied, 9)
            dve.wait_ge(sp_ready, 1)
            nc.vector.scalar_tensor_tensor(out=sD[0:96, :], in0=sD[0:96, :], scalar=0.0, in1=sA[0:96, :],
                                           op0=ALU.max, op1=ALU.add).then_inc(delta_ready, 1)
            dve.wait_ge(decay_ready, 1)
            chain.link(nc.vector.memset(sA[0:96, :].rearrange("p (b s) -> p b s", s=SEQ)[:, :, 0:1], 0.0))
            chain.link(nc.vector.tensor_tensor_scan(sS[0:96, :], sA[0:96, :], sB[0:96, :], 0.0, ALU.mult, ALU.add))
            for lo, hi, at_ in ((0, IMG, 0), (IMG, SEQ, SB * IMG)):
                state, cc = (v[0:96, :].rearrange("p (b s) -> p b s", s=SEQ)[:, :, lo:hi] for v in (sS, sC))
                nc.vector.tensor_tensor(sA[0:96, at_:at_ + SB * (hi - lo)].rearrange("p (b s) -> p b s", b=SB),
                                        state, cc, ALU.mult).then_inc(sc_ready, 1)
            dve.wait_ge(y_psum, 1)
            chain.link(nc.vector.memset(yv[:, :], 0.0))
            for t in range(NT):
                g = (t if t < BATCH else (t - BATCH) * PER) // SB
                rows_ = P if t < BATCH else IROWS if t < NT - 1 else LAST * IMG
                ins = nc.vector.tensor_copy(yv[0:rows_, t:t + 1], PS[0:rows_, Y_BANKS[g], t:t + 1])
            chain.link(ins)
            dve.sem_inc(h_added, AHEAD)

            def add_scan(t, rows, slot):
                ht = h[0:rows, bass.ds(t, 1), :]
                dve.wait_ge(o_psum, t + 1)
                nc.vector.scalar_tensor_tensor(out=ht, in0=PS[0:rows, 4 + slot, 0:D].unsqueeze(1),
                                               scalar=yv[0:rows, bass.ds(t, 1)], in1=ht, op0=ALU.mult, op1=ALU.add)\
                    .then_inc(h_added, 1)
                dve.wait_ge(h_added, t + 1 + AHEAD)
                nc.vector.tensor_tensor(ht, ht, r_bout[0:rows, :].unsqueeze(1), ALU.add).then_inc(hb_added, 1)
                dve.wait_ge(hb_added, t + 1)
                nc.vector.bn_stats(stats[:, bass.ds(t, 1), 0, :], h[:, bass.ds(t, 1), :]).then_inc(stats_ready, 1)
            token_tiles(dve, add_scan)
            if stop <= 2:
                return
            dve_rest(dve, chain, inverse_roots)


def position_table():
    omega = np.arange(D // 4, dtype=np.float32) / np.float32(D // 4 - 1)
    omega = (np.float32(1.0) / np.float32(10000.0) ** omega).astype(np.float32)
    y, x = np.meshgrid(np.arange(GRID), np.arange(GRID), indexing="ij")
    y = y.reshape(-1)[:, None].astype(np.float32) * omega[None, :]
    x = x.reshape(-1)[:, None].astype(np.float32) * omega[None, :]
    pe = np.concatenate((np.sin(x), np.cos(x), np.sin(y), np.cos(y)), axis=1).astype(np.float32)
    table = np.zeros((IPAD, D), np.float32)
    for b in range(PER):
        table[b * IMG + 1:(b + 1) * IMG] = pe
    return table


def shape_constants():
    c = np.zeros((P, NCST), np.float32)
    c[:, 0:P] = np.eye(P)
    c[:, P:2 * P] = np.triu(np.ones((P, P)), 1)
    at = 2 * P
    valid = np.ones((P, NT))
    valid[IROWS:, BATCH:] = 0
    valid[LAST * IMG:, NT - 1] = 0
    c[:, at:at + NT] = valid; at += NT
    reset = np.ones((4, NT)); reset[:, 0] = 0
    c[:, at:at + 4 * NT] = reset.reshape(-1); at += 4 * NT
    c[:, at:at + 4 * NFULL] = np.tile(np.arange(NFULL) * P, 4); at += 4 * NFULL
    c[:, at:at + SLOT1] = np.arange(SLOT1); at += SLOT1
    c[:, at:at + NT] = np.arange(P)[:, None] + P * np.arange(NT)
    return c


def chunks(w, parts):
    return w.reshape(parts, P, -1).transpose(1, 0, 2)


def rope_tables():
    freqs = (np.float32(1.0) / np.float32(10000.0) ** (np.arange(0, D, 2, dtype=np.float32) / np.float32(D)))
    ang = freqs.astype(np.float32)[:, None] * np.arange(SEQ, dtype=np.float32)[None, :]
    cos, sin = np.cos(ang).astype(np.float32), np.sin(ang).astype(np.float32)
    query, key = np.arange(P)[:, None], np.arange(SEQ)[None, :]
    mask_a = np.where(key[:, :P] <= query, 0.0, -1e30)
    mask_b = np.where(key <= query + P, 0.0, -1e30)
    return np.concatenate([cos, sin, -sin, mask_a, mask_b], 1).astype(np.float32)


def lay_out(i):
    f = {k: np.asarray(v) for k, v in i.items()}
    x = f["x"].reshape(BATCH, CH, GRID, PATCH, GRID, PATCH).transpose(0, 2, 4, 3, 5, 1).reshape(BATCH, IMG - 1, PDIM)
    pt = np.zeros((PB, IMG, PDIM), np.float32)
    pt[:BATCH, 1:] = x
    patches = np.zeros((IT, IPAD, PDIM), np.float32)
    patches[:, :IROWS] = pt.reshape(IT, IROWS, PDIM)
    w_in, b_in = f["L0_attn_W_in"], f["L0_attn_b_in"]
    cols = np.zeros((P, 20), np.float32)
    cols[:, 0:6] = f["L0_tok_ln1_g"].reshape(PC, P).T
    cols[:, 6:12] = f["L0_tok_ln1_b"].reshape(PC, P).T
    cols[:, 12:14] = b_in[D:2 * D].reshape(KC, P).T
    cols[:, 14:16] = f["L1_attn_bq"].reshape(P, 2)
    cols[:, 16:18] = f["L1_attn_bk"].reshape(P, 2)
    wbcd = np.zeros((D, 96), np.float32)
    for n in range(3):
        wbcd[:, 32 * n:32 * n + NS] = w_in[:, 2 * D + n * NS:2 * D + (n + 1) * NS]
        cols[32 * n:32 * n + NS, 18] = b_in[2 * D + n * NS:2 * D + (n + 1) * NS]
        cols[32 * n:32 * n + NS, 19] = f["L0_attn_A_log"]
    route = np.concatenate([f["L0_ffn_macro_w"], f["L0_ffn_micro_w"].transpose(1, 0, 2).reshape(D, G0 * E0)], 1)
    small = np.concatenate([chunks(w, KC).reshape(P, -1) for w in (wbcd, w_in[:, D:2 * D], f["L0_attn_W_out"], route)], 1)
    w0 = np.concatenate([np.concatenate([chunks(f["L0_ffn_gate_w"][e], KC).reshape(P, -1),
                                         chunks(f["L0_ffn_up_w"][e], KC).reshape(P, -1),
                                         chunks(f["L0_ffn_down_w"][e], F0 // P).reshape(P, -1)], 1)
                         for e in range(G0 * E0)], 1)
    halves = lambda w: np.concatenate([w.T[:, 0::2], w.T[:, 1::2]], 1)
    wattn = np.concatenate([chunks(w, KC).reshape(P, -1) for w in (
        halves(f["L1_attn_Wq"]), halves(f["L1_attn_Wk"]), f["L1_attn_Wv"].T, f["L1_attn_Wf"].T)] + [rope_tables()], 1)
    w1 = np.concatenate([np.concatenate(
        [chunks(f["L1_ffn_w1"][e][:, s * F0:(s + 1) * F0], KC).reshape(P, -1) for s in range(HF)]
        + [chunks(f["L1_ffn_w2"][e], F1 // P).reshape(P, -1)], 1) for e in range(E1)], 1)
    small1 = np.zeros((P, NSM1), np.float32)
    at = 4 * KC
    small1[:, 0:at] = chunks(f["L1_ffn_wr"], KC).reshape(P, -1)
    small1[:, at:at + (F1 // P) * E1] = f["L1_ffn_b1"].reshape(E1, F1 // P, P).transpose(2, 1, 0).reshape(P, -1)
    at += (F1 // P) * E1
    small1[:, at:at + E1] = f["L1_ffn_br"]
    at += E1
    small1[0:E1, at:at + D] = f["L1_ffn_b2"]
    return {
        "wattn": wattn, "rows_f": np.concatenate([f["L1_attn_bv"], f["L1_attn_bf"]])[None], "w1": w1,
        "wsmall1": small1, "b1rows": f["L1_ffn_b1"].reshape(1, -1),
        "txt": f["txt"], "patches": patches, "wtok": chunks(f["L0_tok_W"], PC), "cols": cols,
        "rows_a": np.concatenate([f[k].reshape(-1) for k in (
            "L0_tok_ln2_g", "L0_tok_ln2_b", "L0_tok_bias", "L0_tok_cls_token", "L0_tok_cls_pos_embedding",
            "L0_attn_b_out")])[None],
        "consts": shape_constants(), "pe_table": position_table(), "wsmall": small, "w0": w0,
    }


def kernel(**inputs):
    import concourse.bacc as _bacc
    from concourse.bass_utils import run_bass_kernel_spmd as _run

    nc = _bacc.Bacc("TRN2", target_bir_lowering=False, num_devices=1)
    arrays, args = {}, {}
    for name, a in lay_out(inputs).items():
        a = np.ascontiguousarray(a)
        arrays[f"in_{name}_dram"] = a
        args[name] = nc.dram_tensor(f"in_{name}_dram", a.shape, mybir.dt.from_np(a.dtype), kind="ExternalInput").ap()
    out = nc.dram_tensor("out_0_dram", (BATCH, SEQ, D), F32, kind="ExternalOutput").ap()
    build(nc, out=out, stop=STOP, **args)
    r = _run(nc, [arrays], core_ids=[0])
    return r.results[0]["out_0_dram"]
```

```python
from contextlib import ExitStack

import numpy as np

import concourse.bass as bass
from concourse import mybir

F32 = mybir.dt.float32
BF16 = mybir.dt.bfloat16
F16 = mybir.dt.float16
I32 = mybir.dt.int32
U32 = mybir.dt.uint32
ALU = mybir.AluOpType
ACT = mybir.ActivationFunctionType
AX = mybir.AxisListType.X
AXS = [mybir.AxisListType.X, mybir.AxisListType.XY]

P = 128
BATCH, TEXT, D = 16, 128, 256
GRID, PATCH, CH = 6, 16, 3
IMG = GRID * GRID + 1
SEQ = IMG + TEXT
PDIM = PATCH * PATCH * CH
PC = PDIM // P
KC = D // P
PER = 3
IT = -(-BATCH // PER)
IROWS = PER * IMG
IPAD = 112
LAST = BATCH - PER * (IT - 1)
NT = BATCH + IT
PB = IT * PER
NS = 16
SG = 3
SB = PB // SG
EPS = 1e-5
G0, E0, F0 = 4, 2, 512
SLOT0 = (BATCH * SEQ + G0 * (P - 1)) // P
W0N = 2 * KC * F0 + (F0 // P) * D
E1, F1, TOPK = 4, 1024, 2
SLOT1 = (TOPK * BATCH * SEQ + E1 * (P - 1)) // P
HF = F1 // F0
W1N = KC * F1 + (F1 // P) * D
W1W = E1 * W1N
PAY0 = D + E0
PAY1 = D + E1
TOKENS = NT * P
DUMP = 2 * TOKENS
RUNS = [(0, 6, P), (6, 6, P), (12, 4, P), (BATCH, IT - 1, IROWS), (NT - 1, 1, LAST * IMG)]
BACK_DVE, BACK_POOL = (0, 2), (1, 3, 4)
OUT_DVE, OUT_POOL = (0, 1, 2), (3, 4)
OUT_LOADS, OUT_STORES = (0, 3, 4, 1, 2), (0, 1, 3, 4, 2)
CW = 1024
NFULL = -(-BATCH * SEQ // P)
NCST = 3 * P + NT + 4 * NT + 4 * NFULL + SLOT1 + NT + TOPK * NT + 3
NCOL = 22
NWS = KC * (96 + D + D + 12)
XW0 = G0 * E0 * W0N
STOP = 5
SCALE = float(D) ** -0.5
NATT = 4 * KC * D + 3 * SEQ + P + SEQ
NSM1 = 4 * KC + (F1 // P) * E1 + E1
ALONE = 12
LATE = XW0 // CW - IT - ALONE
AHEAD = 2
SAT = 17.0


def ceil_even(n):
    return n + n % 2


class Region:

    def __init__(self, t, words, at=0):
        self.t, self.words, self.at = t, words, at

    def take(self, shape, dt=F32):
        n = int(np.prod(shape))
        words = n if dt not in (BF16, F16) else ceil_even(n) // 2
        assert self.at + words <= self.words, (self.at, words, self.words)
        ap = self.t[:, self.at:self.at + words]
        self.at += ceil_even(words)
        if dt != F32:
            ap = ap.bitcast(dt)
        if len(shape) == 1:
            return ap
        names = "abcdef"[:len(shape)]
        kw = {c: s for c, s in zip(names[1:], shape[1:])}
        return ap.rearrange(f"p ({' '.join(names)}) -> p {' '.join(names)}", **kw)


class Chain:

    def __init__(self, eng, sem):
        self.eng, self.sem, self.n, self.loop = eng, sem, 0, None

    def link(self, ins):
        ins.then_inc(self.sem, 1)
        if self.loop is None:
            self.n += 1
            self.eng.wait_ge(self.sem, self.n)
        else:
            self.loop[1] += 1
            self.eng.wait_ge(self.sem, self.loop[0] * self.loop[2] + (self.n + self.loop[1]))

    def begin(self, i, per):
        self.loop = [i, 0, per]

    def end(self, trips):
        assert self.loop[1] == self.loop[2], self.loop
        self.n += trips * self.loop[2]
        self.loop = None


C_BANKS = (0, 5)
Y_BANKS = (6, 7, 0)


def tile_rows(t):
    return P if t < BATCH else IROWS if t < NT - 1 else LAST * IMG


def token_tiles(eng, body, pair_of=None):
    with eng.Fori(0, BATCH // 2) as i:
        if pair_of is not None:
            pair_of[0] = i
        body(2 * i, P, 0)
        body(2 * i + 1, P, 1)
    with eng.Fori(0, (IT - 2) // 2) as j:
        body(BATCH + 2 * j, IROWS, 0)
        body(BATCH + 1 + 2 * j, IROWS, 1)
    body(NT - 2, IROWS, 0)
    body(NT - 1, LAST * IMG, 1)


def pipelined(eng, n, body):
    pairs = (n - 3) // 2
    body(0, 0, 0)
    body(1, 1, 0)
    with eng.Fori(1, 1 + pairs) as j:
        body(2 * j, 0, j)
        body(2 * j + 1, 1, j)
    for i in range(2 + 2 * pairs, n):
        body(i, i % 2, i // 2)


def known(i, value):
    return isinstance(i, int) and i == value


def batch_cols(view, t, rows):
    if rows == P:
        return view[:, :, bass.ds(t * SEQ + IMG, TEXT)]
    nb = rows // IMG
    part = view[:, :, bass.ds((t - BATCH) * (PER * SEQ), PER * SEQ)]
    return part.rearrange("p k (b s) -> p k b s", s=SEQ)[:, :, 0:nb, 0:IMG]


def wait_from(eng, sem, value):
    if isinstance(value, int) and value <= 0:
        return
    eng.wait_ge(sem, value)


def build(nc, txt, patches, wtok, cols, rows_a, consts, pe_table, wsmall, w0, wattn, rows_f, w1, wsmall1,
          b1rows, b2rows, out, stop=99):
    with ExitStack() as ctx:
        def sb(name, shape, dt=F32):
            return ctx.enter_context(nc.sbuf_tensor(name, shape, dt))

        def sem(name):
            return ctx.enter_context(nc.semaphore(name))

        h = sb("h", [P, NT, D])
        XW, YW = G0 * E0 * W0N, 16900
        X = sb("X", [P, XW])
        Y = sb("Y", [P, YW])
        stage = sb("stage", [P, 2, CW])
        cst = sb("cst", [P, NCST])
        ccols = sb("ccols", [P, NCOL])
        wsm = sb("wsm", [P, NWS])
        upper = sb("upper", [P, P], BF16)
        onesb = sb("onesb", [P, P], BF16)
        onesf = sb("onesf", [P, P])
        stats = sb("stats", [P, NT, 2, 6])
        mv = sb("mv", [P, NT, 2])
        rs4 = sb("rs4", [P, 4, NT])
        var, std, rstd, newt = (rs4[:, i, :] for i in range(4))
        yv = sb("yv", [P, NT])
        ra = sb("ra", [P, 12, NT])
        rb = sb("rb", [P, 12, NT])
        rc = sb("rc", [P, 12, NT])
        oh = sb("oh", [P, TOPK, 4, NT])
        ohb = sb("ohb", [P, 4, NT], BF16)
        raf = ra.rearrange("p g t -> p (g t)")
        sm = sb("sm", [P, 32])
        hscale = sb("hscale", [P, 4])
        amax = sb("amax", [P, 4])
        gates = sb("gates", [P, TOPK, NT])
        posf = sb("posf", [P, TOPK, NT])
        pos = sb("pos", [P, TOPK, NT], I32)
        low7 = rc[:, 0:TOPK, :].bitcast(I32)
        high7 = rc[:, TOPK:2 * TOPK, :].bitcast(I32)
        tok = stats.rearrange("p t a b -> p (t a b)")[:, 0:3 * SLOT1].rearrange("p (i s) -> p i s", i=3)
        slotf = sb("slotf", [P, SLOT1])
        slote = sb("slote", [P, SLOT1], I32)
        PS = ctx.enter_context(nc.psum_tensor("PS", [P, 8, 512], F32))

        xs0 = nc.dram_tensor("xs0", [TOKENS, PAY0], F32).ap()
        ys0 = nc.dram_tensor("ys0", [DUMP + 1, D], F32).ap()
        xs1 = nc.dram_tensor("xs1", [TOKENS, PAY1], F32).ap()
        ys1 = nc.dram_tensor("ys1", [DUMP + 1, D], F32).ap()
        source = sb("source", [P, SLOT1], U32)
        dest = sb("dest", [P, SLOT1], U32)

        k_ident = cst[:, 0:P]
        k_upper = cst[:, P:2 * P]
        at = 2 * P
        k_valid = cst[:, at:at + NT]; at += NT
        k_reset = cst[:, at:at + 4 * NT]; at += 4 * NT
        k_fill = cst[:, at:at + 4 * NFULL].rearrange("p (g k) -> p g k", g=4); at += 4 * NFULL
        k_slot = cst[:, at:at + SLOT1]; at += SLOT1
        k_far = cst[:, at:at + NT]; at += NT
        k_tile = cst[:, at:at + TOPK * NT]; at += TOPK * NT
        k_iota = cst[:, at:at + P]; at += P
        k_row, k_patch, k_class = (cst[:, at + i:at + i + 1] for i in range(3))
        c_g1, c_b1 = ccols[:, 0:6], ccols[:, 6:12]
        c_bz, c_bq, c_bk = ccols[:, 12:14], ccols[:, 14:16], ccols[:, 16:18]
        c_bcd, c_alog, c_nega = ccols[0:96, 18:19], ccols[0:96, 19:20], ccols[0:96, 20:21]
        rw = Region(wsm, NWS)
        wbcd = rw.take([KC, 96])
        wz = rw.take([KC, D])
        wout = rw.take([KC, D])
        wr0 = rw.take([KC, 12])

        ry = Region(Y, YW)
        pt = ry.take([IT, PDIM])
        rs = Region(Y, YW)
        GS = SB * SEQ
        sB, sC, sD, sA = (rs.take([GS]) for _ in range(4))
        assert rs.at <= ry.at
        wt = ry.take([PC, D])
        sS = Region(Y, YW, rs.at).take([GS])
        rows = ry.take([6, D])
        r_g2, r_b2, r_tb, r_cls, r_cpos, r_bout = (rows[:, i, :] for i in range(6))
        pay_at = ry.at
        xT = ry.take([KC, PB * SEQ])
        pay = Region(Y, YW, pay_at).take([NT, PAY0])
        pT = ry.take([2, PC, IPAD])
        xn = ry.take([2, D])
        x2T = xn.rearrange("p a (k r) -> p a k r", k=KC)
        gT = ry.take([2, KC, P])
        petab = gT.rearrange("p a k n -> p (a k n)")[:, 0:D]
        rd = Region(Y, YW)
        xin = rd.take([2, PAY0])
        ybuf = rd.take([2, D])
        wall = rd.take([SLOT0, 2])
        xh = rd.take([2, KC, P], F16)
        xl = rd.take([2, KC, P], F16)
        sg = rd.take([2, F0])
        hh = rd.take([2, F0])
        hTh = rd.take([2, 4, P], F16)
        hTl = rd.take([2, 4, P], F16)
        hots0 = Region(Y, YW, rd.at)
        inrow0, intile0 = hots0.take([NT, P], BF16), hots0.take([NT, 3, SLOT0], BF16)
        assert hots0.at <= pay_at
        back = rd.take([NT, D])
        end = Region(X, XW, XW - (NSM1 + 2 * (F1 // P) * E1 + 2 * E1 * D))
        small1 = end.take([NSM1])
        wr1 = small1[:, 0:4 * KC].rearrange("p (k e) -> p k e", k=KC)
        c_b1c = small1[:, 4 * KC:4 * KC + (F1 // P) * E1]
        c_br = small1[:, NSM1 - E1:NSM1]
        gb1 = end.take([(F1 // P) * E1])
        gbh, gbl = end.take([(F1 // P) * E1], F16), end.take([(F1 // P) * E1], F16)
        b2all = end.take([E1, D])
        rest1 = end.take([E1, D])
        XE = XW - (NSM1 + 2 * (F1 // P) * E1 + 2 * E1 * D)
        rx = Region(X, XE)
        wq, wk, wv, wf = (rx.take([KC, D]) for _ in range(4))
        tab = X[:, 4 * KC * D:NATT]
        k_cos, k_sin, k_nsin = (tab[:, i * SEQ:(i + 1) * SEQ] for i in range(3))
        k_maskA, k_maskB = tab[:, 3 * SEQ:3 * SEQ + P], tab[:, 3 * SEQ + P:4 * SEQ + P]
        rx.at = ceil_even(NATT)
        rowsF = rx.take([2, D])
        xnF = rx.take([2, D])
        xTi = rx.take([KC, PB * IMG])
        xTb = rx.take([2, KC, SEQ])
        qkT = rx.take([2, 2, KC, SEQ])
        qT, kT = qkT[:, :, 0], qkT[:, :, 1]
        tcos = rx.take([2, KC, SEQ])
        tsin = rx.take([2, KC, SEQ])
        vb = rx.take([2, 2, D])
        sA1, sB1 = rx.take([P]), rx.take([SEQ])
        pA, pB = rx.take([P]), rx.take([SEQ])
        pT1, pT2 = rx.take([SEQ]), rx.take([SEQ - P])
        oTb = rx.take([KC, P])
        oTi = rx.take([KC, PB * IMG])
        nmax, smax, psum_, rsum = (rx.take([2]) for _ in range(4))
        rg = Region(X, XE)
        b1b = rg.take([E1 * F1])
        early = Region(X, XE, rg.at)
        inrow1, intile1 = early.take([TOPK * NT, P], BF16), early.take([TOPK * NT, 3, SLOT1], BF16)
        back1 = rg.take([NT, D])
        mid1 = rg.take([2, F0])
        assert early.at <= rg.at
        pay1 = rg.take([NT, PAY1])
        back0 = pay1.rearrange("p t n -> p (t n)")[:, 0:NT * D].rearrange("p (t n) -> p t n", t=NT)
        wall1 = rg.take([SLOT1])
        x2G = rg.take([2, KC, P])
        x1in = rg.take([2, PAY1])
        y1buf = rg.take([2, D])
        x1h, x1l = rg.take([2, KC, P], F16), rg.take([2, KC, P], F16)
        hh1 = rg.take([2, F0])
        h1Th, h1Tl = rg.take([2, 4, P], F16), rg.take([2, 4, P], F16)
        csum = rg.take([D])
        w1h = Y[:, 0:W1W // 2].bitcast(F16)
        w1l = Y[:, W1W // 2:W1W].bitcast(F16)
        w0h = X[:, 0:XW // 2].bitcast(F16)
        w0l = X[:, XW // 2:XW].bitcast(F16)

        text_loaded = sem("text_loaded")
        patches_loaded = sem("patches_loaded")
        small_loaded = sem("small_loaded")
        consts_ready = sem("consts_ready")
        pads_zeroed = sem("pads_zeroed")
        dve_done = sem("dve_done")
        act_done = sem("act_done")
        var_ready = sem("var_ready")
        std_ready = sem("std_ready")
        nega_ready = sem("nega_ready")
        patch_normed = sem("patch_normed")
        patch_tr = sem("patch_tr")
        patch_copied = sem("patch_copied")
        tokb_psum = sem("tokb_psum")
        wt_scaled = sem("wt_scaled")
        tok_psum = sem("tok_psum")
        tok_added = sem("tok_added")
        tok_ready = sem("tok_ready")
        xn_ready = sem("xn_ready")
        xn_tr = sem("xn_tr")
        xT_copied = sem("xT_copied")
        bcd_psum = sem("bcd_psum")
        bc_copied = sem("bc_copied")
        dl_copied = sem("dl_copied")
        abs_ready = sem("abs_ready")
        sp_ready = sem("sp_ready")
        delta_ready = sem("delta_ready")
        decay_ready = sem("decay_ready")
        sc_ready = sem("sc_ready")
        y_psum = sem("y_psum")
        z_psum = sem("z_psum")
        g_ready = sem("g_ready")
        o_psum = sem("o_psum")
        h_added = sem("h_added")
        hb_added = sem("hb_added")
        stage_full = [sem("stage_full0"), sem("stage_full1")]
        stage_free = sem("stage_free")
        w_high = sem("w_high")
        own_high = sem("own_high")
        x2_copied = sem("x2_copied")
        stats_ready = sem("stats_ready")
        route_psum = sem("route_psum")
        logits_ready = sem("logits_ready")
        sig_ready = sem("sig_ready")
        choice_ready = sem("choice_ready")
        count_psum = sem("count_psum")
        pay_ready = sem("pay_ready")
        x_in = [sem("x_in0"), sem("x_in1")]
        x_tr = sem("x_tr")
        x_w = sem("x_w")
        x_hi = sem("x_hi")
        x_lo = sem("x_lo")
        gate_psum = sem("gate_psum")
        up_psum = sem("up_psum")
        act_out = sem("act_out")
        h_ready = sem("h_ready")
        hT_psum = sem("hT_psum")
        hT_hi = sem("hT_hi")
        hT_lo = sem("hT_lo")
        y_done = sem("y_done")
        y_copied = sem("y_copied")
        y_out = [sem("y_out0"), sem("y_out1")]
        hot_ready = sem("hot_ready")
        map_psum = sem("map_psum")
        source_ready = sem("source_ready")
        dest_ready = sem("dest_ready")
        rows_stored = sem("rows_stored")
        taken_back = [sem(f"taken_back{i}") for i in range(len(RUNS))]
        added_back = sem("added_back")
        out_written = sem("out_written")
        slots_ready = sem("slots_ready")
        amax_ready = sem("amax_ready")
        amax_row = sem("amax_row")
        amax_all = sem("amax_all")
        amax_psum = sem("amax_psum")
        scale_ready = sem("scale_ready")
        attn_loaded = sem("attn_loaded")
        xTi_copied = sem("xTi_copied")
        xTb_copied = sem("xTb_copied")
        xTb_image = sem("xTb_image")
        q_psum = sem("q_psum")
        k_psum = sem("k_psum")
        v_psum = sem("v_psum")
        rope_mul = sem("rope_mul")
        rope_done = sem("rope_done")
        v_copied = sem("v_copied")
        s_psum = sem("s_psum")
        s_max = sem("s_max")
        p_exp = sem("p_exp")
        p_normed = sem("p_normed")
        pt_psum = sem("pt_psum")
        pt_copied = sem("pt_copied")
        ot_psum = sem("ot_psum")
        ot_copied = sem("ot_copied")
        pr_psum = sem("pr_psum")
        bf_added = sem("bf_added")
        h3_added = sem("h3_added")
        experts1_loaded = sem("experts1_loaded")
        small1_loaded = sem("small1_loaded")
        rest_ready = sem("rest_ready")
        c_copied = sem("c_copied")
        added_pool = sem("added_pool")
        gb_ready = sem("gb_ready")
        gb_split = sem("gb_split")
        c_psum = sem("c_psum")
        biased = sem("biased")
        y_based = sem("y_based")

        NSMALL = 6

        class Layer0:
            scale, unscale = hscale[:, 0:1], hscale[:, 1:2]
            tiles, before, experts = SLOT0, 0, G0
            rows_in, rows_out = xs0, ys0
            wh, wl, per_expert = w0h, w0l, E0 * W0N
            x, y, xhi, xlo, mid, act_, hi, lo = xin, ybuf, xh, xl, sg, hh, hTh, hTl

            def w_in(e, k, up):
                return e * W0N + (up * KC + k) * F0

            def w_out(e, c):
                return e * W0N + 2 * KC * F0 + c * D
            ups, y_banks = 2, (6, 6)

        class Layer1:
            scale, unscale = hscale[:, 2:3], hscale[:, 3:4]
            tiles, before, experts = SLOT1, SLOT0, E1
            rows_in, rows_out = xs1, ys1
            wh, wl, per_expert = w1h, w1l, W1N
            x, y, xhi, xlo, mid, act_, hi, lo = x1in, y1buf, x1h, x1l, mid1, hh1, h1Th, h1Tl

            def w_in(s, k, up):
                return (s * KC + k) * F0

            def w_out(s, c):
                return KC * F1 + (4 * s + c) * D
            ups, y_banks = 1, (6, 2)
        block = ctx.enter_context(nc.Block())

        def dump(sp):
            if stop == 1:
                sp.wait_ge(text_loaded, 16)
            if stop == 2:
                sp.wait_ge(hb_added, NT)
            if stop == 3:
                sp.wait_ge(added_back, len(RUNS))
            if stop == 4:
                sp.wait_ge(h3_added, NT)
                sp.wait_ge(stage_free, AHEAD + XW // CW + W1W // CW)
            n = store_out(sp)
            sp.wait_ge(out_written, 16 * n)

        def store_out(sp, n=0):
            for k in OUT_STORES:
                t, tiles, r = RUNS[k]
                if stop > 4 and k in OUT_DVE:
                    sp.wait_ge(added_back, len(BACK_DVE) + 2 * (OUT_DVE.index(k) + 1))
                if stop > 4 and k in OUT_POOL:
                    sp.wait_ge(added_pool, len(BACK_POOL) + 2 * (OUT_POOL.index(k) + 1))
                if r == P:
                    sp.dma_start(out[t:t + tiles, IMG:SEQ, :].rearrange("b s d -> s b d"), h[:, t:t + tiles, :])\
                        .then_inc(out_written, 16)
                    n += 1
                    continue
                for i in range(r // IMG):
                    first = PER * (t - BATCH)
                    to = out[first + i:first + i + 1] if tiles == 1 else \
                        out[first:first + PER * tiles].rearrange("(j i) s d -> i j s d", i=PER)[i]
                    sp.dma_start(to[:, 0:IMG, :].rearrange("b s d -> s b d"), h[i * IMG:(i + 1) * IMG, t:t + tiles, :])\
                        .then_inc(out_written, 16)
                    n += 1
            return n

        def act_dispatch(act, before, x2T_, bank0):
            def copies(t, slot, j):
                act.wait_ge(xn_tr, before[0] * NT + AHEAD + t + 1)
                nc.scalar.activation(x2T_[:, slot, :, :], PS[:, bank0 + slot, 0:KC * P].rearrange("p (k r) -> p k r", k=KC),
                                     ACT.Copy).then_inc(x2_copied, 1)
            pipelined(act, NT, copies)

        def pe_route(pe, before, x2T_, pay_, weights, n, bank0):
            def product(t, slot):
                pe.wait_ge(x2_copied, before[1] * NT + t + 1)
                for k in range(KC):
                    ins = nc.tensor.matmul(PS[:, 6, bass.ds(t * n, n)], x2T_[:, slot, k, :], weights[:, k, :],
                                           start=(k == 0), stop=(k == KC - 1))
                ins.then_inc(route_psum, 1)

            for t in range(NT):
                pe.wait_ge(xn_ready, before[0] * NT + t + 1)
                for k in range(KC):
                    ins = nc.tensor.transpose(PS[:, bank0 + t % 2, k * P:(k + 1) * P], pay_[:, t, k * P:(k + 1) * P], k_ident)
                ins.then_inc(xn_tr, 1)
                if t:
                    product(t - 1, (t - 1) % 2)
            product(NT - 1, (NT - 1) % 2)

        def pe_count(pe, done):
            pe.wait_ge(choice_ready, done + 1)
            flat = ohb.rearrange("p g t -> p (g t)")
            nc.tensor.matmul(PS[:, 7, 0:4 * NT], upper[:, :], flat, start=True, stop=True)
            nc.tensor.matmul(PS[:, 7, 128:128 + 4 * NT], onesb[:, :], flat, start=True, stop=True)\
                .then_inc(count_psum, 1)

        def pe_slots(pe, done, n, tiles, inrow, intile):
            for i in range(n):
                if i % (n // 2) == 0:
                    pe.wait_ge(hot_ready, 2 * done + i // (n // 2) + 1)
                ins = nc.tensor.matmul(PS[:, 7, 0:3 * tiles], inrow[:, i, :], intile[:, i, :, :].rearrange("p a b -> p (a b)"),
                                       start=(i == 0), stop=(i == n - 1))
            ins.then_inc(map_psum, 1)

        def dve_norm(dve, pay_):
            def norm(t, slot, j):
                nc.vector.tensor_scalar(pay_[:, bass.ds(t, 1), 0:D], h[:, bass.ds(t, 1), :], mv[:, bass.ds(t, 1), 0],
                                        rstd[:, bass.ds(t, 1)], ALU.subtract, ALU.mult).then_inc(xn_ready, 1)
            pipelined(dve, NT, norm)

        def moments_of_all(dve, chain, layer):
            dve.wait_ge(stats_ready, layer * NT)
            for t in range(NT):
                ins = nc.vector.bn_aggr(mv[:, t, :], stats[:, t, 0, :])
            chain.link(ins)

        def over(ap, n):
            return ap.unsqueeze(1).broadcast_to([P, n, NT])

        def first_max(chain, values, top, hot):
            chain.link(nc.vector.tensor_reduce(top, values.rearrange("p g t -> p t g"), AX, ALU.max))
            chain.link(nc.vector.tensor_tensor(hot, values, over(top, 4), ALU.is_equal))
            taken = newt
            chain.link(nc.vector.tensor_copy(taken, hot[:, 0, :]))
            for g in range(1, 4):
                chain.link(nc.vector.tensor_tensor(hot[:, g, :], hot[:, g, :], taken, ALU.is_gt))
                chain.link(nc.vector.tensor_tensor(taken, taken, hot[:, g, :], ALU.max))

        def sum_over(chain, out_, values):
            chain.link(nc.vector.tensor_reduce(out_, values.rearrange("p g t -> p t g"), AX, ALU.add))

        def positions(dve, chain, choices, tiles, done, inrow, intile):
            hot = rc[:, 0:4, :]
            if choices == 2:
                chain.link(nc.vector.tensor_tensor(hot, oh[:, 0], oh[:, 1], ALU.add))
                chain.link(nc.vector.tensor_tensor(hot, hot, over(k_valid, 4), ALU.mult))
            else:
                chain.link(nc.vector.tensor_tensor(hot, oh[:, 0], over(k_valid, 4), ALU.mult))
            nc.vector.tensor_copy(ohb[:, :, :], hot).then_inc(choice_ready, 1)
            dve.wait_ge(count_psum, done + 1)
            before_, total, upto = rc[:, 0:4, :], rc[:, 4:8, :], rc[:, 8:12, :]
            flat = lambda ap: ap.rearrange("p g t -> p (g t)")
            nc.vector.tensor_copy(flat(before_), PS[:, 7, 0:4 * NT])
            chain.link(nc.vector.tensor_copy(flat(total), PS[:, 7, 128:128 + 4 * NT]))
            chain.link(nc.vector.tensor_tensor_scan(flat(upto), k_reset, flat(total), 0.0, ALU.mult, ALU.add))
            n_of = upto[:, :, NT - 1:NT].broadcast_to([P, 4, NFULL])
            full = raf[:, 0:4 * NFULL].rearrange("p (g k) -> p g k", g=4)
            chain.link(nc.vector.tensor_tensor(full, n_of, k_fill, ALU.is_gt))
            tl, st, sl = sm[:, 0:4], sm[:, 4:8], sm[:, 8:12]
            chain.link(nc.vector.tensor_reduce(tl, full, AX, ALU.add))
            chain.link(nc.vector.memset(st[:, 0:1], 0.0))
            for g in range(1, 4):
                chain.link(nc.vector.tensor_tensor(st[:, g:g + 1], st[:, g - 1:g], tl[:, g - 1:g], ALU.add))
            chain.link(nc.vector.tensor_scalar(sl, st, float(P), None, ALU.mult))
            chain.link(nc.vector.tensor_tensor(upto, upto, total, ALU.subtract))
            chain.link(nc.vector.tensor_tensor(before_, before_, upto, ALU.add))
            chain.link(nc.vector.tensor_tensor(before_, before_, sl.unsqueeze(2).broadcast_to([P, 4, NT]), ALU.add))
            for c in range(choices):
                chain.link(nc.vector.tensor_tensor(total, oh[:, c], before_, ALU.mult))
                sum_over(chain, posf[:, c, :], total)
            slots_of = posf[:, 0:choices, :]
            chain.link(nc.vector.tensor_tensor(slots_of, slots_of, k_far.unsqueeze(1).broadcast_to([P, choices, NT]), ALU.add))
            chain.link(nc.vector.tensor_copy(pos[:, 0:choices, :], slots_of))
            chain.link(nc.vector.tensor_scalar(low7[:, 0:choices, :], pos[:, 0:choices, :], P - 1, None, ALU.bitwise_and))
            chain.link(nc.vector.tensor_scalar(high7[:, 0:choices, :], pos[:, 0:choices, :], 7, None,
                                               ALU.logical_shift_right))
            n = choices * NT
            chain.link(nc.vector.tensor_copy(slots_of, high7[:, 0:choices, :]))
            each = lambda ap, m: ap.rearrange("p c t -> p (c t)").unsqueeze(2).broadcast_to([P, n, m])
            along = lambda ap, m: ap.unsqueeze(1).broadcast_to([P, n, m])
            chain.link(nc.vector.tensor_tensor(intile[:, :, 2, :], each(slots_of, tiles), along(k_slot[:, 0:tiles], tiles),
                                               ALU.is_equal))
            chain.link(nc.vector.tensor_copy(slots_of, low7[:, 0:choices, :]))
            nc.vector.tensor_tensor(intile[:, :, 0, :], intile[:, :, 2, :],
                                    k_tile[:, 0:n].unsqueeze(2).broadcast_to([P, n, tiles]), ALU.mult)
            nc.vector.tensor_scalar(intile[:, :, 1, :], intile[:, :, 2, :], k_row, None, ALU.mult)
            half = n // 2
            for c0 in (0, half):
                nc.vector.tensor_tensor(inrow[:, c0:c0 + half, :], each(slots_of, P)[:, c0:c0 + half],
                                        along(k_iota, P)[:, c0:c0 + half], ALU.is_equal).then_inc(hot_ready, 1)
            sf = slotf[:, 0:tiles]
            chain.link(nc.vector.tensor_scalar(sf, k_slot[:, 0:tiles], st[:, 1:2], None, ALU.is_ge))
            for g in (2, 3):
                chain.link(nc.vector.scalar_tensor_tensor(out=sf, in0=k_slot[:, 0:tiles], scalar=st[:, g:g + 1],
                                                          in1=sf, op0=ALU.is_ge, op1=ALU.add))
            nc.vector.tensor_copy(slote[:, 0:tiles], sf).then_inc(slots_ready, 1)
            dve.wait_ge(map_psum, done + 1)
            tile_, row_, taken = (PS[:, 7, i * tiles:(i + 1) * tiles] for i in range(3))
            place, from_, to = (tok[:, i, 0:tiles] for i in range(3))
            chain.link(nc.vector.tensor_copy(from_, row_))
            chain.link(nc.vector.scalar_tensor_tensor(out=place, in0=tile_, scalar=float(P), in1=from_, op0=ALU.mult,
                                                      op1=ALU.add))
            chain.link(nc.vector.tensor_scalar(from_, place, float(TOKENS), -float(TOKENS), ALU.is_ge, ALU.mult))
            chain.link(nc.vector.tensor_tensor(from_, from_, place, ALU.add))
            nc.vector.tensor_copy(source[:, 0:tiles], from_).then_inc(source_ready, 1)
            chain.link(nc.vector.tensor_scalar(to, taken, -float(DUMP), float(DUMP), ALU.mult, ALU.add))
            chain.link(nc.vector.tensor_tensor(to, to, place, ALU.add))
            nc.vector.tensor_copy(dest[:, 0:tiles], to).then_inc(dest_ready, 1)

        def dve_bound(dve, chain, weights, bound):
            chain.link(nc.vector.tensor_reduce(amax[:, 0:1], weights, AXS[len(weights.shape) - 2], ALU.max,
                                               apply_absolute_value=True))
            bound(amax[:, 0:1])
            dve.sem_inc(amax_ready, 1)

        def dve_scale(dve, chain, layer):
            dve.wait_ge(amax_psum, 2 * layer + 1)
            nc.vector.tensor_reduce(amax[0:1, 1:2], PS[0:1, 3, 0:P], AX, ALU.max).then_inc(amax_row, 1)
            dve.wait_ge(amax_psum, 2 * layer + 2)
            top, scale_, un = amax[:, 2:3], hscale[:, 2 * layer:2 * layer + 1], hscale[:, 2 * layer + 1:2 * layer + 2]
            chain.link(nc.vector.tensor_copy(top, PS[:, 3, 256:257]))
            if layer == 0:
                chain.link(nc.vector.tensor_tensor(top, top, top, ALU.mult))
                chain.link(nc.vector.tensor_scalar(un, top, float(D * D) / 2 ** 15, 1e-20, ALU.mult, ALU.max))
            else:
                chain.link(nc.vector.tensor_scalar(un, top, 1.0 / 2 ** 15, 1e-20, ALU.mult, ALU.max))
            chain.link(nc.vector.reciprocal(scale_, un))
            dve.sem_inc(scale_ready, 1)

        def pe_scale(pe, layer):
            pe.wait_ge(amax_ready, layer + 1)
            nc.tensor.transpose(PS[0:1, 3, 0:P], amax[:, 0:1], k_ident).then_inc(amax_psum, 1)
            pe.wait_ge(amax_row, layer + 1)
            nc.tensor.matmul(PS[:, 3, 256:257], onesf[0:1, :], amax[0:1, 1:2], start=True, stop=True).then_inc(amax_psum, 1)

        def ffn_pe(pe, L):
            def transpose_x(i, slot, j):
                pe.wait_ge(x_in[slot], 16 * (j + (L.before + 1) // 2 + 1))
                for k in range(KC):
                    ins = nc.tensor.transpose(PS[:, 7, k * P:(k + 1) * P], L.x[:, slot, k * P:(k + 1) * P], k_ident)
                ins.then_inc(x_tr, 1)

            def products_in(i, s, base, slot):
                if s == 0:
                    pe.wait_ge(x_lo, L.before + i + 1)
                for u in range(L.ups):
                    n = 0
                    for k in range(KC):
                        off = base + L.w_in(s, k, u)
                        for x_, w_ in ((L.xhi, L.wh), (L.xhi, L.wl), (L.xlo, L.wh)):
                            ins = nc.tensor.matmul(PS[:, 2 * u + s, 0:F0], x_[:, slot, k, :], w_[:, bass.ds(off, F0)],
                                                   start=(n == 0), stop=(n == 3 * KC - 1))
                            n += 1
                    ins.then_inc(up_psum if u else gate_psum, 1)

            def transpose_h(i, s):
                pe.wait_ge(h_ready, 2 * (L.before + i) + s + 1)
                for c in range(4):
                    ins = nc.tensor.transpose(PS[:, 4 + s, c * P:(c + 1) * P], L.act_[:, s, c * P:(c + 1) * P], k_ident)
                ins.then_inc(hT_psum, 1)

            def product_out(i, s, base, slot):
                pe.wait_ge(hT_lo, 2 * (L.before + i) + s + 1)
                if s == 0:
                    wait_from(pe, y_copied, L.before + i + 1 - len(set(L.y_banks)))
                for c in range(4):
                    off = base + L.w_out(s, c)
                    for n, (h_, w_) in enumerate(((L.hi, L.wh), (L.hi, L.wl), (L.lo, L.wh))):
                        ins = nc.tensor.matmul(PS[:, L.y_banks[slot], 0:D], h_[:, s, c, :], w_[:, bass.ds(off, D)],
                                               start=(s == 0 and c == 0 and n == 0), stop=(s == 1 and c == 3 and n == 2))
                if s == 1:
                    ins.then_inc(y_done, 1)

            def base_of(i):
                return pe.value_load(slote[0:1, bass.ds(i, 1)], min_val=0, max_val=L.experts - 1) * L.per_expert

            carried = [None, None]

            def tile(i, slot, j):
                base = base_of(i)
                if known(i, 0):
                    transpose_x(0, 0, 0)
                products_in(i, 0, base, slot)
                if not known(i, 0):
                    last = carried[0] if slot == 1 or isinstance(i, int) and carried[1] == i - 1 else base_of(i - 1)
                    transpose_h(i - 1, 1)
                if not known(i, L.tiles - 1):
                    transpose_x(i + 1, 1 - slot, j + slot)
                if not known(i, 0):
                    product_out(i - 1, 0, last, 1 - slot)
                products_in(i, 1, base, slot)
                transpose_h(i, 0)
                if not known(i, 0):
                    product_out(i - 1, 1, last, 1 - slot)
                carried[:] = [base, i if isinstance(i, int) else None]
            pipelined(pe, L.tiles, tile)
            n = L.tiles - 1
            base = base_of(n)
            product_out(n, 0, base, n % 2)
            transpose_h(n, 1)
            product_out(n, 1, base, n % 2)

        def ffn_act(act, L):
            def split_x(i, slot):
                act.wait_ge(x_tr, L.before + i + 1)
                nc.scalar.activation(L.xhi[:, slot].rearrange("p k r -> p (k r)"), PS[:, 7, 0:KC * P], ACT.Copy).then_inc(x_hi, 1)

            def nonlinear(i, s):
                step = 2 * (L.before + i) + s + 1
                if L is Layer0:
                    act.wait_ge(gate_psum, step)
                    nc.scalar.activation(L.mid[:, s, :], PS[:, s, 0:F0], ACT.Silu).then_inc(act_out, 1)
                else:
                    act.wait_ge(biased, 2 * i + s + 1)
                    nc.scalar.activation(L.act_[:, s, :], L.mid[:, s, :], ACT.Gelu).then_inc(h_ready, 1)

            def split_h(i, s):
                act.wait_ge(hT_psum, 2 * (L.before + i) + s + 1)
                nc.scalar.activation(L.hi[:, s, :, :].rearrange("p c r -> p (c r)"), PS[:, 4 + s, 0:F0], ACT.Copy,
                                     scale=L.scale)\
                    .then_inc(hT_hi, 1)

            def copy_y(i, slot, j):
                if L is Layer0:
                    act.wait_ge(y_done, L.before + i + 1)
                else:
                    act.wait_ge(y_based, i + 1)
                if not (isinstance(j, int) and j == 0):
                    act.wait_ge(y_out[slot], 16 * ((L.before + 1) // 2 + j))
                nc.scalar.activation(L.y[:, slot, :], PS[:, L.y_banks[slot], 0:D], ACT.Copy,
                                     scale=L.unscale if L is Layer0 else wall1[:, bass.ds(i, 1)]).then_inc(y_copied, 1)

            def tile(i, slot, j):
                if known(i, 0):
                    split_x(0, 0)
                if L is Layer0:
                    nonlinear(i, 0)
                if not known(i, 0):
                    split_h(i - 1, 1)
                if L is not Layer0:
                    nonlinear(i, 0)
                if not known(i, L.tiles - 1):
                    split_x(i + 1, 1 - slot)
                if L is Layer0:
                    nonlinear(i, 1)
                split_h(i, 0)
                if L is not Layer0:
                    nonlinear(i, 1)
                if not known(i, 0):
                    copy_y(i - 1, 1 - slot, j + slot - 1)
            pipelined(act, L.tiles, tile)
            n = L.tiles - 1
            split_h(n, 1)
            copy_y(n, n % 2, n // 2)

        def ffn_pool(pool, L):
            layer = 1 if L is Layer1 else 0
            pool.wait_ge(rows_stored, 16 * (layer + 1))
            pool.wait_ge(source_ready, layer + 1)
            for n in range(L.tiles + 3):
                if n < L.tiles:
                    if n >= 2:
                        pool.wait_ge(x_tr, L.before + n - 1)
                        pool.wait_ge(x_w, L.before + n - 1)
                    nc.gpsimd.indirect_dma_start(
                        out=L.x[:, n % 2, :], out_offset=None, in_=L.rows_in,
                        in_offset=bass.IndirectOffsetOnAxis(ap=source[:, n:n + 1], axis=0)).then_inc(x_in[n % 2], 16)
                if n == 0:
                    pool.wait_ge(dest_ready, layer + 1)
                i = n - 3
                if i < 0:
                    continue
                pool.wait_ge(y_copied, L.before + i + 1)
                if L.before + i:
                    last = 1 - i % 2
                    pool.wait_ge(y_out[last], 16 * ((L.before + 1 - last) // 2 + (i + 1 - last) // 2))
                nc.gpsimd.indirect_dma_start(out=L.rows_out, out_offset=bass.IndirectOffsetOnAxis(ap=dest[:, i:i + 1], axis=0),
                                             in_=L.y[:, i % 2, :], in_offset=None).then_inc(y_out[i % 2], 16)

        def store_rows(sp, rows_, pay_, n):
            sp.wait_ge(pay_ready, n)
            sp.dma_start(rows_.rearrange("(t p) n -> p t n", p=P), pay_).then_inc(rows_stored, 16)

        def take_back(sp, L, choice, buffer, tile0, n, r, done):
            rows_ = L.rows_out[choice * TOKENS + tile0 * P:choice * TOKENS + (tile0 + n) * P, :]
            sp.dma_start(buffer[0:r, tile0:tile0 + n, :], rows_.rearrange("(t p) n -> p t n", p=P)[0:r, :, :])\
                .then_inc(done, 16)

        def ffn_dve(dve, L):
            def split_x(i, slot, j, e):
                dve.wait_ge(x_hi, L.before + i + 1)
                nc.vector.tensor_tensor(L.xlo[:, slot].rearrange("p k r -> p (k r)"), PS[:, 7, 0:KC * P],
                                        L.xhi[:, slot].rearrange("p k r -> p (k r)"), ALU.subtract).then_inc(x_lo, 1)
                dve.wait_ge(x_in[slot], 16 * (j + (L.before + 1) // 2 + 1))
                if L is Layer0:
                    nc.vector.tensor_copy(wall[:, bass.ds(i, 1), :], L.x[:, slot:slot + 1, D:PAY0]).then_inc(x_w, 1)
                else:
                    nc.vector.tensor_copy(wall1[:, bass.ds(i, 1)], L.x[:, slot, bass.ds(e + D, 1)]).then_inc(x_w, 1)

            def combine(i, s, bias):
                step = 2 * (L.before + i) + s + 1
                if L is Layer0:
                    dve.wait_ge(x_w, i + 1)
                    dve.wait_ge(up_psum, step)
                    dve.wait_ge(act_out, step)
                    nc.vector.scalar_tensor_tensor(out=L.act_[:, s, :].unsqueeze(1), in0=PS[:, 2 + s, 0:F0].unsqueeze(1),
                                                   scalar=wall[:, bass.ds(i, 1), s], in1=L.mid[:, s, :].unsqueeze(1),
                                                   op0=ALU.mult, op1=ALU.mult).then_inc(h_ready, 1)
                else:
                    dve.wait_ge(gate_psum, step)
                    nc.vector.tensor_tensor(L.mid[:, s, :], PS[:, s, 0:F0], b1b[:, bass.ds(bias + s * F0, F0)],
                                            ALU.add).then_inc(biased, 1)

            def split_h(i, s):
                dve.wait_ge(hT_hi, 2 * (L.before + i) + s + 1)
                nc.vector.scalar_tensor_tensor(out=L.lo[:, s, :, :].rearrange("p c r -> p (c r)"), in0=PS[:, 4 + s, 0:F0],
                                               scalar=L.scale, in1=L.hi[:, s, :, :].rearrange("p c r -> p (c r)"),
                                               op0=ALU.mult, op1=ALU.subtract).then_inc(hT_lo, 1)

            def base_y(i, slot, e):
                if L is Layer0:
                    return
                dve.wait_ge(y_done, L.before + i + 1)
                y_ = PS[:, L.y_banks[slot], 0:D].unsqueeze(1)
                nc.vector.scalar_tensor_tensor(out=y_, in0=y_, scalar=L.unscale, in1=rest1[:, bass.ds(e, 1), :],
                                               op0=ALU.mult, op1=ALU.add).then_inc(y_based, 1)

            def expert_of(i):
                if L is Layer0:
                    return None
                return dve.value_load(slote[0:1, bass.ds(i, 1)], min_val=0, max_val=E1 - 1)

            carried, past = [None, None], [None, None]

            def tile(i, slot, j):
                e = carried[0] if slot == 1 or isinstance(i, int) and carried[1] == i else expert_of(i)
                if known(i, 0):
                    split_x(0, 0, 0, e)
                bias = None if L is Layer0 else e * F1
                combine(i, 0, bias)
                if not known(i, 0):
                    split_h(i - 1, 1)
                if not known(i, L.tiles - 1):
                    following = expert_of(i + 1)
                    split_x(i + 1, 1 - slot, j + slot, following)
                    carried[:] = [following, i + 1 if isinstance(i, int) else None]
                combine(i, 1, bias)
                split_h(i, 0)
                if not known(i, 0):
                    last = past[0] if slot == 1 or isinstance(i, int) and past[1] == i - 1 else expert_of(i - 1)
                    base_y(i - 1, 1 - slot, last)
                past[:] = [e, i if isinstance(i, int) else None]
            pipelined(dve, L.tiles, tile)
            n = L.tiles - 1
            split_h(n, 1)
            base_y(n, n % 2, past[0])

        def sp_rest(sp):
            store_rows(sp, xs0, pay, 1)
            for k in range(2):
                sp.wait_ge(y_out[k], 16 * ((SLOT0 + 1 - k) // 2))
            for k, (t, n, r) in enumerate(RUNS):
                take_back(sp, Layer0, 0, back, t, n, r, taken_back[k])
            if stop > 3:
                sp_attention(sp)
            if stop > 4:
                sp_experts1(sp)

        def act_rest(act, roots):
            roots(4)
            act_dispatch(act, (1, 0), x2T, 0)
            act.wait_ge(logits_ready, 1)
            nc.scalar.activation(rb[:, :, :], ra[:, :, :], ACT.Sigmoid).then_inc(sig_ready, 1)
            act.wait_ge(scale_ready, 1)
            ffn_act(act, Layer0)
            if stop > 3:
                act_attention(act, roots)
            if stop > 4:
                act_experts1(act, roots)

        def pe_rest(pe):
            pe_route(pe, (1, 0), x2T, pay, wr0, 12, 0)
            pe_scale(pe, 0)
            pe_count(pe, 0)
            pe_slots(pe, 0, NT, SLOT0, inrow0, intile0)
            pe.wait_ge(stage_free, AHEAD + XW // CW)
            pe.wait_ge(slots_ready, 1)
            pe.wait_ge(dest_ready, 1)
            ffn_pe(pe, Layer0)
            if stop > 3:
                pe_attention(pe)
            if stop > 4:
                pe_experts1(pe)

        def pool_rest(pool):
            ffn_pool(pool, Layer0)
            for k in BACK_POOL:
                t, n, r = RUNS[k]
                pool.wait_ge(taken_back[k], 16)
                nc.gpsimd.tensor_tensor(h[0:r, t:t + n, :], h[0:r, t:t + n, :], back[0:r, t:t + n, :], ALU.add)\
                    .then_inc(added_pool, 1)
            if stop > 3:
                pool_attention(pool)
            if stop > 4:
                pool_experts1(pool)

        def dve_rest(dve, chain, inverse_roots):
            moments_of_all(dve, chain, 1)
            inverse_roots()
            dve_norm(dve, pay)
            dve.wait_ge(stage_free, AHEAD + XW // CW)
            gate_up = w0h.rearrange("p (e n) -> p e n", e=G0 * E0)[:, :, 0:2 * KC * F0]
            dve_bound(dve, chain, gate_up, lambda a_: None)
            dve_scale(dve, chain, 0)
            dve.wait_ge(route_psum, NT)
            nc.vector.tensor_copy(upper[:, :], k_upper)
            nc.vector.tensor_copy(ra[:, :, :], PS[:, 6, 0:12 * NT].rearrange("p (t g) -> p g t", g=12))\
                .then_inc(logits_ready, 1)
            dve.wait_ge(logits_ready, 1)
            top, score, a, b = rc[:, 8, :], rc[:, 9, :], rc[:, 10, :], rc[:, 11, :]
            chain.link(nc.vector.tensor_scalar(rc[:, 0:4, :], ra[:, 0:4, :], SAT, None, ALU.min))
            first_max(chain, rc[:, 0:4, :], top, oh[:, 0])
            dve.wait_ge(sig_ready, 1)
            chain.link(nc.vector.tensor_reduce(score, rb[:, 0:4, :].rearrange("p g t -> p t g"), AX, ALU.max))
            chain.link(nc.vector.tensor_scalar(a, score, 1e-9, None, ALU.add))
            chain.link(nc.vector.reciprocal(a, a))
            chain.link(nc.vector.tensor_tensor(score, score, a, ALU.mult))
            u = ra[:, 0:2, :]
            micro = rb[:, 4:12, :].rearrange("p (g e) t -> p e g t", e=E0)
            for e in range(E0):
                chain.link(nc.vector.tensor_tensor(rc[:, 0:4, :], micro[:, e], oh[:, 0], ALU.mult))
                sum_over(chain, u[:, e, :], rc[:, 0:4, :])
            chain.link(nc.vector.tensor_tensor(a, u[:, 0, :], u[:, 1, :], ALU.add))
            chain.link(nc.vector.tensor_scalar(a, a, 1e-9, None, ALU.add))
            chain.link(nc.vector.reciprocal(a, a))
            chain.link(nc.vector.tensor_tensor(a, a, score, ALU.mult))
            for e in range(E0):
                chain.link(nc.vector.tensor_tensor(pay[:, :, D + e], u[:, e, :], a, ALU.mult))
            dve.sem_inc(pay_ready, 1)
            positions(dve, chain, 1, SLOT0, 0, inrow0, intile0)
            ffn_dve(dve, Layer0)
            for k in BACK_DVE + BACK_POOL:
                t, n, r = RUNS[k]
                if k in BACK_DVE:
                    dve.wait_ge(taken_back[k], 16)
                    nc.vector.tensor_tensor(h[0:r, t:t + n, :], h[0:r, t:t + n, :], back[0:r, t:t + n, :], ALU.add)\
                        .then_inc(added_back, 1)
                    dve.wait_ge(added_back, BACK_DVE.index(k) + 1)
                else:
                    dve.wait_ge(added_pool, BACK_POOL.index(k) + 1)
                for i in range(t, t + n):
                    nc.vector.bn_stats(stats[:, i, 0, :], h[:, i, :]).then_inc(stats_ready, 1)
            if stop > 3:
                dve_attention(dve, chain, inverse_roots)
            if stop > 4:
                dve_experts1(dve, chain, inverse_roots)

        NF = 2 * NT

        def sp_attention(sp):
            sp.wait_ge(y_done, SLOT0)
            sp.dma_start(X[:, 0:NATT], wattn).then_inc(attn_loaded, 16)
            sp.dma_start(rowsF.rearrange("p a n -> p (a n)"), rows_f.broadcast_to([P, 2 * D])).then_inc(attn_loaded, 16)
            sp.dma_start(small1, wsmall1).then_inc(small1_loaded, 16)
            sp.dma_start(b2all.rearrange("p a n -> p (a n)"), b2rows.broadcast_to([P, E1 * D])).then_inc(small1_loaded, 16)
            first = XW // CW
            sp.wait_ge(added_back, len(BACK_DVE))
            sp.wait_ge(added_pool, len(BACK_POOL))
            with sp.Fori(0, W1W // CW // 2) as n:
                for k in range(2):
                    sp.wait_ge(stage_free, first + 2 * n + (k + 1))
                    sp.dma_start(stage[:, k, :], w1[:, bass.ds((2 * n + k) * CW, CW)]).then_inc(stage_full[k], 16)

        def heads(eng, body):
            body(0, 0)
            body(1, 1)
            with eng.Fori(1, BATCH // 2 - 1) as j:
                body(2 * j, 0)
                body(2 * j + 1, 1)
            body(BATCH - 2, 0)
            body(BATCH - 1, 1)

        def pe_attention(pe):
            pe.wait_ge(attn_loaded, 32)
            for n in range(IT):
                pe.wait_ge(xn_ready, NF + n + 1)
                if n:
                    pe.wait_ge(xTi_copied, n)
                for k in range(KC):
                    ins = nc.tensor.transpose(PS[:, 7, k * P:(k + 1) * P], xnF[:, n % 2, k * P:(k + 1) * P], k_ident)
                ins.then_inc(xn_tr, 1)

            def text(b, slot):
                pe.wait_ge(xn_ready, NF + IT + b + 1)
                if known(b, 0):
                    pe.wait_ge(xTi_copied, IT)
                else:
                    pe.wait_ge(xTb_copied, b)
                for k in range(KC):
                    ins = nc.tensor.transpose(PS[:, 7, k * P:(k + 1) * P], xnF[:, slot, k * P:(k + 1) * P], k_ident)
                ins.then_inc(xn_tr, 1)

            def project(b, slot):
                pe.wait_ge(xTb_copied, b + 1)
                pe.wait_ge(xTb_image, b + 1)
                for bank, w_, done in ((0, wq, q_psum), (1, wk, k_psum)):
                    for m in range(KC):
                        for k in range(KC):
                            ins = nc.tensor.matmul(PS[:, bank, m * SEQ:(m + 1) * SEQ], w_[:, k, m * P:(m + 1) * P],
                                                   xTb[:, slot, k, :], start=(k == 0), stop=(k == KC - 1))
                    ins.then_inc(done, 1)
                wait_from(pe, v_copied, b)
                for a, (c0, c1) in enumerate(((0, P), (P, SEQ))):
                    for k in range(KC):
                        ins = nc.tensor.matmul(PS[0:c1 - c0, 2, a * D:(a + 1) * D], xTb[:, slot, k, c0:c1], wv[:, k, :],
                                               start=(k == 0), stop=(k == KC - 1))
                ins.then_inc(v_psum, 1)

            def scores(b, slot):
                pe.wait_ge(rope_done, b + 1)
                for o_, q0, q1, k1 in ((0, 0, P, P), (P, P, SEQ, SEQ)):
                    for m in range(KC):
                        ins = nc.tensor.matmul(PS[0:q1 - q0, 3, o_:o_ + k1], qT[:, slot, m, q0:q1], kT[:, slot, m, 0:k1],
                                               start=(m == 0), stop=(m == KC - 1))
                ins.then_inc(s_psum, 1)

            def transpose_p(b, slot):
                pe.wait_ge(p_normed, b + 1)
                nc.tensor.transpose(PS[:, 4, 0:P], pA, k_ident)
                nc.tensor.transpose(PS[:, 4, P:SEQ], pB[0:SEQ - P, 0:P], k_ident[0:SEQ - P, 0:SEQ - P])
                nc.tensor.transpose(PS[0:SEQ - P, 4, SEQ:2 * SEQ - P], pB[0:SEQ - P, P:SEQ],
                                    k_ident[0:SEQ - P, 0:SEQ - P]).then_inc(pt_psum, 1)

            def values(b, slot):
                pe.wait_ge(pt_copied, b + 1)
                pe.wait_ge(v_copied, b + 1)
                for m in range(KC):
                    nc.tensor.matmul(PS[:, 5, m * SEQ:(m + 1) * SEQ], vb[:, slot, 0, m * P:(m + 1) * P], pT1,
                                     start=True, stop=False)
                    ins = nc.tensor.matmul(PS[:, 5, m * SEQ + P:(m + 1) * SEQ], vb[0:SEQ - P, slot, 1, m * P:(m + 1) * P],
                                           pT2[0:SEQ - P, :], start=False, stop=True)
                ins.then_inc(ot_psum, 1)

            def out_text(b, slot):
                pe.wait_ge(ot_copied, 2 * b + 2)
                wait_from(pe, h3_added, b)
                for m in range(KC):
                    ins = nc.tensor.matmul(PS[:, 6, 0:D], oTb[:, m, :], wf[:, m, :], start=(m == 0), stop=(m == KC - 1))
                ins.then_inc(pr_psum, 1)

            text(0, 0)
            text(1, 1)
            project(0, 0)

            def batch(b, slot):
                scores(b, slot)
                if not known(b, BATCH - 1):
                    project(b + 1, 1 - slot)
                transpose_p(b, slot)
                if not known(b, 0):
                    out_text(b - 1, 1 - slot)
                if not (isinstance(b, int) and b >= BATCH - 2):
                    text(b + 2, slot)
                values(b, slot)
            heads(pe, batch)
            out_text(BATCH - 1, 1)
            for n in range(IT):
                r = tile_rows(BATCH + n)
                if n == 0:
                    pe.wait_ge(h3_added, BATCH)
                for m in range(KC):
                    ins = nc.tensor.matmul(PS[0:r, 6 - n, 0:D], oTi[:, m, n * IROWS:n * IROWS + r], wf[:, m, :],
                                           start=(m == 0), stop=(m == KC - 1))
                ins.then_inc(pr_psum, 1)

        def act_attention(act, roots):
            roots(5)
            for n in range(IT):
                act.wait_ge(xn_tr, AHEAD + NF + n + 1)
                nc.scalar.activation(xTi[:, :, n * IROWS:(n + 1) * IROWS],
                                     PS[:, 7, 0:KC * P].rearrange("p (k r) -> p k r", k=KC)[:, :, 0:IROWS],
                                     ACT.Copy).then_inc(xTi_copied, 1)

            def text(b, slot):
                act.wait_ge(xn_tr, AHEAD + NF + IT + b + 1)
                nc.scalar.activation(xTb[:, slot, :, IMG:SEQ], PS[:, 7, 0:KC * P].rearrange("p (k r) -> p k r", k=KC),
                                     ACT.Copy).then_inc(xTb_copied, 1)

            def exps(b):
                act.wait_ge(s_max, b + 1)
                nc.scalar.activation(pA, sA1, ACT.Exp, bias=nmax[:, 0:1], scale=SCALE, accum_out=psum_[:, 0:1])
                nc.scalar.activation(pB[0:SEQ - P, :], sB1[0:SEQ - P, :], ACT.Exp, bias=nmax[0:SEQ - P, 1:2], scale=SCALE,
                                     accum_out=psum_[0:SEQ - P, 1:2]).then_inc(p_exp, 1)

            def copy_pt(b):
                act.wait_ge(pt_psum, b + 1)
                nc.scalar.activation(pT1, PS[:, 4, 0:SEQ], ACT.Copy)
                nc.scalar.activation(pT2[0:SEQ - P, :], PS[0:SEQ - P, 4, SEQ:2 * SEQ - P], ACT.Copy).then_inc(pt_copied, 1)

            def copy_ot(b):
                act.wait_ge(ot_psum, b + 1)
                o_ = PS[:, 5, 0:KC * SEQ].rearrange("p (k r) -> p k r", k=KC)
                nc.scalar.activation(oTb, o_[:, :, IMG:SEQ], ACT.Copy).then_inc(ot_copied, 1)
                nc.scalar.activation(oTi[:, :, bass.ds(b * IMG, IMG)], o_[:, :, 0:IMG], ACT.Copy).then_inc(ot_copied, 1)

            def chunk(n, k, j):
                act.wait_ge(stage_full[k], 16 * (XW // CW // 2 + j + 1))
                nc.scalar.activation(w1h[:, bass.ds(n * CW, CW)], stage[:, k, :], ACT.Copy).then_inc(w_high, 1)

            act.wait_ge(small1_loaded, 32)
            nc.scalar.activation(gb1, c_b1c, ACT.Gelu).then_inc(gb_ready, 1)
            text(0, 0)
            text(1, 1)

            def run(b, slot, j):
                exps(b)
                copy_pt(b)
                if not (isinstance(b, int) and b >= BATCH - 2):
                    text(b + 2, slot)
                copy_ot(b)
                chunk(b, slot, j)
            run(0, 0, 0)
            run(1, 1, 0)
            with act.Fori(1, BATCH // 2 - 1) as j:
                run(2 * j, 0, j)
                run(2 * j + 1, 1, j)
            run(BATCH - 2, 0, BATCH // 2 - 1)
            run(BATCH - 1, 1, BATCH // 2 - 1)

        def pool_attention(pool):
            pool.wait_ge(attn_loaded, 32)
            pool.wait_ge(xTi_copied, IT)

            def image(b):
                pool.wait_ge(xn_tr, AHEAD + NF + IT + b + 1)
                nc.gpsimd.tensor_copy(xTb[:, b % 2, :, 0:IMG], xTi[:, :, b * IMG:(b + 1) * IMG]).then_inc(xTb_image, 1)

            def rope(b):
                pool.wait_ge(rope_mul, 2 * b + 2)
                nc.gpsimd.tensor_tensor(qkT[:, b % 2], tcos, tsin, ALU.add).then_inc(rope_done, 1)

            def bias(b):
                pool.wait_ge(xn_ready, NF + IT + b + 1)
                nc.gpsimd.tensor_tensor(h[:, b, :], h[:, b, :], rowsF[:, 1, :], ALU.add).then_inc(bf_added, 1)

            def low(n):
                k = n % 2
                pool.wait_ge(w_high, XW // CW - ALONE + n + 1)
                nc.gpsimd.tensor_tensor(w1l[:, n * CW:(n + 1) * CW], stage[:, k, :], w1h[:, n * CW:(n + 1) * CW],
                                        ALU.subtract).then_inc(stage_free, 1)
            for n in range(IT):
                pool.wait_ge(xn_ready, NF + n + 1)
                nc.gpsimd.tensor_tensor(h[:, BATCH + n, :], h[:, BATCH + n, :], rowsF[:, 1, :], ALU.add)\
                    .then_inc(bf_added, 1)
            image(0)
            image(1)
            bias(0)
            bias(1)
            rope(0)
            for b in range(BATCH):
                if b < BATCH - 1:
                    rope(b + 1)
                if b < BATCH - 2:
                    image(b + 2)
                    bias(b + 2)
                low(b)

        def dve_attention(dve, chain, inverse_roots):
            moments_of_all(dve, chain, 2)
            inverse_roots()
            dve.wait_ge(y_done, SLOT0)

            def norm(n, t, slot):
                dve.wait_ge(xn_tr, NF + n + 1)
                nc.vector.tensor_scalar(xnF[:, slot:slot + 1, :], h[:, bass.ds(t, 1), :], mv[:, bass.ds(t, 1), 0],
                                        rstd[:, bass.ds(t, 1)], ALU.subtract, ALU.mult).then_inc(xn_ready, 1)
            for n in range(IT):
                norm(n, BATCH + n, n % 2)
            dve.wait_ge(attn_loaded, 32)

            def rope(b):
                for i, (bank, bias, done) in enumerate(((0, c_bq, q_psum), (1, c_bk, k_psum))):
                    dve.wait_ge(done, b + 1)
                    for m in range(KC):
                        nc.vector.scalar_tensor_tensor(out=tcos[:, i, m, :], in0=PS[:, bank, m * SEQ:(m + 1) * SEQ],
                                                       scalar=bias[:, m:m + 1], in1=k_cos, op0=ALU.add, op1=ALU.mult)
                        ins = nc.vector.scalar_tensor_tensor(
                            out=tsin[:, i, m, :], in0=PS[:, bank, (1 - m) * SEQ:(2 - m) * SEQ],
                            scalar=bias[:, 1 - m:2 - m], in1=k_sin if m else k_nsin, op0=ALU.add, op1=ALU.mult)
                    ins.then_inc(rope_mul, 1)

            def copy_v(b, slot):
                dve.wait_ge(v_psum, b + 1)
                nc.vector.tensor_tensor(vb[:, slot, 0, :], PS[:, 2, 0:D], rowsF[:, 0, :], ALU.add)
                nc.vector.tensor_tensor(vb[0:SEQ - P, slot, 1, :], PS[0:SEQ - P, 2, D:2 * D], rowsF[0:SEQ - P, 0, :],
                                        ALU.add).then_inc(v_copied, 1)

            def maxima(b):
                dve.wait_ge(s_psum, b + 1)
                nc.vector.tensor_tensor(sA1, PS[:, 3, 0:P], k_maskA, ALU.add)
                chain.link(nc.vector.tensor_tensor_reduce(sB1[0:SEQ - P, :], PS[0:SEQ - P, 3, P:P + SEQ],
                                                          k_maskB[0:SEQ - P, :], 1.0, -3e38, ALU.add, ALU.max,
                                                          smax[0:SEQ - P, 1:2]))
                chain.link(nc.vector.tensor_reduce(smax[:, 0:1], sA1, AX, ALU.max))
                nc.vector.tensor_scalar(nmax, smax, -SCALE, None, ALU.mult).then_inc(s_max, 1)

            def normalise_p(b):
                dve.wait_ge(p_exp, b + 1)
                chain.link(nc.vector.reciprocal(rsum, psum_))
                nc.vector.tensor_scalar(pA, pA, rsum[:, 0:1], None, ALU.mult)
                nc.vector.tensor_scalar(pB[0:SEQ - P, :], pB[0:SEQ - P, :], rsum[0:SEQ - P, 1:2], None, ALU.mult)\
                    .then_inc(p_normed, 1)

            def add_text(b):
                dve.wait_ge(bf_added, IT + b + 1)
                dve.wait_ge(pr_psum, b + 1)
                hb = h[:, bass.ds(b, 1), :]
                nc.vector.tensor_tensor(hb, PS[:, 6, 0:D].unsqueeze(1), hb, ALU.add).then_inc(h3_added, 1)
                dve.wait_ge(h3_added, b + 1)
                nc.vector.bn_stats(stats[:, bass.ds(b, 1), 0, :], hb).then_inc(stats_ready, 1)

            chain.link(nc.vector.memset(smax[:, :], 0.0))
            chain.link(nc.vector.memset(psum_[:, :], 1.0))
            dve.wait_ge(gb_ready, 1)
            chain.link(nc.vector.tensor_copy(gbh, gb1))
            nc.vector.tensor_tensor(gbl, gb1, gbh, ALU.subtract).then_inc(gb_split, 1)
            norm(IT, 0, 0)
            norm(IT + 1, 1, 1)
            rope(0)
            copy_v(0, 0)

            def batch(b, slot):
                maxima(b)
                if not (isinstance(b, int) and b >= BATCH - 2):
                    norm(b + (IT + 2), b + 2, slot)
                normalise_p(b)
                if not known(b, BATCH - 1):
                    rope(b + 1)
                    copy_v(b + 1, 1 - slot)
                if not known(b, 0):
                    add_text(b - 1)
            body = batch
            body(0, 0)
            body(1, 1)
            with dve.Fori(1, BATCH // 2 - 1) as j:
                chain.begin(j - 1, 6)
                body(2 * j, 0)
                body(2 * j + 1, 1)
                chain.end(BATCH // 2 - 2)
            body(BATCH - 2, 0)
            body(BATCH - 1, 1)
            add_text(BATCH - 1)
            for n in range(IT):
                r = tile_rows(BATCH + n)
                dve.wait_ge(pr_psum, BATCH + n + 1)
                hb = h[0:r, BATCH + n, :]
                nc.vector.tensor_tensor(hb, PS[0:r, 6 - n, 0:D], hb, ALU.add).then_inc(h3_added, 1)
                dve.wait_ge(h3_added, BATCH + n + 1)
                nc.vector.bn_stats(stats[:, BATCH + n, 0, :], h[:, BATCH + n, :]).then_inc(stats_ready, 1)

        def sp_experts1(sp):
            sp.wait_ge(h3_added, NT)
            sp.dma_start(b1b, b1rows.broadcast_to([P, E1 * F1])).then_inc(experts1_loaded, 16)
            store_rows(sp, xs1, pay1, 2)
            for k in range(2):
                sp.wait_ge(y_out[k], 16 * ((SLOT0 + 1 - k) // 2 + (SLOT1 + 1 - k) // 2))
            for k in OUT_LOADS:
                t, n, r = RUNS[k]
                take_back(sp, Layer1, 0, back0, t, n, r, taken_back[k])
                take_back(sp, Layer1, 1, back1, t, n, r, taken_back[k])

        def act_experts1(act, roots):
            roots(6)
            act_dispatch(act, (3, 1), x2G, 1)
            act.wait_ge(logits_ready, 3)
            nc.scalar.activation(rb[:, 0, :], rb[:, 1, :], ACT.Exp).then_inc(sig_ready, 1)
            act.wait_ge(c_psum, 2)
            for i, bank in enumerate(C_BANKS):
                nc.scalar.activation(rest1[:, 2 * i:2 * i + 2, :], PS[:, bank, :].rearrange("p (e n) -> p e n", e=2),
                                     ACT.Copy).then_inc(c_copied, 1)
            act.wait_ge(scale_ready, 2)
            ffn_act(act, Layer1)

        def pe_experts1(pe):
            pe.wait_ge(small1_loaded, 32)

            def biases_out(first):
                for e in (first, first + 1):
                    n = 0
                    for c in range(F1 // P):
                        off = e * W1N + KC * F1 + c * D
                        for g_, w_ in ((gbh, w1h), (gbh, w1l), (gbl, w1h)):
                            left = g_[:, c * E1 + e:c * E1 + e + 1].broadcast_to([P, P])
                            ins = nc.tensor.matmul(PS[:, C_BANKS[first // 2], (e % 2) * D:(e % 2 + 1) * D], left,
                                                   w_[:, off:off + D], start=(n == 0), stop=(n == 3 * (F1 // P) - 1))
                            n += 1
                ins.then_inc(c_psum, 1)
            pe.wait_ge(stage_free, AHEAD + XW // CW + W1W // CW)
            pe.wait_ge(gb_split, 1)
            biases_out(0)
            pe_route(pe, (3, 1), x2G, pay1, wr1, 4, 1)
            pe_scale(pe, 1)
            biases_out(2)
            pe_count(pe, 1)
            pe_slots(pe, 1, TOPK * NT, SLOT1, inrow1, intile1)
            pe.wait_ge(slots_ready, 2)
            pe.wait_ge(dest_ready, 2)
            ffn_pe(pe, Layer1)

        def pool_experts1(pool):
            chain = Chain(pool, rest_ready)
            pool.wait_ge(c_copied, 2)
            chain.link(nc.gpsimd.tensor_tensor(rest1, rest1, b2all, ALU.add))
            chain.link(nc.gpsimd.tensor_tensor(csum, rest1[:, 0, :], rest1[:, 1, :], ALU.add))
            for e in (2, 3):
                chain.link(nc.gpsimd.tensor_tensor(csum, csum, rest1[:, e, :], ALU.add))
            chain.link(nc.gpsimd.tensor_tensor(rest1, b2all, rest1, ALU.subtract))
            chain.link(nc.gpsimd.tensor_tensor(rest1, rest1, csum.unsqueeze(1).broadcast_to([P, E1, D]), ALU.add))
            ffn_pool(pool, Layer1)
            add_both(pool, nc.gpsimd, OUT_POOL, added_pool, len(BACK_POOL))

        def dve_experts1(dve, chain, inverse_roots):
            moments_of_all(dve, chain, 3)
            inverse_roots()
            dve_norm(dve, pay1)
            def add_bias(a_):
                chain.link(nc.vector.tensor_reduce(amax[:, 3:4], c_b1c, AX, ALU.max, apply_absolute_value=True))
                chain.link(nc.vector.scalar_tensor_tensor(out=a_, in0=a_, scalar=float(D), in1=amax[:, 3:4],
                                                          op0=ALU.mult, op1=ALU.add))
            dve.wait_ge(stage_free, AHEAD + XW // CW + W1W // CW)
            dve_bound(dve, chain, w1h.rearrange("p (e n) -> p e n", e=E1)[:, :, 0:KC * F1], add_bias)
            dve_scale(dve, chain, 1)
            dve.wait_ge(route_psum, 2 * NT)
            lg, l2 = ra[:, 0:4, :], ra[:, 4:8, :]
            nc.vector.tensor_tensor(lg, PS[:, 6, 0:4 * NT].rearrange("p (t g) -> p g t", g=4),
                                    c_br.unsqueeze(2).broadcast_to([P, 4, NT]), ALU.add).then_inc(logits_ready, 1)
            dve.wait_ge(logits_ready, 2)
            v1, v2 = ra[:, 8, :], ra[:, 9, :]
            first_max(chain, lg, v1, oh[:, 0])
            chain.link(nc.vector.scalar_tensor_tensor(out=l2, in0=oh[:, 0], scalar=-1e30, in1=lg, op0=ALU.mult, op1=ALU.add))
            first_max(chain, l2, v2, oh[:, 1])
            nc.vector.tensor_tensor(rb[:, 1, :], v2, v1, ALU.subtract).then_inc(logits_ready, 1)
            dve.wait_ge(sig_ready, 2)
            ga, gb_ = gates[:, 0, :], gates[:, 1, :]
            chain.link(nc.vector.tensor_scalar(ra[:, 10, :], rb[:, 0, :], 1.0, None, ALU.add))
            chain.link(nc.vector.reciprocal(ga, ra[:, 10, :]))
            chain.link(nc.vector.tensor_tensor(gb_, ga, rb[:, 0, :], ALU.mult))
            chain.link(nc.vector.tensor_tensor(rb[:, 4:8, :], oh[:, 0], over(ga, 4), ALU.mult))
            chain.link(nc.vector.tensor_tensor(rb[:, 8:12, :], oh[:, 1], over(gb_, 4), ALU.mult))
            chain.link(nc.vector.tensor_tensor(rb[:, 4:8, :], rb[:, 4:8, :], rb[:, 8:12, :], ALU.add))
            chain.link(nc.vector.tensor_copy(pay1[:, :, D:PAY1], rb[:, 4:8, :].rearrange("p g t -> p t g")))
            dve.sem_inc(pay_ready, 1)
            positions(dve, chain, TOPK, SLOT1, 1, inrow1, intile1)
            dve.wait_ge(rest_ready, 6)
            ffn_dve(dve, Layer1)
            add_both(dve, nc.vector, OUT_DVE, added_back, len(BACK_DVE))

        def add_both(eng, engine, runs, done, before):
            for i, k in enumerate(runs):
                t, n, r = RUNS[k]
                eng.wait_ge(taken_back[k], 16 * 3)
                for c, part in enumerate((back0, back1)):
                    engine.tensor_tensor(h[0:r, t:t + n, :], h[0:r, t:t + n, :], part[0:r, t:t + n, :], ALU.add)\
                        .then_inc(done, 1)
                    eng.wait_ge(done, before + 2 * i + c + 1)

        @block.sync
        def _(sp):
            sp.dma_start(pt[0:IPAD, :, :], patches.rearrange("j r f -> r j f")).then_inc(patches_loaded, 16)
            sp.dma_start(wt, wtok).then_inc(small_loaded, 16)
            sp.dma_start(ccols[:, 0:20], cols).then_inc(small_loaded, 16)
            sp.dma_start(rows.rearrange("p a n -> p (a n)"), rows_a.broadcast_to([P, 6 * D])).then_inc(small_loaded, 16)
            sp.dma_start(cst[:, :], consts).then_inc(small_loaded, 16)
            sp.dma_start(petab[0:IPAD, :], pe_table).then_inc(small_loaded, 16)
            sp.dma_start(wsm[:, :], wsmall).then_inc(small_loaded, 16)
            sp.dma_start(h[:, 0:BATCH, :], txt.rearrange("b s d -> s b d")).then_inc(text_loaded, 16)
            with sp.Fori(0, XW // CW // 2) as n:
                for k in range(2):
                    sp.wait_ge(stage_free, 2 * n + (k + 1))
                    sp.dma_start(stage[:, k, :], w0[:, bass.ds((2 * n + k) * CW, CW)]).then_inc(stage_full[k], 16)
            if stop <= 2:
                dump(sp)
                return
            sp_rest(sp)
            dump(sp)

        def split_chunks(pool, hi, lo, words, first):
            for n in range(first, first + words // CW):
                cols_ = slice((n - first) * CW, (n - first + 1) * CW)
                if IT <= n < IT + ALONE:
                    pool.wait_ge(stage_full[n % 2], 16 * (n // 2 + 1))
                    nc.gpsimd.tensor_copy(hi[:, cols_], stage[:, n % 2, :]).then_inc(own_high, 1)
                    pool.wait_ge(own_high, n - IT + 1)
                else:
                    pool.wait_ge(w_high, n + 1 if n < IT else n + 1 - ALONE)
                nc.gpsimd.tensor_tensor(lo[:, cols_], stage[:, n % 2, :], hi[:, cols_], ALU.subtract)\
                    .then_inc(stage_free, 1)

        @block.gpsimd
        def _(pool):
            nc.gpsimd.memset(onesb[:, :], 1.0).then_inc(consts_ready, 1)
            nc.gpsimd.memset(onesf[:, :], 1.0).then_inc(consts_ready, 1)
            nc.gpsimd.memset(xT[:, :, BATCH * SEQ:], 0.0).then_inc(pads_zeroed, 1)
            pool.wait_ge(pads_zeroed, 1)
            nc.gpsimd.memset(h[96:P, BATCH:NT, :], 0.0).then_inc(pads_zeroed, 1)
            pool.wait_ge(pads_zeroed, 2)
            pool.sem_inc(stage_free, 2)
            split_chunks(pool, w0h, w0l, XW, 0)
            if stop > 2:
                pool_rest(pool)

        @block.scalar
        def _(act):
            chain = Chain(act, act_done)
            pair_of = [0]

            def roots(n):
                act.wait_ge(var_ready, n)
                nc.scalar.activation(std, var, ACT.Sqrt).then_inc(std_ready, 1)

            def high_half(high, n, k, j):
                act.wait_ge(stage_full[k], 16 * (j + 1))
                nc.scalar.activation(high[:, bass.ds(n * CW, CW)], stage[:, k, :], ACT.Copy).then_inc(w_high, 1)

            act.wait_ge(small_loaded, 16 * NSMALL)
            chain.link(nc.scalar.activation(c_nega, c_alog, ACT.Exp))
            nc.scalar.mul(c_nega, c_nega, -1.0).then_inc(nega_ready, 1)
            roots(1)
            for j in range(IT):
                for half in range(2):
                    act.wait_ge(patch_tr, 2 * j + half + 1)
                    if j >= 2:
                        act.wait_ge(tok_psum, j - 1)
                    bank = PS[:, 1 + 2 * (j % 2) + half, 0:3 * IPAD].rearrange("p (c r) -> p c r", c=3)
                    nc.scalar.activation(pT[:, j % 2, 3 * half:3 * half + 3, :], bank, ACT.Copy)\
                        .then_inc(patch_copied, 1)
                high_half(w0h, j, j % 2, j // 2)
            roots(2)
            act.sem_inc(xT_copied, AHEAD)
            roots(3)

            def copy_xT(t, rows, slot):
                act.wait_ge(xn_tr, t + 1 + AHEAD)
                src = PS[:, slot, 0:KC * P].rearrange("p (k r) -> p k r", k=KC)[:, :, 0:rows]
                if rows != P:
                    src = src.rearrange("p k (b s) -> p k b s", s=IMG)
                nc.scalar.activation(batch_cols(xT, t, rows), src, ACT.Copy).then_inc(xT_copied, 1)

            act.wait_ge(pads_zeroed, 2)
            token_tiles(act, copy_xT)
            for n in range(9):
                g, c = n // 3, (n % 3) * 2 * SEQ
                act.wait_ge(bcd_psum, n + 1)
                nc.scalar.activation(sD[32 * g:32 * g + 32, c:c + 2 * SEQ], PS[64:96, n % 2 + 2, 0:2 * SEQ],
                                     ACT.Identity, bias=c_bcd[64:96, :]).then_inc(dl_copied, 1)
            act.wait_ge(dl_copied, 9)
            chain.link(nc.scalar.activation(sA[0:96, :], sD[0:96, :], ACT.Abs))
            chain.link(nc.scalar.activation(sA[0:96, :], sA[0:96, :], ACT.Exp, scale=-1.0))
            nc.scalar.activation(sA[0:96, :], sA[0:96, :], ACT.Ln, bias=1.0).then_inc(sp_ready, 1)
            act.wait_ge(delta_ready, 1)
            nc.scalar.activation(sA[0:96, :], sD[0:96, :], ACT.Exp, scale=c_nega).then_inc(decay_ready, 1)

            def gelu_z(t, rows, slot):
                for m in range(KC):
                    act.wait_ge(z_psum, t + 1)
                    ins = nc.scalar.activation(gT[:, slot, m, 0:rows], PS[:, 2 + slot, m * P:m * P + rows], ACT.Gelu,
                                               bias=c_bz[:, m:m + 1])
                ins.then_inc(g_ready, 1)

            first = IT + ALONE
            with act.Fori(0, LATE // 2) as i:
                for k in range(2):
                    gelu_z(2 * i + k, P, k)
                    high_half(w0h, 2 * i + (k + first), k, i + first // 2)
            with act.Fori(LATE // 2, BATCH // 2) as i:
                for k in range(2):
                    gelu_z(2 * i + k, P, k)
            for t in range(BATCH, NT):
                gelu_z(t, tile_rows(t), t % 2)
            if stop <= 2:
                return
            act_rest(act, roots)

        @block.tensor
        def _(pe):
            pe.wait_ge(small_loaded, 16 * NSMALL)
            for c in range(PC):
                ins = nc.tensor.matmul(PS[:, 0, 0:D], c_b1[:, c:c + 1].broadcast_to([P, P]), wt[:, c, :],
                                       start=(c == 0), stop=(c == PC - 1))
            ins.then_inc(tokb_psum, 1)

            def tok_matmul(j):
                pe.wait_ge(patch_copied, 2 * j + 2)
                if j == 0:
                    pe.wait_ge(wt_scaled, 1)
                if j >= 2:
                    pe.wait_ge(tok_added, j - 1)
                for c in range(PC):
                    ins = nc.tensor.matmul(PS[0:IPAD, 5 + j % 2, 0:D], pT[:, j % 2, c, :], wt[:, c, :],
                                           start=(c == 0), stop=(c == PC - 1))
                ins.then_inc(tok_psum, 1)

            for j in range(IT):
                pe.wait_ge(patch_normed, j + 1)
                if j >= 2:
                    pe.wait_ge(patch_copied, 2 * j - 2)
                for half in range(2):
                    for c in range(3):
                        ins = nc.tensor.transpose(PS[:, 1 + 2 * (j % 2) + half, c * IPAD:(c + 1) * IPAD],
                                                  pt[0:IPAD, j, (3 * half + c) * P:(3 * half + c + 1) * P],
                                                  k_ident[0:IPAD, 0:IPAD])
                    ins.then_inc(patch_tr, 1)
                if j >= 1:
                    tok_matmul(j - 1)
            tok_matmul(IT - 1)

            pe.sem_inc(xn_tr, AHEAD)

            def tr(t, rows, slot):
                pe.wait_ge(xn_ready, t + 1)
                pe.wait_ge(xT_copied, t + 1)
                for k in range(KC):
                    ins = nc.tensor.transpose(PS[:, slot, k * P:(k + 1) * P], xn[:, slot, k * P:(k + 1) * P], k_ident)
                ins.then_inc(xn_tr, 1)
            token_tiles(pe, tr)
            for n in range(PB // 2):
                if n == 0:
                    pe.wait_ge(xT_copied, NT + AHEAD)
                if n >= 2:
                    pe.wait_ge(bc_copied, n - 1)
                    pe.wait_ge(dl_copied, n - 1)
                for k in range(KC):
                    ins = nc.tensor.matmul(PS[0:96, 2 + n % 2, 0:2 * SEQ], wbcd[:, k, :],
                                           xT[:, k, 2 * n * SEQ:2 * (n + 1) * SEQ], start=(k == 0), stop=(k == KC - 1))
                ins.then_inc(bcd_psum, 1)

            def scan_sum():
                pe.wait_ge(sc_ready, 2)
                for t in range(NT):
                    b0 = t if t < BATCH else (t - BATCH) * PER
                    g, b = b0 // SB, b0 % SB
                    nb = min(PER, BATCH - b0)
                    rows_ = P if t < BATCH else nb * IMG
                    c = SB * IMG + b * TEXT if t < BATCH else b * IMG
                    part = sA[32 * g:32 * g + 32, c:c + rows_]
                    ins = nc.tensor.matmul(PS[0:rows_, Y_BANKS[g], t:t + 1], part, onesf[32 * g:32 * g + 32, 0:1],
                                           start=True, stop=True)
                ins.then_inc(y_psum, 1)

            def z_matmul(t, rows, slot):
                for m in range(KC):
                    out_ = PS[:, 2 + slot, m * P:m * P + rows]
                    if rows != P:
                        out_ = out_.rearrange("p (b s) -> p b s", s=IMG)
                    for k in range(KC):
                        rhs = batch_cols(xT, t, rows)[:, k]
                        ins = nc.tensor.matmul(out_, wz[:, k, m * P:(m + 1) * P], rhs, start=(k == 0),
                                               stop=(k == KC - 1))
                ins.then_inc(z_psum, 1)

            def o_matmul(t, rows, slot):
                pe.wait_ge(g_ready, t + 1)
                pe.wait_ge(h_added, t + 1)
                for k in range(KC):
                    ins = nc.tensor.matmul(PS[0:rows, 4 + slot, 0:D], gT[:, slot, k, 0:rows], wout[:, k, :],
                                           start=(k == 0), stop=(k == KC - 1))
                ins.then_inc(o_psum, 1)

            pe.wait_ge(bc_copied, 9)
            pe.wait_ge(dl_copied, 9)
            z_matmul(0, P, 0)
            z_matmul(1, P, 1)
            scan_sum()
            o_matmul(0, P, 0)
            with pe.Fori(1, BATCH // 2) as i:
                z_matmul(2 * i, P, 0)
                o_matmul(2 * i - 1, P, 1)
                z_matmul(2 * i + 1, P, 1)
                o_matmul(2 * i, P, 0)
            for t in range(BATCH, NT):
                z_matmul(t, tile_rows(t), t % 2)
                o_matmul(t - 1, tile_rows(t - 1), (t - 1) % 2)
            o_matmul(NT - 1, tile_rows(NT - 1), (NT - 1) % 2)
            if stop <= 2:
                return
            pe_rest(pe)

        @block.vector
        def _(dve):
            chain = Chain(dve, dve_done)
            ln_count = [0]

            def moments(t, count=1):
                chain.link(nc.vector.bn_stats(stats[:, bass.ds(t, 1), 0, :], h[:, bass.ds(t, 1), :]))
                chain.link(nc.vector.bn_aggr(mv[:, bass.ds(t, 1), :], stats[:, bass.ds(t, 1), 0, :]))

            def inverse_roots():
                nc.vector.tensor_scalar(var, mv[:, :, 1], EPS, None, ALU.add).then_inc(var_ready, 1)
                ln_count[0] += 1
                dve.wait_ge(std_ready, ln_count[0])
                chain.link(nc.vector.reciprocal(rstd, std))
                chain.link(nc.vector.tensor_tensor(newt, rstd, rstd, ALU.mult))
                chain.link(nc.vector.tensor_tensor(newt, newt, var, ALU.mult))
                chain.link(nc.vector.tensor_scalar(newt, newt, -0.5, 1.5, ALU.mult, ALU.add))
                chain.link(nc.vector.tensor_tensor(rstd, rstd, newt, ALU.mult))

            chain.link(nc.vector.memset(mv[:, :, :], 0.0))
            dve.wait_ge(patches_loaded, 16)
            for j in range(IT):
                for half in range(2):
                    ins = nc.vector.bn_stats(stats[0:IPAD, BATCH + j, half, :], pt[0:IPAD, j, half * 384:(half + 1) * 384])
            chain.link(ins)
            for j in range(IT):
                ins = nc.vector.bn_aggr(mv[0:IPAD, j, :], stats[0:IPAD, BATCH + j, :, :].rearrange("p a b -> p (a b)"))
            chain.link(ins)
            inverse_roots()
            for j in range(IT):
                nc.vector.tensor_scalar(pt[0:IPAD, j, :], pt[0:IPAD, j, :], mv[0:IPAD, j, 0:1], rstd[0:IPAD, j:j + 1],
                                        ALU.subtract, ALU.mult).then_inc(patch_normed, 1)
            dve.wait_ge(tokb_psum, 1)
            chain.link(nc.vector.tensor_tensor(r_tb, PS[:, 0, 0:D], r_tb, ALU.add))
            for c in range(PC):
                ins = nc.vector.tensor_scalar(wt[:, c, :], wt[:, c, :], c_g1[:, c:c + 1], None, ALU.mult)
            ins.then_inc(wt_scaled, 1)
            chain.link(nc.vector.tensor_tensor(r_cls, r_cls, r_cpos, ALU.add))
            for row_, at_rows in ((r_b2, k_patch), (r_cls, k_class)):
                chain.link(nc.vector.scalar_tensor_tensor(out=petab[0:IPAD, :], in0=row_[0:IPAD, :], scalar=at_rows[0:IPAD, :],
                                                          in1=petab[0:IPAD, :], op0=ALU.mult, op1=ALU.add))
            dve.wait_ge(text_loaded, 16)
            for t in range(BATCH):
                ins = nc.vector.bn_stats(stats[:, t, 0, :], h[:, t, :])
            chain.link(ins)
            dve.wait_ge(pads_zeroed, 2)
            for j in range(IT):
                dve.wait_ge(tok_psum, j + 1)
                ins = nc.vector.tensor_tensor(h[0:IPAD, BATCH + j, :], PS[0:IPAD, 5 + j % 2, 0:D], r_tb[0:IPAD, :],
                                              ALU.add)
                ins.then_inc(tok_added, 1)
            dve.wait_ge(tok_added, IT)
            for j in range(IT):
                ins = nc.vector.bn_stats(stats[0:IPAD, BATCH + j, 0, :], h[0:IPAD, BATCH + j, :])
            chain.link(ins)
            for j in range(IT):
                ins = nc.vector.bn_aggr(mv[0:IPAD, j, :], stats[0:IPAD, BATCH + j, 0, :])
            chain.link(ins)
            inverse_roots()
            chain.link(nc.vector.tensor_scalar(rstd, rstd, k_patch, None, ALU.mult))
            for j in range(IT):
                ins = nc.vector.tensor_scalar(h[0:IPAD, BATCH + j, :], h[0:IPAD, BATCH + j, :], mv[0:IPAD, j, 0:1],
                                              rstd[0:IPAD, j:j + 1], ALU.subtract, ALU.mult)
            chain.link(ins)
            image = h[0:IPAD, BATCH:NT, :]
            chain.link(nc.vector.tensor_tensor(image, image, r_g2[0:IPAD, :].unsqueeze(1).broadcast_to([IPAD, IT, D]),
                                               ALU.mult))
            nc.vector.tensor_tensor(image, image, petab[0:IPAD, :].unsqueeze(1).broadcast_to([IPAD, IT, D]),
                                    ALU.add).then_inc(tok_ready, 1)

            dve.wait_ge(tok_ready, 1)
            for t in range(BATCH, NT):
                ins = nc.vector.bn_stats(stats[:, t, 0, :], h[:, t, :])
            chain.link(ins)
            for t in range(NT):
                ins = nc.vector.bn_aggr(mv[:, t, :], stats[:, t, 0, :])
            chain.link(ins)
            inverse_roots()

            def norm(t, rows, slot):
                dve.wait_ge(xn_tr, t + 1)
                nc.vector.tensor_scalar(xn[:, slot, :], h[:, bass.ds(t, 1), :], mv[:, bass.ds(t, 1), 0],
                                        rstd[:, bass.ds(t, 1)], ALU.subtract, ALU.mult).then_inc(xn_ready, 1)
            token_tiles(dve, norm)
            for n in range(9):
                g, c = n // 3, (n % 3) * 2 * SEQ
                dve.wait_ge(bcd_psum, n + 1)
                nc.vector.tensor_scalar(sB[32 * g:32 * g + 32, c:c + 2 * SEQ], PS[0:32, n % 2 + 2, 0:2 * SEQ],
                                        c_bcd[0:32, :], None, ALU.add)
                nc.vector.tensor_scalar(sC[32 * g:32 * g + 32, c:c + 2 * SEQ], PS[32:64, n % 2 + 2, 0:2 * SEQ],
                                        c_bcd[32:64, :], None, ALU.add).then_inc(bc_copied, 1)
            dve.wait_ge(bc_copied, 9)
            dve.wait_ge(sp_ready, 1)
            nc.vector.scalar_tensor_tensor(out=sD[0:96, :], in0=sD[0:96, :], scalar=0.0, in1=sA[0:96, :],
                                           op0=ALU.max, op1=ALU.add).then_inc(delta_ready, 1)
            dve.wait_ge(decay_ready, 1)
            chain.link(nc.vector.memset(sA[0:96, :].rearrange("p (b s) -> p b s", s=SEQ)[:, :, 0:1], 0.0))
            chain.link(nc.vector.tensor_tensor_scan(sS[0:96, :], sA[0:96, :], sB[0:96, :], 0.0, ALU.mult, ALU.add))
            for lo, hi, at_ in ((0, IMG, 0), (IMG, SEQ, SB * IMG)):
                state, cc = (v[0:96, :].rearrange("p (b s) -> p b s", s=SEQ)[:, :, lo:hi] for v in (sS, sC))
                nc.vector.tensor_tensor(sA[0:96, at_:at_ + SB * (hi - lo)].rearrange("p (b s) -> p b s", b=SB),
                                        state, cc, ALU.mult).then_inc(sc_ready, 1)
            dve.wait_ge(y_psum, 1)
            chain.link(nc.vector.memset(yv[:, :], 0.0))
            for t in range(NT):
                g = (t if t < BATCH else (t - BATCH) * PER) // SB
                rows_ = P if t < BATCH else IROWS if t < NT - 1 else LAST * IMG
                ins = nc.vector.tensor_copy(yv[0:rows_, t:t + 1], PS[0:rows_, Y_BANKS[g], t:t + 1])
            chain.link(ins)
            dve.sem_inc(h_added, AHEAD)

            def add_scan(t, rows, slot):
                ht = h[0:rows, bass.ds(t, 1), :]
                dve.wait_ge(o_psum, t + 1)
                nc.vector.scalar_tensor_tensor(out=ht, in0=PS[0:rows, 4 + slot, 0:D].unsqueeze(1),
                                               scalar=yv[0:rows, bass.ds(t, 1)], in1=ht, op0=ALU.mult, op1=ALU.add)\
                    .then_inc(h_added, 1)
                dve.wait_ge(h_added, t + 1 + AHEAD)
                nc.vector.tensor_tensor(ht, ht, r_bout[0:rows, :].unsqueeze(1), ALU.add).then_inc(hb_added, 1)
                dve.wait_ge(hb_added, t + 1)
                nc.vector.bn_stats(stats[:, bass.ds(t, 1), 0, :], h[:, bass.ds(t, 1), :]).then_inc(stats_ready, 1)
            token_tiles(dve, add_scan)
            if stop <= 2:
                return
            dve_rest(dve, chain, inverse_roots)


def position_table():
    omega = np.arange(D // 4, dtype=np.float32) / np.float32(D // 4 - 1)
    omega = (np.float32(1.0) / np.float32(10000.0) ** omega).astype(np.float32)
    y, x = np.meshgrid(np.arange(GRID), np.arange(GRID), indexing="ij")
    y = y.reshape(-1)[:, None].astype(np.float32) * omega[None, :]
    x = x.reshape(-1)[:, None].astype(np.float32) * omega[None, :]
    pe = np.concatenate((np.sin(x), np.cos(x), np.sin(y), np.cos(y)), axis=1).astype(np.float32)
    table = np.zeros((IPAD, D), np.float32)
    for b in range(PER):
        table[b * IMG + 1:(b + 1) * IMG] = pe
    return table


def shape_constants():
    c = np.zeros((P, NCST), np.float32)
    c[:, 0:P] = np.eye(P)
    c[:, P:2 * P] = np.triu(np.ones((P, P)), 1)
    at = 2 * P
    valid = np.ones((P, NT))
    valid[IROWS:, BATCH:] = 0
    valid[LAST * IMG:, NT - 1] = 0
    c[:, at:at + NT] = valid; at += NT
    reset = np.ones((4, NT)); reset[:, 0] = 0
    c[:, at:at + 4 * NT] = reset.reshape(-1); at += 4 * NT
    c[:, at:at + 4 * NFULL] = np.tile(np.arange(NFULL) * P, 4); at += 4 * NFULL
    c[:, at:at + SLOT1] = np.arange(SLOT1); at += SLOT1
    c[:, at:at + NT] = (1 - valid) * 2.0 ** 20; at += NT
    c[:, at:at + TOPK * NT] = np.arange(TOPK * NT); at += TOPK * NT
    c[:, at:at + P] = np.arange(P); at += P
    c[:, at] = np.arange(P)
    c[:IROWS, at + 1] = np.arange(IROWS) % IMG != 0
    c[:IROWS, at + 2] = np.arange(IROWS) % IMG == 0
    return c


def chunks(w, parts):
    return w.reshape(parts, P, -1).transpose(1, 0, 2)


def rope_tables():
    freqs = (np.float32(1.0) / np.float32(10000.0) ** (np.arange(0, D, 2, dtype=np.float32) / np.float32(D)))
    ang = freqs.astype(np.float32)[:, None] * np.arange(SEQ, dtype=np.float32)[None, :]
    cos, sin = np.cos(ang).astype(np.float32), np.sin(ang).astype(np.float32)
    query, key = np.arange(P)[:, None], np.arange(SEQ)[None, :]
    mask_a = np.where(key[:, :P] <= query, 0.0, -1e30)
    mask_b = np.where(key <= query + P, 0.0, -1e30)
    return np.concatenate([cos, sin, -sin, mask_a, mask_b], 1).astype(np.float32)


def lay_out(i):
    f = {k: np.asarray(v) for k, v in i.items()}
    x = f["x"].reshape(BATCH, CH, GRID, PATCH, GRID, PATCH).transpose(0, 2, 4, 3, 5, 1).reshape(BATCH, IMG - 1, PDIM)
    pt = np.zeros((PB, IMG, PDIM), np.float32)
    pt[:BATCH, 1:] = x
    patches = np.zeros((IT, IPAD, PDIM), np.float32)
    patches[:, :IROWS] = pt.reshape(IT, IROWS, PDIM)
    w_in, b_in = f["L0_attn_W_in"], f["L0_attn_b_in"]
    cols = np.zeros((P, 20), np.float32)
    cols[:, 0:6] = f["L0_tok_ln1_g"].reshape(PC, P).T
    cols[:, 6:12] = f["L0_tok_ln1_b"].reshape(PC, P).T
    cols[:, 12:14] = b_in[D:2 * D].reshape(KC, P).T
    cols[:, 14:16] = f["L1_attn_bq"].reshape(P, 2)
    cols[:, 16:18] = f["L1_attn_bk"].reshape(P, 2)
    wbcd = np.zeros((D, 96), np.float32)
    for n in range(3):
        wbcd[:, 32 * n:32 * n + NS] = w_in[:, 2 * D + n * NS:2 * D + (n + 1) * NS]
        cols[32 * n:32 * n + NS, 18] = b_in[2 * D + n * NS:2 * D + (n + 1) * NS]
        cols[32 * n:32 * n + NS, 19] = f["L0_attn_A_log"]
    route = np.concatenate([f["L0_ffn_macro_w"], f["L0_ffn_micro_w"].transpose(1, 0, 2).reshape(D, G0 * E0)], 1)
    small = np.concatenate([chunks(w, KC).reshape(P, -1) for w in (wbcd, w_in[:, D:2 * D], f["L0_attn_W_out"], route)], 1)
    w0 = np.concatenate([np.concatenate([chunks(f["L0_ffn_gate_w"][e], KC).reshape(P, -1),
                                         chunks(f["L0_ffn_up_w"][e], KC).reshape(P, -1),
                                         chunks(f["L0_ffn_down_w"][e], F0 // P).reshape(P, -1)], 1)
                         for e in range(G0 * E0)], 1)
    halves = lambda w: np.concatenate([w.T[:, 0::2], w.T[:, 1::2]], 1)
    wattn = np.concatenate([chunks(w, KC).reshape(P, -1) for w in (
        halves(f["L1_attn_Wq"]), halves(f["L1_attn_Wk"]), f["L1_attn_Wv"].T, f["L1_attn_Wf"].T)] + [rope_tables()], 1)
    w1 = np.concatenate([np.concatenate(
        [chunks(f["L1_ffn_w1"][e][:, s * F0:(s + 1) * F0], KC).reshape(P, -1) for s in range(HF)]
        + [chunks(f["L1_ffn_w2"][e], F1 // P).reshape(P, -1)], 1) for e in range(E1)], 1)
    small1 = np.zeros((P, NSM1), np.float32)
    at = 4 * KC
    small1[:, 0:at] = chunks(f["L1_ffn_wr"], KC).reshape(P, -1)
    small1[:, at:at + (F1 // P) * E1] = f["L1_ffn_b1"].reshape(E1, F1 // P, P).transpose(2, 1, 0).reshape(P, -1)
    at += (F1 // P) * E1
    small1[:, at:at + E1] = f["L1_ffn_br"]
    return {
        "wattn": wattn, "rows_f": np.concatenate([f["L1_attn_bv"], f["L1_attn_bf"]])[None], "w1": w1,
        "wsmall1": small1, "b1rows": f["L1_ffn_b1"].reshape(1, -1), "b2rows": f["L1_ffn_b2"].reshape(1, -1),
        "txt": f["txt"], "patches": patches, "wtok": chunks(f["L0_tok_W"], PC), "cols": cols,
        "rows_a": np.concatenate([f[k].reshape(-1) for k in (
            "L0_tok_ln2_g", "L0_tok_ln2_b", "L0_tok_bias", "L0_tok_cls_token", "L0_tok_cls_pos_embedding",
            "L0_attn_b_out")])[None],
        "consts": shape_constants(), "pe_table": position_table(), "wsmall": small, "w0": w0,
    }


def kernel(**inputs):
    import concourse.bacc as _bacc
    from concourse.bass_utils import run_bass_kernel_spmd as _run

    nc = _bacc.Bacc("TRN2", target_bir_lowering=False, num_devices=1)
    arrays, args = {}, {}
    for name, a in lay_out(inputs).items():
        a = np.ascontiguousarray(a)
        arrays[f"in_{name}_dram"] = a
        args[name] = nc.dram_tensor(f"in_{name}_dram", a.shape, mybir.dt.from_np(a.dtype), kind="ExternalInput").ap()
    out = nc.dram_tensor("out_0_dram", (BATCH, SEQ, D), F32, kind="ExternalOutput").ap()
    build(nc, out=out, stop=STOP, **args)
    r = _run(nc, [arrays], core_ids=[0])
    return r.results[0]["out_0_dram"]
```

```python
from contextlib import ExitStack

import numpy as np

import concourse.bass as bass
from concourse import mybir

F32 = mybir.dt.float32
BF16 = mybir.dt.bfloat16
F16 = mybir.dt.float16
I32 = mybir.dt.int32
U32 = mybir.dt.uint32
ALU = mybir.AluOpType
ACT = mybir.ActivationFunctionType
AX = mybir.AxisListType.X
AXS = [mybir.AxisListType.X, mybir.AxisListType.XY]

P = 128
BATCH, TEXT, D = 16, 128, 256
GRID, PATCH, CH = 6, 16, 3
IMG = GRID * GRID + 1
SEQ = IMG + TEXT
PDIM = PATCH * PATCH * CH
PC = PDIM // P
KC = D // P
PER = 3
IT = -(-BATCH // PER)
IROWS = PER * IMG
IPAD = 112
LAST = BATCH - PER * (IT - 1)
NT = BATCH + IT
PB = IT * PER
NS = 16
SG = 3
SB = PB // SG
EPS = 1e-5
G0, E0, F0 = 4, 2, 512
SLOT0 = (BATCH * SEQ + G0 * (P - 1)) // P
W0N = 2 * KC * F0 + (F0 // P) * D
E1, F1, TOPK = 4, 1024, 2
T1 = 2 * P
PAIRS1 = (TOPK * BATCH * SEQ + E1 * (T1 - 1)) // T1
SLOT1 = 2 * PAIRS1
HF = F1 // F0
W1N = KC * F1 + (F1 // P) * D
W1W = E1 * W1N
PAY0 = D + E0
PAY1 = D + E1
TOKENS = NT * P
DUMP = 2 * TOKENS
RUNS = [(0, 6, P), (6, 6, P), (12, 4, P), (BATCH, IT - 1, IROWS), (NT - 1, 1, LAST * IMG)]
BACK_DVE, BACK_POOL = (0, 2), (1, 3, 4)
OUT_DVE, OUT_POOL = (0, 1, 2), (3, 4)
OUT_LOADS, OUT_STORES = (0, 3, 4, 1, 2), (0, 1, 3, 4, 2)
CW = 1024
NFULL = -(-BATCH * SEQ // P)
NCST = 3 * P + NT + 4 * NT + 4 * NFULL + SLOT1 + NT + TOPK * NT + 3
NCOL = 22
NWS = KC * (96 + D + D + 12)
XW0 = G0 * E0 * W0N
SCALE = float(D) ** -0.5
NATT = 4 * KC * D + 3 * SEQ + P + SEQ
NSM1 = 4 * KC + (F1 // P) * E1 + E1
ALONE = 12
LATE = XW0 // CW - IT - ALONE
BEFORE = 4
AHEAD = 2
SAT = 17.0


def ceil_even(n):
    return n + n % 2


class Region:

    def __init__(self, t, words, at=0):
        self.t, self.words, self.at = t, words, at

    def take(self, shape, dt=F32):
        n = int(np.prod(shape))
        words = n if dt not in (BF16, F16) else ceil_even(n) // 2
        assert self.at + words <= self.words, (self.at, words, self.words)
        ap = self.t[:, self.at:self.at + words]
        self.at += ceil_even(words)
        if dt != F32:
            ap = ap.bitcast(dt)
        if len(shape) == 1:
            return ap
        names = "abcdef"[:len(shape)]
        kw = {c: s for c, s in zip(names[1:], shape[1:])}
        return ap.rearrange(f"p ({' '.join(names)}) -> p {' '.join(names)}", **kw)


class Chain:

    def __init__(self, eng, sem):
        self.eng, self.sem, self.n, self.loop = eng, sem, 0, None

    def link(self, ins):
        ins.then_inc(self.sem, 1)
        if self.loop is None:
            self.n += 1
            self.eng.wait_ge(self.sem, self.n)
        else:
            self.loop[1] += 1
            self.eng.wait_ge(self.sem, self.loop[0] * self.loop[2] + (self.n + self.loop[1]))

    def begin(self, i, per):
        self.loop = [i, 0, per]

    def end(self, trips):
        assert self.loop[1] == self.loop[2], self.loop
        self.n += trips * self.loop[2]
        self.loop = None


C_BANKS = (0, 5)
Y_BANKS = (6, 7, 0)


def tile_rows(t):
    return P if t < BATCH else IROWS if t < NT - 1 else LAST * IMG


def token_tiles(eng, body, pair_of=None):
    with eng.Fori(0, BATCH // 2) as i:
        if pair_of is not None:
            pair_of[0] = i
        body(2 * i, P, 0)
        body(2 * i + 1, P, 1)
    image_tiles(eng, body)


def image_tiles(eng, body):
    with eng.Fori(0, (IT - 2) // 2) as j:
        body(BATCH + 2 * j, IROWS, 0)
        body(BATCH + 1 + 2 * j, IROWS, 1)
    body(NT - 2, IROWS, 0)
    body(NT - 1, LAST * IMG, 1)


def pipelined(eng, n, body):
    pairs = (n - 3) // 2
    body(0, 0, 0)
    body(1, 1, 0)
    with eng.Fori(1, 1 + pairs) as j:
        body(2 * j, 0, j)
        body(2 * j + 1, 1, j)
    for i in range(2 + 2 * pairs, n):
        body(i, i % 2, i // 2)


def known(i, value):
    return isinstance(i, int) and i == value


def batch_cols(view, t, rows):
    if rows == P:
        return view[:, :, bass.ds(t * SEQ + IMG, TEXT)]
    nb = rows // IMG
    part = view[:, :, bass.ds((t - BATCH) * (PER * SEQ), PER * SEQ)]
    return part.rearrange("p k (b s) -> p k b s", s=SEQ)[:, :, 0:nb, 0:IMG]


def wait_from(eng, sem, value):
    if isinstance(value, int) and value <= 0:
        return
    eng.wait_ge(sem, value)


def build(nc, txt, patches, wtok, cols, rows_a, consts, pe_table, wsmall, w0, wattn, rows_f, w1, wsmall1,
          b2rows, out):
    with ExitStack() as ctx:
        def sb(name, shape, dt=F32):
            return ctx.enter_context(nc.sbuf_tensor(name, shape, dt))

        def sem(name):
            return ctx.enter_context(nc.semaphore(name))

        h = sb("h", [P, NT, D])
        XW, YW = G0 * E0 * W0N, 16900
        X = sb("X", [P, XW])
        Y = sb("Y", [P, YW])
        stage = sb("stage", [P, 2, CW])
        cst = sb("cst", [P, NCST])
        ccols = sb("ccols", [P, NCOL])
        wsm = sb("wsm", [P, NWS])
        upper = sb("upper", [P, P], BF16)
        onesb = sb("onesb", [P, P], BF16)
        onesf = sb("onesf", [P, P])
        stats = sb("stats", [P, NT, 2, 6])
        mv = sb("mv", [P, NT, 2])
        rs4 = sb("rs4", [P, 4, NT])
        var, std, rstd, newt = (rs4[:, i, :] for i in range(4))
        yv = sb("yv", [P, NT])
        ra = sb("ra", [P, 12, NT])
        rb = sb("rb", [P, 12, NT])
        rc = sb("rc", [P, 12, NT])
        oh = sb("oh", [P, TOPK, 4, NT])
        ohb = sb("ohb", [P, 4, NT], BF16)
        raf = ra.rearrange("p g t -> p (g t)")
        sm = sb("sm", [P, 32])
        hscale = sb("hscale", [P, 4])
        amax = sb("amax", [P, 4])
        gates = sb("gates", [P, TOPK, NT])
        posf = sb("posf", [P, TOPK, NT])
        pos = sb("pos", [P, TOPK, NT], I32)
        low7 = rc[:, 0:TOPK, :].bitcast(I32)
        high7 = rc[:, TOPK:2 * TOPK, :].bitcast(I32)
        tok = stats.rearrange("p t a b -> p (t a b)")[:, 0:3 * SLOT1].rearrange("p (i s) -> p i s", i=3)
        slote = sb("slote", [P, SLOT1], I32)
        PS = ctx.enter_context(nc.psum_tensor("PS", [P, 8, 512], F32))

        xs0 = nc.dram_tensor("xs0", [TOKENS, PAY0], F32).ap()
        ys0 = nc.dram_tensor("ys0", [DUMP + SLOT0, D], F32).ap()
        xs1 = nc.dram_tensor("xs1", [TOKENS, PAY1], F32).ap()
        ys1 = nc.dram_tensor("ys1", [DUMP + SLOT1, D], F32).ap()
        source = sb("source", [P, SLOT1], U32)
        dest = sb("dest", [P, SLOT1], U32)

        k_ident = cst[:, 0:P]
        k_upper = cst[:, P:2 * P]
        at = 2 * P
        k_valid = cst[:, at:at + NT]; at += NT
        k_reset = cst[:, at:at + 4 * NT]; at += 4 * NT
        k_fill = cst[:, at:at + 4 * NFULL].rearrange("p (g k) -> p g k", g=4); at += 4 * NFULL
        k_slot = cst[:, at:at + SLOT1]; at += SLOT1
        k_far = cst[:, at:at + NT]; at += NT
        k_tile = cst[:, at:at + TOPK * NT]; at += TOPK * NT
        k_iota = cst[:, at:at + P]; at += P
        k_row, k_patch, k_class = (cst[:, at + i:at + i + 1] for i in range(3))
        c_g1, c_b1 = ccols[:, 0:6], ccols[:, 6:12]
        c_bz, c_bq, c_bk = ccols[:, 12:14], ccols[:, 14:16], ccols[:, 16:18]
        c_bcd, c_alog, c_nega = ccols[0:96, 18:19], ccols[0:96, 19:20], ccols[0:96, 20:21]
        rw = Region(wsm, NWS)
        wbcd = rw.take([KC, 96])
        wz = rw.take([KC, D])
        wout = rw.take([KC, D])
        wr0 = rw.take([KC, 12])

        ry = Region(Y, YW)
        pt = ry.take([IT, PDIM])
        rs = Region(Y, YW)
        GS = SB * SEQ
        sB, sC, sD, sA = (rs.take([GS]) for _ in range(4))
        assert rs.at <= ry.at
        wt = ry.take([PC, D])
        sS = Region(Y, YW, rs.at).take([GS])
        rows = ry.take([6, D])
        r_g2, r_b2, r_tb, r_cls, r_cpos, r_bout = (rows[:, i, :] for i in range(6))
        pay_at = ry.at
        xT = ry.take([KC, PB * SEQ])
        pay = Region(Y, YW, pay_at).take([NT, PAY0])
        pT = ry.take([2, PC, IPAD])
        xn = ry.take([2, D])
        x2T = xn.rearrange("p a (k r) -> p a k r", k=KC)
        gT = ry.take([2, KC, P])
        petab = gT.rearrange("p a k n -> p (a k n)")[:, 0:D]
        rd = Region(Y, YW)
        xin = rd.take([2, PAY0])
        ybuf = rd.take([2, D])
        wall = rd.take([SLOT0, 2])
        xh = rd.take([2, KC, P], F16)
        xl = rd.take([2, KC, P], F16)
        sg = rd.take([2, F0])
        hh = rd.take([2, F0])
        hTh = rd.take([2, 4, P], F16)
        hTl = rd.take([2, 4, P], F16)
        hots0 = Region(Y, YW, rd.at)
        inrow0, intile0 = hots0.take([NT, P], BF16), hots0.take([NT, 3, SLOT0], BF16)
        assert hots0.at <= pay_at
        back = rd.take([NT, D])
        xnt = X[:, XW - BATCH * D:XW].rearrange("p (t n) -> p t n", t=BATCH)
        XNT_CHUNK = (XW - BATCH * D - XW // 2) // (CW // 2)
        end = Region(X, XW, XW - (NSM1 + 2 * (F1 // P) * E1 + 2 * E1 * D))
        small1 = end.take([NSM1])
        wr1 = small1[:, 0:4 * KC].rearrange("p (k e) -> p k e", k=KC)
        c_b1c = small1[:, 4 * KC:4 * KC + (F1 // P) * E1]
        c_br = small1[:, NSM1 - E1:NSM1]
        gb1 = end.take([(F1 // P) * E1])
        gbh, gbl = end.take([(F1 // P) * E1], F16), end.take([(F1 // P) * E1], F16)
        b2all = end.take([E1, D])
        rest1 = end.take([E1, D])
        XE = XW - (NSM1 + 2 * (F1 // P) * E1 + 2 * E1 * D)
        rx = Region(X, XE)
        wq, wk, wv, wf = (rx.take([KC, D]) for _ in range(4))
        tab = X[:, 4 * KC * D:NATT]
        k_cos, k_sin, k_nsin = (tab[:, i * SEQ:(i + 1) * SEQ] for i in range(3))
        k_maskA, k_maskB = tab[:, 3 * SEQ:3 * SEQ + P], tab[:, 3 * SEQ + P:4 * SEQ + P]
        rx.at = ceil_even(NATT)
        rowsF = rx.take([2, D])
        xnF = rx.take([2, D])
        xTi = rx.take([KC, PB * IMG])
        xTb = rx.take([2, KC, SEQ])
        qkT = rx.take([2, 2, KC, SEQ])
        qT, kT = qkT[:, :, 0], qkT[:, :, 1]
        tcos = rx.take([2, KC, SEQ])
        tsin = rx.take([2, KC, SEQ])
        vb = rx.take([2, 2, D])
        sA1, sB1 = rx.take([P]), rx.take([SEQ])
        pA, pB = rx.take([P]), rx.take([SEQ])
        pT1, pT2 = rx.take([SEQ]), rx.take([SEQ - P])
        oTb = rx.take([KC, P])
        oTi = rx.take([KC, PB * IMG])
        nmax, smax, psum_, rsum = (rx.take([2]) for _ in range(4))
        rg = Region(X, XE)
        early = Region(X, XE, rg.at)
        inrow1, intile1 = early.take([TOPK * NT, P], BF16), early.take([TOPK * NT, 3, SLOT1], BF16)
        back1 = rg.take([NT, D])
        hh1 = rg.take([2, 4, T1])
        assert early.at <= rg.at
        pay1 = rg.take([NT, PAY1])
        back0 = pay1.rearrange("p t n -> p (t n)")[:, 0:NT * D].rearrange("p (t n) -> p t n", t=NT)
        wall1 = rg.take([SLOT1])
        bias1 = rg.take([2, F1 // P])
        x2G = rg.take([2, KC, P])
        x1in = rg.take([2, 2, PAY1])
        y1buf = rg.take([2, 2, D])
        x1h, x1l = rg.take([2, KC, T1], F16), rg.take([2, KC, T1], F16)
        h1Th, h1Tl = rg.take([2, 4, T1], F16), rg.take([2, 4, T1], F16)
        csum = rg.take([D])
        w1h = Y[:, 0:W1W // 2].bitcast(F16)
        w1l = Y[:, W1W // 2:W1W].bitcast(F16)
        w0h = X[:, 0:XW // 2].bitcast(F16)
        w0l = X[:, XW // 2:XW].bitcast(F16)

        text_loaded = sem("text_loaded")
        patches_loaded = sem("patches_loaded")
        small_loaded = sem("small_loaded")
        consts_ready = sem("consts_ready")
        pads_zeroed = sem("pads_zeroed")
        dve_done = sem("dve_done")
        act_done = sem("act_done")
        var_ready = sem("var_ready")
        std_ready = sem("std_ready")
        nega_ready = sem("nega_ready")
        patch_normed = sem("patch_normed")
        patch_tr = sem("patch_tr")
        patch_copied = sem("patch_copied")
        tokb_psum = sem("tokb_psum")
        wt_scaled = sem("wt_scaled")
        tok_psum = sem("tok_psum")
        tok_added = sem("tok_added")
        tok_ready = sem("tok_ready")
        xn_ready = sem("xn_ready")
        xn_tr = sem("xn_tr")
        xT_copied = sem("xT_copied")
        bcd_psum = sem("bcd_psum")
        bc_copied = sem("bc_copied")
        dl_copied = sem("dl_copied")
        sp_ready = sem("sp_ready")
        delta_ready = sem("delta_ready")
        decay_ready = sem("decay_ready")
        sc_ready = sem("sc_ready")
        y_psum = sem("y_psum")
        z_psum = sem("z_psum")
        g_ready = sem("g_ready")
        o_psum = sem("o_psum")
        h_added = sem("h_added")
        hb_added = sem("hb_added")
        stage_full = [sem("stage_full0"), sem("stage_full1")]
        stage_free = sem("stage_free")
        w_high = sem("w_high")
        own_high = sem("own_high")
        x2_copied = sem("x2_copied")
        stats_ready = sem("stats_ready")
        route_psum = sem("route_psum")
        logits_ready = sem("logits_ready")
        sig_ready = sem("sig_ready")
        choice_ready = sem("choice_ready")
        count_psum = sem("count_psum")
        pay_ready = sem("pay_ready")
        x_in = [sem("x_in0"), sem("x_in1")]
        x_tr = sem("x_tr")
        x_w = sem("x_w")
        x_hi = sem("x_hi")
        x_lo = sem("x_lo")
        gate_psum = sem("gate_psum")
        up_psum = sem("up_psum")
        act_out = sem("act_out")
        h_ready = sem("h_ready")
        hT_psum = sem("hT_psum")
        hT_hi = sem("hT_hi")
        hT_lo = sem("hT_lo")
        y_done = sem("y_done")
        y_copied = sem("y_copied")
        y_out = [sem("y_out0"), sem("y_out1")]
        hot_ready = sem("hot_ready")
        map_psum = sem("map_psum")
        source_ready = sem("source_ready")
        dest_ready = sem("dest_ready")
        rows_stored = sem("rows_stored")
        taken_back = [sem(f"taken_back{i}") for i in range(len(RUNS))]
        added_back = sem("added_back")
        out_written = sem("out_written")
        slots_ready = sem("slots_ready")
        amax_ready = sem("amax_ready")
        amax_row = sem("amax_row")
        amax_psum = sem("amax_psum")
        scale_ready = sem("scale_ready")
        attn_loaded = sem("attn_loaded")
        xTi_copied = sem("xTi_copied")
        xTb_copied = sem("xTb_copied")
        xTb_image = sem("xTb_image")
        q_psum = sem("q_psum")
        k_psum = sem("k_psum")
        v_psum = sem("v_psum")
        rope_mul = sem("rope_mul")
        rope_done = sem("rope_done")
        v_copied = sem("v_copied")
        s_psum = sem("s_psum")
        s_max = sem("s_max")
        p_exp = sem("p_exp")
        p_normed = sem("p_normed")
        pt_psum = sem("pt_psum")
        pt_copied = sem("pt_copied")
        ot_psum = sem("ot_psum")
        ot_copied = sem("ot_copied")
        pr_psum = sem("pr_psum")
        bf_added = sem("bf_added")
        h3_added = sem("h3_added")
        small1_loaded = sem("small1_loaded")
        rest_ready = sem("rest_ready")
        c_copied = sem("c_copied")
        added_pool = sem("added_pool")
        gb_ready = sem("gb_ready")
        gb_split = sem("gb_split")
        c_psum = sem("c_psum")
        biased = sem("biased")
        x1_in = [sem("x1_in0"), sem("x1_in1")]
        x1_tr = sem("x1_tr")
        x1_hi = sem("x1_hi")
        x1_lo = sem("x1_lo")
        x1_w = sem("x1_w")
        in_psum = sem("in_psum")
        gelu_ready = sem("gelu_ready")
        h1_hi = sem("h1_hi")
        h1_lo = sem("h1_lo")
        y1_done = sem("y1_done")
        y1_based = sem("y1_based")
        y1_copied = sem("y1_copied")
        y1_out = [sem(f"y1_out{i}") for i in range(4)]

        NSMALL = 6

        block = ctx.enter_context(nc.Block())

        def store_out(sp):
            n = 0
            for k in OUT_STORES:
                t, tiles, r = RUNS[k]
                if k in OUT_DVE:
                    sp.wait_ge(added_back, len(BACK_DVE) + 2 * (OUT_DVE.index(k) + 1))
                else:
                    sp.wait_ge(added_pool, len(BACK_POOL) + 2 * (OUT_POOL.index(k) + 1))
                if r == P:
                    sp.dma_start(out[t:t + tiles, IMG:SEQ, :].rearrange("b s d -> s b d"), h[:, t:t + tiles, :])\
                        .then_inc(out_written, 16)
                    n += 1
                    continue
                for i in range(r // IMG):
                    first = PER * (t - BATCH)
                    to = out[first + i:first + i + 1] if tiles == 1 else \
                        out[first:first + PER * tiles].rearrange("(j i) s d -> i j s d", i=PER)[i]
                    sp.dma_start(to[:, 0:IMG, :].rearrange("b s d -> s b d"), h[i * IMG:(i + 1) * IMG, t:t + tiles, :])\
                        .then_inc(out_written, 16)
                    n += 1
            sp.wait_ge(out_written, 16 * n)

        def act_dispatch(act, before, x2T_, bank0):
            def copies(t, slot, j):
                act.wait_ge(xn_tr, before[0] * NT + AHEAD + t + 1)
                nc.scalar.activation(x2T_[:, slot, :, :], PS[:, bank0 + slot, 0:KC * P].rearrange("p (k r) -> p k r", k=KC),
                                     ACT.Copy).then_inc(x2_copied, 1)
            pipelined(act, NT, copies)

        def pe_route(pe, before, x2T_, pay_, weights, n, bank0):
            def product(t, slot):
                pe.wait_ge(x2_copied, before[1] * NT + t + 1)
                for k in range(KC):
                    ins = nc.tensor.matmul(PS[:, 6, bass.ds(t * n, n)], x2T_[:, slot, k, :], weights[:, k, :],
                                           start=(k == 0), stop=(k == KC - 1))
                ins.then_inc(route_psum, 1)

            for t in range(NT):
                pe.wait_ge(xn_ready, before[0] * NT + t + 1)
                for k in range(KC):
                    ins = nc.tensor.transpose(PS[:, bank0 + t % 2, k * P:(k + 1) * P], pay_[:, t, k * P:(k + 1) * P], k_ident)
                ins.then_inc(xn_tr, 1)
                if t:
                    product(t - 1, (t - 1) % 2)
            product(NT - 1, (NT - 1) % 2)

        def pe_count(pe, done):
            pe.wait_ge(choice_ready, done + 1)
            flat = ohb.rearrange("p g t -> p (g t)")
            nc.tensor.matmul(PS[:, 7, 0:4 * NT], upper[:, :], flat, start=True, stop=True)
            nc.tensor.matmul(PS[:, 7, 128:128 + 4 * NT], onesb[:, :], flat, start=True, stop=True)\
                .then_inc(count_psum, 1)

        def pe_slots(pe, done, n, tiles, inrow, intile):
            for i in range(n):
                if i % (n // 2) == 0:
                    pe.wait_ge(hot_ready, 2 * done + i // (n // 2) + 1)
                ins = nc.tensor.matmul(PS[:, 7, 0:3 * tiles], inrow[:, i, :], intile[:, i, :, :].rearrange("p a b -> p (a b)"),
                                       start=(i == 0), stop=(i == n - 1))
            ins.then_inc(map_psum, 1)

        def dve_norm(dve, pay_):
            def norm(t, slot, j):
                nc.vector.tensor_scalar(pay_[:, bass.ds(t, 1), 0:D], h[:, bass.ds(t, 1), :], mv[:, bass.ds(t, 1), 0],
                                        rstd[:, bass.ds(t, 1)], ALU.subtract, ALU.mult).then_inc(xn_ready, 1)
            pipelined(dve, NT, norm)

        def moments_of_all(dve, chain, layer):
            dve.wait_ge(stats_ready, layer * NT)
            for t in range(NT):
                ins = nc.vector.bn_aggr(mv[:, t, :], stats[:, t, 0, :])
            chain.link(ins)

        def over(ap, n):
            return ap.unsqueeze(1).broadcast_to([P, n, NT])

        def first_max(chain, values, top, hot):
            chain.link(nc.vector.tensor_reduce(top, values.rearrange("p g t -> p t g"), AX, ALU.max))
            chain.link(nc.vector.tensor_tensor(hot, values, over(top, 4), ALU.is_equal))
            taken = newt
            chain.link(nc.vector.tensor_copy(taken, hot[:, 0, :]))
            for g in range(1, 4):
                chain.link(nc.vector.tensor_tensor(hot[:, g, :], hot[:, g, :], taken, ALU.is_gt))
                chain.link(nc.vector.tensor_tensor(taken, taken, hot[:, g, :], ALU.max))

        def sum_over(chain, out_, values):
            chain.link(nc.vector.tensor_reduce(out_, values.rearrange("p g t -> p t g"), AX, ALU.add))

        def positions(dve, chain, choices, tiles, done, inrow, intile, unit):
            hot = rc[:, 0:4, :]
            if choices == 2:
                chain.link(nc.vector.tensor_tensor(hot, oh[:, 0], oh[:, 1], ALU.add))
                chain.link(nc.vector.tensor_tensor(hot, hot, over(k_valid, 4), ALU.mult))
            else:
                chain.link(nc.vector.tensor_tensor(hot, oh[:, 0], over(k_valid, 4), ALU.mult))
            nc.vector.tensor_copy(ohb[:, :, :], hot).then_inc(choice_ready, 1)
            dve.wait_ge(count_psum, done + 1)
            before_, total, upto = rc[:, 0:4, :], rc[:, 4:8, :], rc[:, 8:12, :]
            flat = lambda ap: ap.rearrange("p g t -> p (g t)")
            nc.vector.tensor_copy(flat(before_), PS[:, 7, 0:4 * NT])
            chain.link(nc.vector.tensor_copy(flat(total), PS[:, 7, 128:128 + 4 * NT]))
            chain.link(nc.vector.tensor_tensor_scan(flat(upto), k_reset, flat(total), 0.0, ALU.mult, ALU.add))
            most = -(-NFULL // unit)
            n_of = upto[:, :, NT - 1:NT].broadcast_to([P, 4, most])
            full = raf[:, 0:4 * most].rearrange("p (g k) -> p g k", g=4)
            chain.link(nc.vector.tensor_tensor(full, n_of, k_fill[:, :, 0:NFULL:unit], ALU.is_gt))
            tl, st, sl = sm[:, 0:4], sm[:, 4:8], sm[:, 8:12]
            chain.link(nc.vector.tensor_reduce(tl, full, AX, ALU.add))
            chain.link(nc.vector.memset(st[:, 0:1], 0.0))
            for g in range(1, 4):
                chain.link(nc.vector.tensor_tensor(st[:, g:g + 1], st[:, g - 1:g], tl[:, g - 1:g], ALU.add))
            chain.link(nc.vector.tensor_scalar(sl, st, float(P * unit), None, ALU.mult))
            chain.link(nc.vector.tensor_tensor(upto, upto, total, ALU.subtract))
            chain.link(nc.vector.tensor_tensor(before_, before_, upto, ALU.add))
            chain.link(nc.vector.tensor_tensor(before_, before_, sl.unsqueeze(2).broadcast_to([P, 4, NT]), ALU.add))
            for c in range(choices):
                chain.link(nc.vector.tensor_tensor(total, oh[:, c], before_, ALU.mult))
                sum_over(chain, posf[:, c, :], total)
            slots_of = posf[:, 0:choices, :]
            chain.link(nc.vector.tensor_tensor(slots_of, slots_of, k_far.unsqueeze(1).broadcast_to([P, choices, NT]), ALU.add))
            chain.link(nc.vector.tensor_copy(pos[:, 0:choices, :], slots_of))
            chain.link(nc.vector.tensor_scalar(low7[:, 0:choices, :], pos[:, 0:choices, :], P - 1, None, ALU.bitwise_and))
            chain.link(nc.vector.tensor_scalar(high7[:, 0:choices, :], pos[:, 0:choices, :], 7, None,
                                               ALU.logical_shift_right))
            n = choices * NT
            chain.link(nc.vector.tensor_copy(slots_of, high7[:, 0:choices, :]))
            each = lambda ap, m: ap.rearrange("p c t -> p (c t)").unsqueeze(2).broadcast_to([P, n, m])
            along = lambda ap, m: ap.unsqueeze(1).broadcast_to([P, n, m])
            chain.link(nc.vector.tensor_tensor(intile[:, :, 2, :], each(slots_of, tiles), along(k_slot[:, 0:tiles], tiles),
                                               ALU.is_equal))
            chain.link(nc.vector.tensor_copy(slots_of, low7[:, 0:choices, :]))
            nc.vector.tensor_tensor(intile[:, :, 0, :], intile[:, :, 2, :],
                                    k_tile[:, 0:n].unsqueeze(2).broadcast_to([P, n, tiles]), ALU.mult)
            nc.vector.tensor_scalar(intile[:, :, 1, :], intile[:, :, 2, :], k_row, None, ALU.mult)
            half = n // 2
            for c0 in (0, half):
                nc.vector.tensor_tensor(inrow[:, c0:c0 + half, :], each(slots_of, P)[:, c0:c0 + half],
                                        along(k_iota, P)[:, c0:c0 + half], ALU.is_equal).then_inc(hot_ready, 1)
            units = tiles // unit
            sf = tok[:, 0, 0:units]
            chain.link(nc.vector.tensor_scalar(sf, k_slot[:, 0:units], st[:, 1:2], None, ALU.is_ge))
            for g in (2, 3):
                chain.link(nc.vector.scalar_tensor_tensor(out=sf, in0=k_slot[:, 0:units], scalar=st[:, g:g + 1],
                                                          in1=sf, op0=ALU.is_ge, op1=ALU.add))
            nc.vector.tensor_copy(slote[:, 0:units], sf).then_inc(slots_ready, 1)
            dve.wait_ge(map_psum, done + 1)
            tile_, row_, taken = (PS[:, 7, i * tiles:(i + 1) * tiles] for i in range(3))
            place, from_, to = (tok[:, i, 0:tiles] for i in range(3))
            chain.link(nc.vector.tensor_copy(from_, row_))
            chain.link(nc.vector.scalar_tensor_tensor(out=place, in0=tile_, scalar=float(P), in1=from_, op0=ALU.mult,
                                                      op1=ALU.add))
            chain.link(nc.vector.tensor_scalar(from_, place, float(TOKENS), -float(TOKENS), ALU.is_ge, ALU.mult))
            chain.link(nc.vector.tensor_tensor(from_, from_, place, ALU.add))
            nc.vector.tensor_copy(source[:, 0:tiles], from_).then_inc(source_ready, 1)
            dve.wait_ge(source_ready, done + 1)
            chain.link(nc.vector.tensor_scalar(from_, k_slot[:, 0:tiles], float(DUMP), None, ALU.add))
            chain.link(nc.vector.tensor_tensor(to, from_, taken, ALU.mult))
            chain.link(nc.vector.tensor_tensor(to, from_, to, ALU.subtract))
            chain.link(nc.vector.tensor_tensor(to, to, place, ALU.add))
            nc.vector.tensor_copy(dest[:, 0:tiles], to).then_inc(dest_ready, 1)

        def dve_bound(dve, chain, weights, bound):
            chain.link(nc.vector.tensor_reduce(amax[:, 0:1], weights, AXS[len(weights.shape) - 2], ALU.max,
                                               apply_absolute_value=True))
            bound(amax[:, 0:1])
            dve.sem_inc(amax_ready, 1)

        def dve_scale(dve, chain, layer):
            dve.wait_ge(amax_psum, 2 * layer + 1)
            nc.vector.tensor_reduce(amax[0:1, 1:2], PS[0:1, 3, 0:P], AX, ALU.max).then_inc(amax_row, 1)
            dve.wait_ge(amax_psum, 2 * layer + 2)
            top, scale_, un = amax[:, 2:3], hscale[:, 2 * layer:2 * layer + 1], hscale[:, 2 * layer + 1:2 * layer + 2]
            chain.link(nc.vector.tensor_copy(top, PS[:, 3, 256:257]))
            if layer == 0:
                chain.link(nc.vector.tensor_tensor(top, top, top, ALU.mult))
                chain.link(nc.vector.tensor_scalar(un, top, float(D * D) / 2 ** 15, 1e-20, ALU.mult, ALU.max))
            else:
                chain.link(nc.vector.tensor_scalar(un, top, 1.0 / 2 ** 15, 1e-20, ALU.mult, ALU.max))
            chain.link(nc.vector.reciprocal(scale_, un))
            dve.sem_inc(scale_ready, 1)

        def pe_scale(pe, layer):
            pe.wait_ge(amax_ready, layer + 1)
            nc.tensor.transpose(PS[0:1, 3, 0:P], amax[:, 0:1], k_ident).then_inc(amax_psum, 1)
            pe.wait_ge(amax_row, layer + 1)
            nc.tensor.matmul(PS[:, 3, 256:257], onesf[0:1, :], amax[0:1, 1:2], start=True, stop=True).then_inc(amax_psum, 1)

        def store_rows(sp, rows_, pay_, n):
            sp.wait_ge(pay_ready, n)
            sp.dma_start(rows_.rearrange("(t p) n -> p t n", p=P), pay_).then_inc(rows_stored, 16)

        def take_back(sp, results, choice, buffer, k):
            tile0, n, r = RUNS[k]
            rows_ = results[choice * TOKENS + tile0 * P:choice * TOKENS + (tile0 + n) * P, :]
            sp.dma_start(buffer[0:r, tile0:tile0 + n, :], rows_.rearrange("(t p) n -> p t n", p=P)[0:r, :, :])\
                .then_inc(taken_back[k], 16)

        def expert_weights(pe, w_hi, w_lo, words, i, experts):
            e = pe.value_load(slote[0:1, bass.ds(i, 1)], min_val=0, max_val=experts - 1)
            return tuple(w_.rearrange("p (e n) -> p e n", n=words)[:, bass.ds(e, 1), :].rearrange("p e n -> p (e n)")
                         for w_ in (w_hi, w_lo))

        def pe_experts0(pe):
            def transpose_x(i, slot, j):
                pe.wait_ge(x_in[slot], 16 * (j + 1))
                for k in range(KC):
                    ins = nc.tensor.transpose(PS[:, 7, k * P:(k + 1) * P], xin[:, slot, k * P:(k + 1) * P], k_ident)
                ins.then_inc(x_tr, 1)

            def products_in(i, s, w_, slot):
                if s == 0:
                    pe.wait_ge(x_lo, i + 1)
                for u in range(2):
                    n = 0
                    for k in range(KC):
                        off = s * W0N + (u * KC + k) * F0
                        for x_, part in ((xh, w_[0]), (xh, w_[1]), (xl, w_[0])):
                            ins = nc.tensor.matmul(PS[:, 2 * u + s, 0:F0], x_[:, slot, k, :], part[:, off:off + F0],
                                                   start=(n == 0), stop=(n == 3 * KC - 1))
                            n += 1
                    ins.then_inc(up_psum if u else gate_psum, 1)

            def transpose_h(i, s):
                pe.wait_ge(h_ready, 2 * i + s + 1)
                for c in range(4):
                    ins = nc.tensor.transpose(PS[:, 4 + s, c * P:(c + 1) * P], hh[:, s, c * P:(c + 1) * P], k_ident)
                ins.then_inc(hT_psum, 1)

            def product_out(i, s, w_):
                pe.wait_ge(hT_lo, 2 * i + s + 1)
                if s == 0:
                    wait_from(pe, y_copied, i)
                for c in range(4):
                    off = s * W0N + 2 * KC * F0 + c * D
                    for n, (h_, part) in enumerate(((hTh, w_[0]), (hTh, w_[1]), (hTl, w_[0]))):
                        ins = nc.tensor.matmul(PS[:, 6, 0:D], h_[:, s, c, :], part[:, off:off + D],
                                               start=(s == 0 and c == 0 and n == 0), stop=(s == 1 and c == 3 and n == 2))
                if s == 1:
                    ins.then_inc(y_done, 1)

            def weights(i):
                return expert_weights(pe, w0h, w0l, E0 * W0N, i, G0)
            held = [None, None]

            def tile(i, slot, j):
                w_ = weights(i)
                if known(i, 0):
                    transpose_x(0, 0, 0)
                products_in(i, 0, w_, slot)
                if not known(i, 0):
                    last = held[1] if slot == 1 or isinstance(i, int) and held[0] == i - 1 else weights(i - 1)
                    transpose_h(i - 1, 1)
                if not known(i, SLOT0 - 1):
                    transpose_x(i + 1, 1 - slot, j + slot)
                if not known(i, 0):
                    product_out(i - 1, 0, last)
                products_in(i, 1, w_, slot)
                transpose_h(i, 0)
                if not known(i, 0):
                    product_out(i - 1, 1, last)
                held[:] = [i if isinstance(i, int) else None, w_]
            pipelined(pe, SLOT0, tile)
            n = SLOT0 - 1
            w_ = weights(n)
            product_out(n, 0, w_)
            transpose_h(n, 1)
            product_out(n, 1, w_)

        def act_experts0(act):
            def split_x(i, slot):
                act.wait_ge(x_tr, i + 1)
                nc.scalar.activation(xh[:, slot].rearrange("p k r -> p (k r)"), PS[:, 7, 0:KC * P], ACT.Copy)\
                    .then_inc(x_hi, 1)

            def nonlinear(i, s):
                act.wait_ge(gate_psum, 2 * i + s + 1)
                nc.scalar.activation(sg[:, s, :], PS[:, s, 0:F0], ACT.Silu).then_inc(act_out, 1)

            def split_h(i, s):
                act.wait_ge(hT_psum, 2 * i + s + 1)
                nc.scalar.activation(hTh[:, s, :, :].rearrange("p c r -> p (c r)"), PS[:, 4 + s, 0:F0], ACT.Copy,
                                     scale=hscale[:, 0:1]).then_inc(hT_hi, 1)

            def copy_y(i, slot, j):
                act.wait_ge(y_done, i + 1)
                if not (isinstance(j, int) and j == 0):
                    act.wait_ge(y_out[slot], 16 * j)
                nc.scalar.activation(ybuf[:, slot, :], PS[:, 6, 0:D], ACT.Copy, scale=hscale[:, 1:2])\
                    .then_inc(y_copied, 1)

            def tile(i, slot, j):
                if known(i, 0):
                    split_x(0, 0)
                nonlinear(i, 0)
                if not known(i, 0):
                    split_h(i - 1, 1)
                if not known(i, SLOT0 - 1):
                    split_x(i + 1, 1 - slot)
                nonlinear(i, 1)
                split_h(i, 0)
                if not known(i, 0):
                    copy_y(i - 1, 1 - slot, j + slot - 1)
            pipelined(act, SLOT0, tile)
            n = SLOT0 - 1
            split_h(n, 1)
            copy_y(n, n % 2, n // 2)

        def dve_experts0(dve):
            def split_x(i, slot, j):
                dve.wait_ge(x_hi, i + 1)
                nc.vector.tensor_tensor(xl[:, slot].rearrange("p k r -> p (k r)"), PS[:, 7, 0:KC * P],
                                        xh[:, slot].rearrange("p k r -> p (k r)"), ALU.subtract).then_inc(x_lo, 1)
                dve.wait_ge(x_in[slot], 16 * (j + 1))
                nc.vector.tensor_copy(wall[:, bass.ds(i, 1), :], xin[:, slot:slot + 1, D:PAY0]).then_inc(x_w, 1)

            def combine(i, s):
                step = 2 * i + s + 1
                dve.wait_ge(x_w, i + 1)
                dve.wait_ge(up_psum, step)
                dve.wait_ge(act_out, step)
                nc.vector.scalar_tensor_tensor(out=hh[:, s, :].unsqueeze(1), in0=PS[:, 2 + s, 0:F0].unsqueeze(1),
                                               scalar=wall[:, bass.ds(i, 1), s], in1=sg[:, s, :].unsqueeze(1),
                                               op0=ALU.mult, op1=ALU.mult).then_inc(h_ready, 1)

            def split_h(i, s):
                dve.wait_ge(hT_hi, 2 * i + s + 1)
                nc.vector.scalar_tensor_tensor(out=hTl[:, s, :, :].rearrange("p c r -> p (c r)"), in0=PS[:, 4 + s, 0:F0],
                                               scalar=hscale[:, 0:1], in1=hTh[:, s, :, :].rearrange("p c r -> p (c r)"),
                                               op0=ALU.mult, op1=ALU.subtract).then_inc(hT_lo, 1)

            def tile(i, slot, j):
                if known(i, 0):
                    split_x(0, 0, 0)
                combine(i, 0)
                if not known(i, 0):
                    split_h(i - 1, 1)
                if not known(i, SLOT0 - 1):
                    split_x(i + 1, 1 - slot, j + slot)
                combine(i, 1)
                split_h(i, 0)
            pipelined(dve, SLOT0, tile)
            split_h(SLOT0 - 1, 1)

        def pool_slots(pool, tiles, lag, gather, send):
            for n in range(tiles + lag):
                if n < tiles:
                    gather(n)
                if n >= lag:
                    send(n - lag)

        def pool_slots0(pool):
            pool.wait_ge(rows_stored, 16)
            pool.wait_ge(source_ready, 1)
            pool.wait_ge(dest_ready, 1)

            def gather(n):
                if n >= 2:
                    pool.wait_ge(x_tr, n - 1)
                    pool.wait_ge(x_w, n - 1)
                nc.gpsimd.indirect_dma_start(
                    out=xin[:, n % 2, :], out_offset=None, in_=xs0,
                    in_offset=bass.IndirectOffsetOnAxis(ap=source[:, n:n + 1], axis=0)).then_inc(x_in[n % 2], 16)

            def send(i):
                pool.wait_ge(y_copied, i + 1)
                nc.gpsimd.indirect_dma_start(
                    out=ys0, out_offset=bass.IndirectOffsetOnAxis(ap=dest[:, i:i + 1], axis=0),
                    in_=ybuf[:, i % 2, :], in_offset=None).then_inc(y_out[i % 2], 16)
            pool_slots(pool, SLOT0, 3, gather, send)

        def pe_experts1(pe):
            def transpose_x(i, slot, j):
                pe.wait_ge(x1_in[slot], 32 * (j + 1))
                for k in range(KC):
                    for a in range(2):
                        ins = nc.tensor.transpose(PS[:, 7, (2 * k + a) * P:(2 * k + a + 1) * P],
                                                  x1in[:, slot, a, k * P:(k + 1) * P], k_ident)
                ins.then_inc(x1_tr, 1)

            def products_in(i, s, w_, slot):
                if s == 0:
                    pe.wait_ge(x1_lo, i + 1)
                if not known(i, 0):
                    pe.wait_ge(gelu_ready, 2 * i + s - 1)
                for c in range(4):
                    n = 0
                    for k in range(KC):
                        off = (s * KC + k) * F0 + c * P
                        for x_, part in ((x1h, w_[0]), (x1l, w_[0]), (x1h, w_[1])):
                            ins = nc.tensor.matmul(PS[:, 2 * s + c // 2, (c % 2) * T1:(c % 2 + 1) * T1], part[:, off:off + P],
                                                   x_[:, slot, k, :], start=(n == 0), stop=(n == 3 * KC - 1))
                            n += 1
                ins.then_inc(in_psum, 1)

            def product_out(i, s, w_):
                pe.wait_ge(h1_lo, 2 * i + s + 1)
                if s == 0:
                    wait_from(pe, y1_copied, 2 * i)
                for a in range(2):
                    for c in range(4):
                        off = KC * F1 + (4 * s + c) * D
                        for n, (h_, part) in enumerate(((h1Th, w_[0]), (h1Th, w_[1]), (h1Tl, w_[0]))):
                            ins = nc.tensor.matmul(PS[:, 4 + a, 0:D], h_[:, s, c, a * P:(a + 1) * P], part[:, off:off + D],
                                                   start=(s == 0 and c == 0 and n == 0),
                                                   stop=(s == 1 and c == 3 and n == 2))
                ins.then_inc(y1_done, 1)

            def weights(i):
                return expert_weights(pe, w1h, w1l, W1N, i, E1)
            held = [None, None]

            def tile(i, slot, j):
                w_ = weights(i)
                if known(i, 0):
                    transpose_x(0, 0, 0)
                products_in(i, 0, w_, slot)
                if not known(i, 0):
                    last = held[1] if slot == 1 or isinstance(i, int) and held[0] == i - 1 else weights(i - 1)
                if not known(i, PAIRS1 - 1):
                    transpose_x(i + 1, 1 - slot, j + slot)
                if not known(i, 0):
                    product_out(i - 1, 0, last)
                products_in(i, 1, w_, slot)
                if not known(i, 0):
                    product_out(i - 1, 1, last)
                held[:] = [i if isinstance(i, int) else None, w_]
            pipelined(pe, PAIRS1, tile)
            n = PAIRS1 - 1
            w_ = weights(n)
            product_out(n, 0, w_)
            product_out(n, 1, w_)

        def act_experts1(act):
            def split_x(i, slot):
                act.wait_ge(x1_tr, i + 1)
                nc.scalar.activation(x1h[:, slot].rearrange("p k r -> p (k r)"), PS[:, 7, :], ACT.Copy).then_inc(x1_hi, 1)

            def nonlinear(i, s, slot):
                act.wait_ge(in_psum, 2 * i + s + 1)
                if not known(i, 0):
                    act.wait_ge(h1_lo, 2 * i + s - 1)
                if s == 0:
                    act.wait_ge(biased, i + 1)
                for c in range(4):
                    f = 4 * s + c
                    ins = nc.scalar.activation(hh1[:, s, c, :], PS[:, 2 * s + c // 2, (c % 2) * T1:(c % 2 + 1) * T1],
                                               ACT.Gelu, bias=bias1[:, slot, f:f + 1])
                ins.then_inc(gelu_ready, 1)

            def copy_y(i, slot, j):
                for a in range(2):
                    act.wait_ge(y1_based, 2 * i + a + 1)
                    if not (isinstance(j, int) and j == 0):
                        act.wait_ge(y1_out[2 * slot + a], 16 * j)
                    nc.scalar.activation(y1buf[:, slot, a, :], PS[:, 4 + a, 0:D], ACT.Copy,
                                         scale=wall1[:, bass.ds(2 * i + a, 1)]).then_inc(y1_copied, 1)

            def tile(i, slot, j):
                if known(i, 0):
                    split_x(0, 0)
                nonlinear(i, 0, slot)
                if not known(i, PAIRS1 - 1):
                    split_x(i + 1, 1 - slot)
                nonlinear(i, 1, slot)
                if not known(i, 0):
                    copy_y(i - 1, 1 - slot, j + slot - 1)
            pipelined(act, PAIRS1, tile)
            copy_y(PAIRS1 - 1, (PAIRS1 - 1) % 2, (PAIRS1 - 1) // 2)

        def dve_experts1(dve):
            def split_x(i, slot, j, e):
                dve.wait_ge(x1_hi, i + 1)
                nc.vector.tensor_tensor(x1l[:, slot].rearrange("p k r -> p (k r)"), PS[:, 7, :],
                                        x1h[:, slot].rearrange("p k r -> p (k r)"), ALU.subtract).then_inc(x1_lo, 1)
                dve.wait_ge(x1_in[slot], 32 * (j + 1))
                nc.vector.tensor_copy(wall1[:, bass.ds(2 * i, 2)].unsqueeze(2), x1in[:, slot, :, bass.ds(e + D, 1)])\
                    .then_inc(x1_w, 1)
                if not (isinstance(i, int) and i < 2):
                    dve.wait_ge(gelu_ready, 2 * i - 2)
                nc.vector.tensor_copy(bias1[:, slot:slot + 1, :],
                                      c_b1c.rearrange("p (e f) -> p e f", e=E1)[:, bass.ds(e, 1), :]).then_inc(biased, 1)

            def split_h(i, s):
                step = 2 * i + s + 1
                act_, hi_, lo_ = (v[:, s].rearrange("p c r -> p (c r)") for v in (hh1, h1Th, h1Tl))
                dve.wait_ge(gelu_ready, step)
                if not known(i, 0):
                    dve.wait_ge(y1_done, step - 2)
                nc.vector.tensor_scalar(hi_, act_, hscale[:, 2:3], None, ALU.mult).then_inc(h1_hi, 1)
                dve.wait_ge(h1_hi, step)
                nc.vector.scalar_tensor_tensor(out=lo_, in0=act_, scalar=hscale[:, 2:3], in1=hi_, op0=ALU.mult,
                                               op1=ALU.subtract).then_inc(h1_lo, 1)

            def base_y(i, e):
                dve.wait_ge(y1_done, 2 * i + 2)
                for a in range(2):
                    y_ = PS[:, 4 + a, 0:D].unsqueeze(1)
                    nc.vector.scalar_tensor_tensor(out=y_, in0=y_, scalar=hscale[:, 3:4], in1=rest1[:, bass.ds(e, 1), :],
                                                   op0=ALU.mult, op1=ALU.add).then_inc(y1_based, 1)

            def expert_of(i):
                return dve.value_load(slote[0:1, bass.ds(i, 1)], min_val=0, max_val=E1 - 1)

            def tile(i, slot, j):
                if known(i, 0):
                    split_x(0, 0, 0, expert_of(0))
                if not known(i, PAIRS1 - 1):
                    split_x(i + 1, 1 - slot, j + slot, expert_of(i + 1))
                split_h(i, 0)
                if not known(i, 0):
                    base_y(i - 1, expert_of(i - 1))
                split_h(i, 1)
            pipelined(dve, PAIRS1, tile)
            base_y(PAIRS1 - 1, expert_of(PAIRS1 - 1))

        def pool_slots1(pool):
            pool.wait_ge(rows_stored, 32)
            pool.wait_ge(source_ready, 2)
            pool.wait_ge(dest_ready, 2)

            def gather(n):
                if n >= 4:
                    pool.wait_ge(x1_tr, n // 2 - 1)
                    pool.wait_ge(x1_w, n // 2 - 1)
                nc.gpsimd.indirect_dma_start(
                    out=x1in[:, n // 2 % 2, n % 2, :], out_offset=None, in_=xs1,
                    in_offset=bass.IndirectOffsetOnAxis(ap=source[:, n:n + 1], axis=0)).then_inc(x1_in[n // 2 % 2], 16)

            def send(i):
                pool.wait_ge(y1_copied, i + 1)
                nc.gpsimd.indirect_dma_start(
                    out=ys1, out_offset=bass.IndirectOffsetOnAxis(ap=dest[:, i:i + 1], axis=0),
                    in_=y1buf[:, i // 2 % 2, i % 2, :], in_offset=None).then_inc(y1_out[i % 4], 16)
            pool_slots(pool, SLOT1, 8, gather, send)

        def sp_rest(sp):
            store_rows(sp, xs0, pay, 1)
            for k in range(2):
                sp.wait_ge(y_out[k], 16 * ((SLOT0 + 1 - k) // 2))
            for k in range(len(RUNS)):
                take_back(sp, ys0, 0, back, k)
            sp_attention(sp)
            sp_layer1(sp)

        def act_rest(act, roots):
            roots(5)
            act_dispatch(act, (1, 0), x2T, 0)
            act.wait_ge(logits_ready, 1)
            nc.scalar.activation(rb[:, :, :], ra[:, :, :], ACT.Sigmoid).then_inc(sig_ready, 1)
            act.wait_ge(scale_ready, 1)
            act_experts0(act)
            act_attention(act, roots)
            act_layer1(act, roots)

        def pe_rest(pe):
            pe_route(pe, (1, 0), x2T, pay, wr0, 12, 0)
            pe_scale(pe, 0)
            pe_count(pe, 0)
            pe_slots(pe, 0, NT, SLOT0, inrow0, intile0)
            pe.wait_ge(stage_free, AHEAD + XW // CW)
            pe.wait_ge(slots_ready, 1)
            pe.wait_ge(dest_ready, 1)
            pe_experts0(pe)
            pe_attention(pe)
            pe_layer1(pe)

        def pool_rest(pool):
            pool_slots0(pool)
            for k in BACK_POOL:
                t, n, r = RUNS[k]
                pool.wait_ge(taken_back[k], 16)
                nc.gpsimd.tensor_tensor(h[0:r, t:t + n, :], h[0:r, t:t + n, :], back[0:r, t:t + n, :], ALU.add)\
                    .then_inc(added_pool, 1)
            pool_attention(pool)
            pool_layer1(pool)

        def dve_rest(dve, chain, inverse_roots):
            moments_of_all(dve, chain, 1)
            inverse_roots()
            dve_norm(dve, pay)
            dve.wait_ge(stage_free, AHEAD + XW // CW)
            gate_up = w0h.rearrange("p (e n) -> p e n", e=G0 * E0)[:, :, 0:2 * KC * F0]
            dve_bound(dve, chain, gate_up, lambda a_: None)
            dve_scale(dve, chain, 0)
            dve.wait_ge(route_psum, NT)
            nc.vector.tensor_copy(upper[:, :], k_upper)
            nc.vector.tensor_copy(ra[:, :, :], PS[:, 6, 0:12 * NT].rearrange("p (t g) -> p g t", g=12))\
                .then_inc(logits_ready, 1)
            dve.wait_ge(logits_ready, 1)
            top, score, a, b = rc[:, 8, :], rc[:, 9, :], rc[:, 10, :], rc[:, 11, :]
            chain.link(nc.vector.tensor_scalar(rc[:, 0:4, :], ra[:, 0:4, :], SAT, None, ALU.min))
            first_max(chain, rc[:, 0:4, :], top, oh[:, 0])
            dve.wait_ge(sig_ready, 1)
            chain.link(nc.vector.tensor_reduce(score, rb[:, 0:4, :].rearrange("p g t -> p t g"), AX, ALU.max))
            chain.link(nc.vector.tensor_scalar(a, score, 1e-9, None, ALU.add))
            chain.link(nc.vector.reciprocal(a, a))
            chain.link(nc.vector.tensor_tensor(score, score, a, ALU.mult))
            u = ra[:, 0:2, :]
            micro = rb[:, 4:12, :].rearrange("p (g e) t -> p e g t", e=E0)
            for e in range(E0):
                chain.link(nc.vector.tensor_tensor(rc[:, 0:4, :], micro[:, e], oh[:, 0], ALU.mult))
                sum_over(chain, u[:, e, :], rc[:, 0:4, :])
            chain.link(nc.vector.tensor_tensor(a, u[:, 0, :], u[:, 1, :], ALU.add))
            chain.link(nc.vector.tensor_scalar(a, a, 1e-9, None, ALU.add))
            chain.link(nc.vector.reciprocal(a, a))
            chain.link(nc.vector.tensor_tensor(a, a, score, ALU.mult))
            for e in range(E0):
                chain.link(nc.vector.tensor_tensor(pay[:, :, D + e], u[:, e, :], a, ALU.mult))
            dve.sem_inc(pay_ready, 1)
            positions(dve, chain, 1, SLOT0, 0, inrow0, intile0, 1)
            dve_experts0(dve)
            for k in BACK_DVE + BACK_POOL:
                t, n, r = RUNS[k]
                if k in BACK_DVE:
                    dve.wait_ge(taken_back[k], 16)
                    nc.vector.tensor_tensor(h[0:r, t:t + n, :], h[0:r, t:t + n, :], back[0:r, t:t + n, :], ALU.add)\
                        .then_inc(added_back, 1)
                    dve.wait_ge(added_back, BACK_DVE.index(k) + 1)
                else:
                    dve.wait_ge(added_pool, BACK_POOL.index(k) + 1)
                for i in range(t, t + n):
                    nc.vector.bn_stats(stats[:, i, 0, :], h[:, i, :]).then_inc(stats_ready, 1)
            dve_attention(dve, chain, inverse_roots)
            dve_layer1(dve, chain, inverse_roots)

        NF = 2 * NT

        def sp_attention(sp):
            sp.wait_ge(y_done, SLOT0)
            sp.dma_start(X[:, 0:NATT], wattn).then_inc(attn_loaded, 16)
            sp.dma_start(rowsF.rearrange("p a n -> p (a n)"), rows_f.broadcast_to([P, 2 * D])).then_inc(attn_loaded, 16)
            sp.dma_start(small1, wsmall1).then_inc(small1_loaded, 16)
            sp.dma_start(b2all.rearrange("p a n -> p (a n)"), b2rows.broadcast_to([P, E1 * D])).then_inc(small1_loaded, 16)
            first = XW // CW
            sp.wait_ge(added_back, len(BACK_DVE))
            sp.wait_ge(added_pool, len(BACK_POOL))
            with sp.Fori(0, W1W // CW // 2) as n:
                for k in range(2):
                    sp.wait_ge(stage_free, first + 2 * n + (k + 1))
                    sp.dma_start(stage[:, k, :], w1[:, bass.ds((2 * n + k) * CW, CW)]).then_inc(stage_full[k], 16)

        def heads(eng, body):
            body(0, 0)
            body(1, 1)
            with eng.Fori(1, BATCH // 2 - 1) as j:
                body(2 * j, 0)
                body(2 * j + 1, 1)
            body(BATCH - 2, 0)
            body(BATCH - 1, 1)

        def pe_attention(pe):
            pe.wait_ge(attn_loaded, 32)
            for n in range(IT):
                pe.wait_ge(xn_ready, NF + n + 1)
                if n:
                    pe.wait_ge(xTi_copied, n)
                for k in range(KC):
                    ins = nc.tensor.transpose(PS[:, 7, k * P:(k + 1) * P], xnF[:, n % 2, k * P:(k + 1) * P], k_ident)
                ins.then_inc(xn_tr, 1)

            def text(b, slot):
                pe.wait_ge(xn_ready, NF + IT + b + 1)
                if known(b, 0):
                    pe.wait_ge(xTi_copied, IT)
                else:
                    pe.wait_ge(xTb_copied, b)
                for k in range(KC):
                    ins = nc.tensor.transpose(PS[:, 7, k * P:(k + 1) * P], xnF[:, slot, k * P:(k + 1) * P], k_ident)
                ins.then_inc(xn_tr, 1)

            def project(b, slot):
                pe.wait_ge(xTb_copied, b + 1)
                pe.wait_ge(xTb_image, b + 1)
                for bank, w_, done in ((0, wq, q_psum), (1, wk, k_psum)):
                    for m in range(KC):
                        for k in range(KC):
                            ins = nc.tensor.matmul(PS[:, bank, m * SEQ:(m + 1) * SEQ], w_[:, k, m * P:(m + 1) * P],
                                                   xTb[:, slot, k, :], start=(k == 0), stop=(k == KC - 1))
                    ins.then_inc(done, 1)
                wait_from(pe, v_copied, b)
                for a, (c0, c1) in enumerate(((0, P), (P, SEQ))):
                    for k in range(KC):
                        ins = nc.tensor.matmul(PS[0:c1 - c0, 2, a * D:(a + 1) * D], xTb[:, slot, k, c0:c1], wv[:, k, :],
                                               start=(k == 0), stop=(k == KC - 1))
                ins.then_inc(v_psum, 1)

            def scores(b, slot):
                pe.wait_ge(rope_done, 2 * b + 2)
                for o_, q0, q1, k1 in ((0, 0, P, P), (P, P, SEQ, SEQ)):
                    for m in range(KC):
                        ins = nc.tensor.matmul(PS[0:q1 - q0, 3, o_:o_ + k1], qT[:, slot, m, q0:q1], kT[:, slot, m, 0:k1],
                                               start=(m == 0), stop=(m == KC - 1))
                ins.then_inc(s_psum, 1)

            def transpose_p(b, slot):
                pe.wait_ge(p_normed, b + 1)
                nc.tensor.transpose(PS[:, 4, 0:P], pA, k_ident)
                nc.tensor.transpose(PS[:, 4, P:SEQ], pB[0:SEQ - P, 0:P], k_ident[0:SEQ - P, 0:SEQ - P])
                nc.tensor.transpose(PS[0:SEQ - P, 4, SEQ:2 * SEQ - P], pB[0:SEQ - P, P:SEQ],
                                    k_ident[0:SEQ - P, 0:SEQ - P]).then_inc(pt_psum, 1)

            def values(b, slot):
                pe.wait_ge(pt_copied, b + 1)
                pe.wait_ge(v_copied, b + 1)
                for m in range(KC):
                    nc.tensor.matmul(PS[:, 5, m * SEQ:(m + 1) * SEQ], vb[:, slot, 0, m * P:(m + 1) * P], pT1,
                                     start=True, stop=False)
                    ins = nc.tensor.matmul(PS[:, 5, m * SEQ + P:(m + 1) * SEQ], vb[0:SEQ - P, slot, 1, m * P:(m + 1) * P],
                                           pT2[0:SEQ - P, :], start=False, stop=True)
                ins.then_inc(ot_psum, 1)

            def out_text(b, slot):
                pe.wait_ge(ot_copied, 2 * b + 2)
                wait_from(pe, h3_added, b)
                for m in range(KC):
                    ins = nc.tensor.matmul(PS[:, 6, 0:D], oTb[:, m, :], wf[:, m, :], start=(m == 0), stop=(m == KC - 1))
                ins.then_inc(pr_psum, 1)

            text(0, 0)
            text(1, 1)
            project(0, 0)

            def batch(b, slot):
                scores(b, slot)
                if not known(b, BATCH - 1):
                    project(b + 1, 1 - slot)
                transpose_p(b, slot)
                if not known(b, 0):
                    out_text(b - 1, 1 - slot)
                if not (isinstance(b, int) and b >= BATCH - 2):
                    text(b + 2, slot)
                values(b, slot)
            heads(pe, batch)
            out_text(BATCH - 1, 1)
            for n in range(IT):
                r = tile_rows(BATCH + n)
                if n == 0:
                    pe.wait_ge(h3_added, BATCH)
                for m in range(KC):
                    ins = nc.tensor.matmul(PS[0:r, 6 - n, 0:D], oTi[:, m, n * IROWS:n * IROWS + r], wf[:, m, :],
                                           start=(m == 0), stop=(m == KC - 1))
                ins.then_inc(pr_psum, 1)

        def act_attention(act, roots):
            roots(6)
            for n in range(IT):
                act.wait_ge(xn_tr, AHEAD + NF + n + 1)
                nc.scalar.activation(xTi[:, :, n * IROWS:(n + 1) * IROWS],
                                     PS[:, 7, 0:KC * P].rearrange("p (k r) -> p k r", k=KC)[:, :, 0:IROWS],
                                     ACT.Copy).then_inc(xTi_copied, 1)

            def text(b, slot):
                act.wait_ge(xn_tr, AHEAD + NF + IT + b + 1)
                nc.scalar.activation(xTb[:, slot, :, IMG:SEQ], PS[:, 7, 0:KC * P].rearrange("p (k r) -> p k r", k=KC),
                                     ACT.Copy).then_inc(xTb_copied, 1)

            def exps(b):
                act.wait_ge(s_max, b + 1)
                nc.scalar.activation(pA, sA1, ACT.Exp, bias=nmax[:, 0:1], scale=SCALE, accum_out=psum_[:, 0:1])
                nc.scalar.activation(pB[0:SEQ - P, :], sB1[0:SEQ - P, :], ACT.Exp, bias=nmax[0:SEQ - P, 1:2], scale=SCALE,
                                     accum_out=psum_[0:SEQ - P, 1:2]).then_inc(p_exp, 1)

            def copy_pt(b):
                act.wait_ge(pt_psum, b + 1)
                nc.scalar.activation(pT1, PS[:, 4, 0:SEQ], ACT.Copy)
                nc.scalar.activation(pT2[0:SEQ - P, :], PS[0:SEQ - P, 4, SEQ:2 * SEQ - P], ACT.Copy).then_inc(pt_copied, 1)

            def copy_ot(b):
                act.wait_ge(ot_psum, b + 1)
                o_ = PS[:, 5, 0:KC * SEQ].rearrange("p (k r) -> p k r", k=KC)
                nc.scalar.activation(oTb, o_[:, :, IMG:SEQ], ACT.Copy).then_inc(ot_copied, 1)
                nc.scalar.activation(oTi[:, :, bass.ds(b * IMG, IMG)], o_[:, :, 0:IMG], ACT.Copy).then_inc(ot_copied, 1)

            def chunk(n, k, j):
                act.wait_ge(stage_full[k], 16 * (XW // CW // 2 + j + 1))
                nc.scalar.activation(w1h[:, bass.ds(n * CW, CW)], stage[:, k, :], ACT.Copy).then_inc(w_high, 1)

            act.wait_ge(small1_loaded, 32)
            nc.scalar.activation(gb1, c_b1c, ACT.Gelu).then_inc(gb_ready, 1)
            text(0, 0)
            text(1, 1)

            def run(b, slot, j):
                exps(b)
                copy_pt(b)
                if not (isinstance(b, int) and b >= BATCH - 2):
                    text(b + 2, slot)
                copy_ot(b)
                chunk(b, slot, j)
            run(0, 0, 0)
            run(1, 1, 0)
            with act.Fori(1, BATCH // 2 - 1) as j:
                run(2 * j, 0, j)
                run(2 * j + 1, 1, j)
            run(BATCH - 2, 0, BATCH // 2 - 1)
            run(BATCH - 1, 1, BATCH // 2 - 1)

        def pool_attention(pool):
            pool.wait_ge(attn_loaded, 32)
            pool.wait_ge(xTi_copied, IT)

            def image(b):
                pool.wait_ge(xn_tr, AHEAD + NF + IT + b + 1)
                nc.gpsimd.tensor_copy(xTb[:, b % 2, :, 0:IMG], xTi[:, :, b * IMG:(b + 1) * IMG]).then_inc(xTb_image, 1)

            def rope(b):
                for i in range(2):
                    pool.wait_ge(rope_mul, 2 * b + i + 1)
                    nc.gpsimd.tensor_tensor(qkT[:, b % 2, i], tcos[:, i], tsin[:, i], ALU.add).then_inc(rope_done, 1)

            def bias(b):
                pool.wait_ge(xn_ready, NF + IT + b + 1)
                nc.gpsimd.tensor_tensor(h[:, b, :], h[:, b, :], rowsF[:, 1, :], ALU.add).then_inc(bf_added, 1)

            def low(n):
                k = n % 2
                pool.wait_ge(w_high, XW // CW - ALONE + n + 1)
                nc.gpsimd.tensor_tensor(w1l[:, n * CW:(n + 1) * CW], stage[:, k, :], w1h[:, n * CW:(n + 1) * CW],
                                        ALU.subtract).then_inc(stage_free, 1)
            for n in range(IT):
                pool.wait_ge(xn_ready, NF + n + 1)
                nc.gpsimd.tensor_tensor(h[:, BATCH + n, :], h[:, BATCH + n, :], rowsF[:, 1, :], ALU.add)\
                    .then_inc(bf_added, 1)
            image(0)
            image(1)
            bias(0)
            bias(1)
            rope(0)
            for b in range(BATCH):
                if b < BATCH - 1:
                    rope(b + 1)
                if b < BATCH - 2:
                    image(b + 2)
                    bias(b + 2)
                low(b)

        def dve_attention(dve, chain, inverse_roots):
            moments_of_all(dve, chain, 2)
            inverse_roots()
            dve.wait_ge(y_done, SLOT0)

            def norm(n, t, slot):
                dve.wait_ge(xn_tr, NF + n + 1)
                nc.vector.tensor_scalar(xnF[:, slot:slot + 1, :], h[:, bass.ds(t, 1), :], mv[:, bass.ds(t, 1), 0],
                                        rstd[:, bass.ds(t, 1)], ALU.subtract, ALU.mult).then_inc(xn_ready, 1)
            for n in range(IT):
                norm(n, BATCH + n, n % 2)
            dve.wait_ge(attn_loaded, 32)

            def rope(b):
                for i, (bank, bias, done) in enumerate(((0, c_bq, q_psum), (1, c_bk, k_psum))):
                    dve.wait_ge(done, b + 1)
                    for m in range(KC):
                        nc.vector.scalar_tensor_tensor(out=tcos[:, i, m, :], in0=PS[:, bank, m * SEQ:(m + 1) * SEQ],
                                                       scalar=bias[:, m:m + 1], in1=k_cos, op0=ALU.add, op1=ALU.mult)
                        ins = nc.vector.scalar_tensor_tensor(
                            out=tsin[:, i, m, :], in0=PS[:, bank, (1 - m) * SEQ:(2 - m) * SEQ],
                            scalar=bias[:, 1 - m:2 - m], in1=k_sin if m else k_nsin, op0=ALU.add, op1=ALU.mult)
                    ins.then_inc(rope_mul, 1)

            def copy_v(b, slot):
                dve.wait_ge(v_psum, b + 1)
                nc.vector.tensor_tensor(vb[:, slot, 0, :], PS[:, 2, 0:D], rowsF[:, 0, :], ALU.add)
                nc.vector.tensor_tensor(vb[0:SEQ - P, slot, 1, :], PS[0:SEQ - P, 2, D:2 * D], rowsF[0:SEQ - P, 0, :],
                                        ALU.add).then_inc(v_copied, 1)

            def maxima(b):
                dve.wait_ge(s_psum, b + 1)
                nc.vector.tensor_tensor(sA1, PS[:, 3, 0:P], k_maskA, ALU.add)
                chain.link(nc.vector.tensor_tensor_reduce(sB1[0:SEQ - P, :], PS[0:SEQ - P, 3, P:P + SEQ],
                                                          k_maskB[0:SEQ - P, :], 1.0, -3e38, ALU.add, ALU.max,
                                                          smax[0:SEQ - P, 1:2]))
                chain.link(nc.vector.tensor_reduce(smax[:, 0:1], sA1, AX, ALU.max))
                nc.vector.tensor_scalar(nmax, smax, -SCALE, None, ALU.mult).then_inc(s_max, 1)

            def normalise_p(b):
                dve.wait_ge(p_exp, b + 1)
                chain.link(nc.vector.reciprocal(rsum, psum_))
                nc.vector.tensor_scalar(pA, pA, rsum[:, 0:1], None, ALU.mult)
                nc.vector.tensor_scalar(pB[0:SEQ - P, :], pB[0:SEQ - P, :], rsum[0:SEQ - P, 1:2], None, ALU.mult)\
                    .then_inc(p_normed, 1)

            def add_text(b):
                dve.wait_ge(bf_added, IT + b + 1)
                dve.wait_ge(pr_psum, b + 1)
                hb = h[:, bass.ds(b, 1), :]
                nc.vector.tensor_tensor(hb, PS[:, 6, 0:D].unsqueeze(1), hb, ALU.add).then_inc(h3_added, 1)
                dve.wait_ge(h3_added, b + 1)
                nc.vector.bn_stats(stats[:, bass.ds(b, 1), 0, :], hb).then_inc(stats_ready, 1)

            chain.link(nc.vector.memset(smax[:, :], 0.0))
            chain.link(nc.vector.memset(psum_[:, :], 1.0))
            dve.wait_ge(gb_ready, 1)
            chain.link(nc.vector.tensor_copy(gbh, gb1))
            nc.vector.tensor_tensor(gbl, gb1, gbh, ALU.subtract).then_inc(gb_split, 1)
            norm(IT, 0, 0)
            norm(IT + 1, 1, 1)
            rope(0)
            copy_v(0, 0)

            def batch(b, slot):
                maxima(b)
                if not (isinstance(b, int) and b >= BATCH - 2):
                    norm(b + (IT + 2), b + 2, slot)
                normalise_p(b)
                if not known(b, BATCH - 1):
                    rope(b + 1)
                    copy_v(b + 1, 1 - slot)
                if not known(b, 0):
                    add_text(b - 1)
            batch(0, 0)
            batch(1, 1)
            with dve.Fori(1, BATCH // 2 - 1) as j:
                chain.begin(j - 1, 6)
                batch(2 * j, 0)
                batch(2 * j + 1, 1)
                chain.end(BATCH // 2 - 2)
            batch(BATCH - 2, 0)
            batch(BATCH - 1, 1)
            add_text(BATCH - 1)
            for n in range(IT):
                r = tile_rows(BATCH + n)
                dve.wait_ge(pr_psum, BATCH + n + 1)
                hb = h[0:r, BATCH + n, :]
                nc.vector.tensor_tensor(hb, PS[0:r, 6 - n, 0:D], hb, ALU.add).then_inc(h3_added, 1)
                dve.wait_ge(h3_added, BATCH + n + 1)
                nc.vector.bn_stats(stats[:, BATCH + n, 0, :], h[:, BATCH + n, :]).then_inc(stats_ready, 1)

        def sp_layer1(sp):
            sp.wait_ge(h3_added, NT)
            store_rows(sp, xs1, pay1, 2)
            for k in range(4):
                sp.wait_ge(y1_out[k], 16 * ((SLOT1 + 3 - k) // 4))
            for k in OUT_LOADS:
                take_back(sp, ys1, 0, back0, k)
                take_back(sp, ys1, 1, back1, k)

        def act_layer1(act, roots):
            roots(7)
            act_dispatch(act, (3, 1), x2G, 1)
            act.wait_ge(logits_ready, 3)
            nc.scalar.activation(rb[:, 0, :], rb[:, 1, :], ACT.Exp).then_inc(sig_ready, 1)
            act.wait_ge(c_psum, 2)
            for i, bank in enumerate(C_BANKS):
                nc.scalar.activation(rest1[:, 2 * i:2 * i + 2, :], PS[:, bank, :].rearrange("p (e n) -> p e n", e=2),
                                     ACT.Copy).then_inc(c_copied, 1)
            act.wait_ge(scale_ready, 2)
            act_experts1(act)

        def pe_layer1(pe):
            pe.wait_ge(small1_loaded, 32)

            def biases_out(first):
                for e in (first, first + 1):
                    n = 0
                    for c in range(F1 // P):
                        off = e * W1N + KC * F1 + c * D
                        for g_, w_ in ((gbh, w1h), (gbh, w1l), (gbl, w1h)):
                            left = g_[:, e * (F1 // P) + c:e * (F1 // P) + c + 1].broadcast_to([P, P])
                            ins = nc.tensor.matmul(PS[:, C_BANKS[first // 2], (e % 2) * D:(e % 2 + 1) * D], left,
                                                   w_[:, off:off + D], start=(n == 0), stop=(n == 3 * (F1 // P) - 1))
                            n += 1
                ins.then_inc(c_psum, 1)
            pe.wait_ge(stage_free, AHEAD + XW // CW + W1W // CW)
            pe.wait_ge(gb_split, 1)
            biases_out(0)
            pe_route(pe, (3, 1), x2G, pay1, wr1, 4, 1)
            pe_scale(pe, 1)
            biases_out(2)
            pe_count(pe, 1)
            pe_slots(pe, 1, TOPK * NT, SLOT1, inrow1, intile1)
            pe.wait_ge(slots_ready, 2)
            pe.wait_ge(dest_ready, 2)
            pe_experts1(pe)

        def pool_layer1(pool):
            chain = Chain(pool, rest_ready)
            pool.wait_ge(c_copied, 2)
            chain.link(nc.gpsimd.tensor_tensor(rest1, rest1, b2all, ALU.add))
            chain.link(nc.gpsimd.tensor_tensor(csum, rest1[:, 0, :], rest1[:, 1, :], ALU.add))
            for e in (2, 3):
                chain.link(nc.gpsimd.tensor_tensor(csum, csum, rest1[:, e, :], ALU.add))
            chain.link(nc.gpsimd.tensor_tensor(rest1, b2all, rest1, ALU.subtract))
            chain.link(nc.gpsimd.tensor_tensor(rest1, rest1, csum.unsqueeze(1).broadcast_to([P, E1, D]), ALU.add))
            pool_slots1(pool)
            add_both(pool, nc.gpsimd, OUT_POOL, added_pool, len(BACK_POOL))

        def dve_layer1(dve, chain, inverse_roots):
            moments_of_all(dve, chain, 3)
            inverse_roots()
            dve_norm(dve, pay1)
            def add_bias(a_):
                chain.link(nc.vector.tensor_reduce(amax[:, 3:4], c_b1c, AX, ALU.max, apply_absolute_value=True))
                chain.link(nc.vector.scalar_tensor_tensor(out=a_, in0=a_, scalar=float(D), in1=amax[:, 3:4],
                                                          op0=ALU.mult, op1=ALU.add))
            dve.wait_ge(stage_free, AHEAD + XW // CW + W1W // CW)
            dve_bound(dve, chain, w1h.rearrange("p (e n) -> p e n", e=E1)[:, :, 0:KC * F1], add_bias)
            dve_scale(dve, chain, 1)
            dve.wait_ge(route_psum, 2 * NT)
            lg, l2 = ra[:, 0:4, :], ra[:, 4:8, :]
            nc.vector.tensor_tensor(lg, PS[:, 6, 0:4 * NT].rearrange("p (t g) -> p g t", g=4),
                                    c_br.unsqueeze(2).broadcast_to([P, 4, NT]), ALU.add).then_inc(logits_ready, 1)
            dve.wait_ge(logits_ready, 2)
            v1, v2 = ra[:, 8, :], ra[:, 9, :]
            first_max(chain, lg, v1, oh[:, 0])
            chain.link(nc.vector.scalar_tensor_tensor(out=l2, in0=oh[:, 0], scalar=-1e30, in1=lg, op0=ALU.mult, op1=ALU.add))
            first_max(chain, l2, v2, oh[:, 1])
            nc.vector.tensor_tensor(rb[:, 1, :], v2, v1, ALU.subtract).then_inc(logits_ready, 1)
            dve.wait_ge(sig_ready, 2)
            ga, gb_ = gates[:, 0, :], gates[:, 1, :]
            chain.link(nc.vector.tensor_scalar(ra[:, 10, :], rb[:, 0, :], 1.0, None, ALU.add))
            chain.link(nc.vector.reciprocal(ga, ra[:, 10, :]))
            chain.link(nc.vector.tensor_tensor(gb_, ga, rb[:, 0, :], ALU.mult))
            chain.link(nc.vector.tensor_tensor(rb[:, 4:8, :], oh[:, 0], over(ga, 4), ALU.mult))
            chain.link(nc.vector.tensor_tensor(rb[:, 8:12, :], oh[:, 1], over(gb_, 4), ALU.mult))
            chain.link(nc.vector.tensor_tensor(rb[:, 4:8, :], rb[:, 4:8, :], rb[:, 8:12, :], ALU.add))
            chain.link(nc.vector.tensor_copy(pay1[:, :, D:PAY1], rb[:, 4:8, :].rearrange("p g t -> p t g")))
            dve.sem_inc(pay_ready, 1)
            positions(dve, chain, TOPK, SLOT1, 1, inrow1, intile1, 2)
            dve.wait_ge(rest_ready, 6)
            dve_experts1(dve)
            add_both(dve, nc.vector, OUT_DVE, added_back, len(BACK_DVE))

        def add_both(eng, engine, runs, done, before):
            for i, k in enumerate(runs):
                t, n, r = RUNS[k]
                eng.wait_ge(taken_back[k], 16 * 3)
                for c, part in enumerate((back0, back1)):
                    engine.tensor_tensor(h[0:r, t:t + n, :], h[0:r, t:t + n, :], part[0:r, t:t + n, :], ALU.add)\
                        .then_inc(done, 1)
                    eng.wait_ge(done, before + 2 * i + c + 1)

        @block.sync
        def _(sp):
            sp.dma_start(pt[0:IPAD, :, :], patches.rearrange("j r f -> r j f")).then_inc(patches_loaded, 16)
            sp.dma_start(wt, wtok).then_inc(small_loaded, 16)
            sp.dma_start(ccols[:, 0:20], cols).then_inc(small_loaded, 16)
            sp.dma_start(rows.rearrange("p a n -> p (a n)"), rows_a.broadcast_to([P, 6 * D])).then_inc(small_loaded, 16)
            sp.dma_start(cst[:, :], consts).then_inc(small_loaded, 16)
            sp.dma_start(petab[0:IPAD, :], pe_table).then_inc(small_loaded, 16)
            sp.dma_start(wsm[:, :], wsmall).then_inc(small_loaded, 16)
            sp.dma_start(h[:, 0:BATCH, :], txt.rearrange("b s d -> s b d")).then_inc(text_loaded, 16)
            with sp.Fori(0, XW // CW // 2) as n:
                for k in range(2):
                    sp.wait_ge(stage_free, 2 * n + (k + 1))
                    sp.dma_start(stage[:, k, :], w0[:, bass.ds((2 * n + k) * CW, CW)]).then_inc(stage_full[k], 16)
            sp_rest(sp)
            store_out(sp)

        def split_chunks(pool, hi, lo, words, first):
            for n in range(first, first + words // CW):
                cols_ = slice((n - first) * CW, (n - first + 1) * CW)
                if first == 0 and n == XNT_CHUNK:
                    pool.wait_ge(xn_tr, AHEAD + BATCH)
                if IT <= n < IT + ALONE:
                    pool.wait_ge(stage_full[n % 2], 16 * (n // 2 + 1))
                    nc.gpsimd.tensor_copy(hi[:, cols_], stage[:, n % 2, :]).then_inc(own_high, 1)
                    pool.wait_ge(own_high, n - IT + 1)
                else:
                    pool.wait_ge(w_high, n + 1 if n < IT else n + 1 - ALONE)
                nc.gpsimd.tensor_tensor(lo[:, cols_], stage[:, n % 2, :], hi[:, cols_], ALU.subtract)\
                    .then_inc(stage_free, 1)

        @block.gpsimd
        def _(pool):
            nc.gpsimd.memset(onesb[:, :], 1.0).then_inc(consts_ready, 1)
            nc.gpsimd.memset(onesf[:, :], 1.0).then_inc(consts_ready, 1)
            nc.gpsimd.memset(xT[:, :, BATCH * SEQ:], 0.0).then_inc(pads_zeroed, 1)
            pool.wait_ge(pads_zeroed, 1)
            nc.gpsimd.memset(h[96:P, BATCH:NT, :], 0.0).then_inc(pads_zeroed, 1)
            pool.wait_ge(pads_zeroed, 2)
            pool.sem_inc(stage_free, 2)
            split_chunks(pool, w0h, w0l, XW, 0)
            pool_rest(pool)

        @block.scalar
        def _(act):
            chain = Chain(act, act_done)
            pair_of = [0]

            def roots(n):
                act.wait_ge(var_ready, n)
                nc.scalar.activation(std, var, ACT.Sqrt).then_inc(std_ready, 1)

            def high_half(high, n, k, j):
                act.wait_ge(stage_full[k], 16 * (j + 1))
                nc.scalar.activation(high[:, bass.ds(n * CW, CW)], stage[:, k, :], ACT.Copy).then_inc(w_high, 1)

            act.wait_ge(small_loaded, 16 * NSMALL)
            chain.link(nc.scalar.activation(c_nega, c_alog, ACT.Exp))
            nc.scalar.mul(c_nega, c_nega, -1.0).then_inc(nega_ready, 1)
            roots(1)
            for j in range(IT):
                for half in range(2):
                    act.wait_ge(patch_tr, 2 * j + half + 1)
                    if j >= 2:
                        act.wait_ge(tok_psum, j - 1)
                    bank = PS[:, 1 + 2 * (j % 2) + half, 0:3 * IPAD].rearrange("p (c r) -> p c r", c=3)
                    nc.scalar.activation(pT[:, j % 2, 3 * half:3 * half + 3, :], bank, ACT.Copy)\
                        .then_inc(patch_copied, 1)
                high_half(w0h, j, j % 2, j // 2)
                if j == 3:
                    roots(2)
            act.sem_inc(xT_copied, AHEAD)

            def copy_xT(t, rows, slot):
                act.wait_ge(xn_tr, t + 1 + AHEAD)
                src = PS[:, slot, 0:KC * P].rearrange("p (k r) -> p k r", k=KC)[:, :, 0:rows]
                if rows != P:
                    src = src.rearrange("p k (b s) -> p k b s", s=IMG)
                nc.scalar.activation(batch_cols(xT, t, rows), src, ACT.Copy).then_inc(xT_copied, 1)

            act.wait_ge(pads_zeroed, 2)
            with act.Fori(0, BATCH // 4) as i:
                copy_xT(2 * i, P, 0)
                copy_xT(2 * i + 1, P, 1)
            roots(3)
            with act.Fori(BATCH // 4, BATCH // 2) as i:
                copy_xT(2 * i, P, 0)
                copy_xT(2 * i + 1, P, 1)
            roots(4)
            image_tiles(act, copy_xT)
            for n in range(9):
                g, c = n // 3, (n % 3) * 2 * SEQ
                act.wait_ge(bcd_psum, n + 1)
                nc.scalar.activation(sD[32 * g:32 * g + 32, c:c + 2 * SEQ], PS[64:96, n % 2 + 2, 0:2 * SEQ],
                                     ACT.Identity, bias=c_bcd[64:96, :]).then_inc(dl_copied, 1)
            act.wait_ge(dl_copied, 9)
            chain.link(nc.scalar.activation(sA[0:96, :], sD[0:96, :], ACT.Abs))
            chain.link(nc.scalar.activation(sA[0:96, :], sA[0:96, :], ACT.Exp, scale=-1.0))
            nc.scalar.activation(sA[0:96, :], sA[0:96, :], ACT.Ln, bias=1.0).then_inc(sp_ready, 1)
            act.wait_ge(delta_ready, 1)
            nc.scalar.activation(sA[0:96, :], sD[0:96, :], ACT.Exp, scale=c_nega).then_inc(decay_ready, 1)

            def gelu_z(t, rows, slot):
                for m in range(KC):
                    act.wait_ge(z_psum, t + 1)
                    ins = nc.scalar.activation(gT[:, slot, m, 0:rows], PS[:, 2 + slot, m * P:m * P + rows], ACT.Gelu,
                                               bias=c_bz[:, m:m + 1])
                ins.then_inc(g_ready, 1)

            first = IT + ALONE - 2 * BEFORE
            with act.Fori(0, BEFORE) as i:
                for k in range(2):
                    gelu_z(2 * i + k, P, k)
            with act.Fori(BEFORE, BEFORE + LATE // 2) as i:
                for k in range(2):
                    gelu_z(2 * i + k, P, k)
                    high_half(w0h, 2 * i + (k + first), k, i + first // 2)
            with act.Fori(BEFORE + LATE // 2, BATCH // 2) as i:
                for k in range(2):
                    gelu_z(2 * i + k, P, k)
            for t in range(BATCH, NT):
                gelu_z(t, tile_rows(t), t % 2)
            act_rest(act, roots)

        @block.tensor
        def _(pe):
            pe.wait_ge(small_loaded, 16 * NSMALL)
            for c in range(PC):
                ins = nc.tensor.matmul(PS[:, 0, 0:D], c_b1[:, c:c + 1].broadcast_to([P, P]), wt[:, c, :],
                                       start=(c == 0), stop=(c == PC - 1))
            ins.then_inc(tokb_psum, 1)

            def tok_matmul(j):
                pe.wait_ge(patch_copied, 2 * j + 2)
                if j == 0:
                    pe.wait_ge(wt_scaled, 1)
                if j >= 2:
                    pe.wait_ge(tok_added, j - 1)
                for c in range(PC):
                    ins = nc.tensor.matmul(PS[0:IPAD, 5 + j % 2, 0:D], pT[:, j % 2, c, :], wt[:, c, :],
                                           start=(c == 0), stop=(c == PC - 1))
                ins.then_inc(tok_psum, 1)

            for j in range(IT):
                pe.wait_ge(patch_normed, j + 1)
                if j >= 2:
                    pe.wait_ge(patch_copied, 2 * j - 2)
                for half in range(2):
                    for c in range(3):
                        ins = nc.tensor.transpose(PS[:, 1 + 2 * (j % 2) + half, c * IPAD:(c + 1) * IPAD],
                                                  pt[0:IPAD, j, (3 * half + c) * P:(3 * half + c + 1) * P],
                                                  k_ident[0:IPAD, 0:IPAD])
                    ins.then_inc(patch_tr, 1)
                if j >= 1:
                    tok_matmul(j - 1)
            tok_matmul(IT - 1)

            pe.sem_inc(xn_tr, AHEAD)

            def tr(t, rows, slot, tokens=xn):
                pe.wait_ge(xn_ready, t + 1)
                pe.wait_ge(xT_copied, t + 1)
                for k in range(KC):
                    ins = nc.tensor.transpose(PS[:, slot, k * P:(k + 1) * P], tokens[:, slot, k * P:(k + 1) * P],
                                              k_ident)
                ins.then_inc(xn_tr, 1)
            for t in range(BATCH):
                tr(t, P, t % 2, xnt[:, t - t % 2:, :])
            image_tiles(pe, tr)
            for n in range(PB // 2):
                if n == 0:
                    pe.wait_ge(xT_copied, NT + AHEAD)
                if n >= 2:
                    pe.wait_ge(bc_copied, n - 1)
                    pe.wait_ge(dl_copied, n - 1)
                for k in range(KC):
                    ins = nc.tensor.matmul(PS[0:96, 2 + n % 2, 0:2 * SEQ], wbcd[:, k, :],
                                           xT[:, k, 2 * n * SEQ:2 * (n + 1) * SEQ], start=(k == 0), stop=(k == KC - 1))
                ins.then_inc(bcd_psum, 1)

            def scan_sum():
                pe.wait_ge(sc_ready, 2)
                for t in range(NT):
                    b0 = t if t < BATCH else (t - BATCH) * PER
                    g, b = b0 // SB, b0 % SB
                    nb = min(PER, BATCH - b0)
                    rows_ = P if t < BATCH else nb * IMG
                    c = SB * IMG + b * TEXT if t < BATCH else b * IMG
                    part = sA[32 * g:32 * g + 32, c:c + rows_]
                    ins = nc.tensor.matmul(PS[0:rows_, Y_BANKS[g], t:t + 1], part, onesf[32 * g:32 * g + 32, 0:1],
                                           start=True, stop=True)
                ins.then_inc(y_psum, 1)

            def z_matmul(t, rows, slot):
                for m in range(KC):
                    out_ = PS[:, 2 + slot, m * P:m * P + rows]
                    if rows != P:
                        out_ = out_.rearrange("p (b s) -> p b s", s=IMG)
                    for k in range(KC):
                        rhs = batch_cols(xT, t, rows)[:, k]
                        ins = nc.tensor.matmul(out_, wz[:, k, m * P:(m + 1) * P], rhs, start=(k == 0),
                                               stop=(k == KC - 1))
                ins.then_inc(z_psum, 1)

            def o_matmul(t, rows, slot):
                pe.wait_ge(g_ready, t + 1)
                pe.wait_ge(h_added, t + 1)
                for k in range(KC):
                    ins = nc.tensor.matmul(PS[0:rows, 4 + slot, 0:D], gT[:, slot, k, 0:rows], wout[:, k, :],
                                           start=(k == 0), stop=(k == KC - 1))
                ins.then_inc(o_psum, 1)

            pe.wait_ge(bc_copied, 9)
            pe.wait_ge(dl_copied, 9)
            z_matmul(0, P, 0)
            z_matmul(1, P, 1)
            scan_sum()
            o_matmul(0, P, 0)
            with pe.Fori(1, BATCH // 2) as i:
                z_matmul(2 * i, P, 0)
                o_matmul(2 * i - 1, P, 1)
                z_matmul(2 * i + 1, P, 1)
                o_matmul(2 * i, P, 0)
            for t in range(BATCH, NT):
                z_matmul(t, tile_rows(t), t % 2)
                o_matmul(t - 1, tile_rows(t - 1), (t - 1) % 2)
            o_matmul(NT - 1, tile_rows(NT - 1), (NT - 1) % 2)
            pe_rest(pe)

        @block.vector
        def _(dve):
            chain = Chain(dve, dve_done)
            ln_count = [0]

            def inverse_roots():
                nc.vector.tensor_scalar(var, mv[:, :, 1], EPS, None, ALU.add).then_inc(var_ready, 1)
                ln_count[0] += 1
                dve.wait_ge(std_ready, ln_count[0])
                chain.link(nc.vector.reciprocal(rstd, std))
                chain.link(nc.vector.tensor_tensor(newt, rstd, rstd, ALU.mult))
                chain.link(nc.vector.tensor_tensor(newt, newt, var, ALU.mult))
                chain.link(nc.vector.tensor_scalar(newt, newt, -0.5, 1.5, ALU.mult, ALU.add))
                chain.link(nc.vector.tensor_tensor(rstd, rstd, newt, ALU.mult))

            chain.link(nc.vector.memset(mv[:, :, :], 0.0))
            dve.wait_ge(patches_loaded, 16)
            for j in range(IT):
                for half in range(2):
                    ins = nc.vector.bn_stats(stats[0:IPAD, BATCH + j, half, :], pt[0:IPAD, j, half * 384:(half + 1) * 384])
            chain.link(ins)
            for j in range(IT):
                ins = nc.vector.bn_aggr(mv[0:IPAD, BATCH + j, :], stats[0:IPAD, BATCH + j, :, :].rearrange("p a b -> p (a b)"))
            chain.link(ins)
            inverse_roots()
            for j in range(IT):
                nc.vector.tensor_scalar(pt[0:IPAD, j, :], pt[0:IPAD, j, :], mv[0:IPAD, BATCH + j, 0:1],
                                        rstd[0:IPAD, BATCH + j:BATCH + j + 1],
                                        ALU.subtract, ALU.mult).then_inc(patch_normed, 1)
            dve.wait_ge(tokb_psum, 1)
            chain.link(nc.vector.tensor_tensor(r_tb, PS[:, 0, 0:D], r_tb, ALU.add))
            for c in range(PC):
                ins = nc.vector.tensor_scalar(wt[:, c, :], wt[:, c, :], c_g1[:, c:c + 1], None, ALU.mult)
            ins.then_inc(wt_scaled, 1)
            chain.link(nc.vector.tensor_tensor(r_cls, r_cls, r_cpos, ALU.add))
            for row_, at_rows in ((r_b2, k_patch), (r_cls, k_class)):
                chain.link(nc.vector.scalar_tensor_tensor(out=petab[0:IPAD, :], in0=row_[0:IPAD, :], scalar=at_rows[0:IPAD, :],
                                                          in1=petab[0:IPAD, :], op0=ALU.mult, op1=ALU.add))
            dve.wait_ge(text_loaded, 16)
            for t in range(BATCH):
                ins = nc.vector.bn_stats(stats[:, t, 0, :], h[:, t, :])
            chain.link(ins)

            def add_patches(j):
                dve.wait_ge(tok_psum, j + 1)
                nc.vector.tensor_tensor(h[0:IPAD, BATCH + j, :], PS[0:IPAD, 5 + j % 2, 0:D], r_tb[0:IPAD, :],
                                        ALU.add).then_inc(tok_added, 1)

            dve.wait_ge(pads_zeroed, 2)
            add_patches(0)
            add_patches(1)
            for t in range(BATCH):
                ins = nc.vector.bn_aggr(mv[:, t, :], stats[:, t, 0, :])
            chain.link(ins)
            inverse_roots()
            for j in range(IT):
                if j >= 2:
                    add_patches(j)
                for t in range(j * BATCH // IT, (j + 1) * BATCH // IT):
                    nc.vector.tensor_scalar(xnt[:, t, :], h[:, t, :], mv[:, t, 0:1], rstd[:, t:t + 1], ALU.subtract,
                                            ALU.mult).then_inc(xn_ready, 1)
            dve.wait_ge(tok_added, IT)
            for j in range(IT):
                ins = nc.vector.bn_stats(stats[0:IPAD, BATCH + j, 0, :], h[0:IPAD, BATCH + j, :])
            chain.link(ins)
            for j in range(IT):
                ins = nc.vector.bn_aggr(mv[0:IPAD, BATCH + j, :], stats[0:IPAD, BATCH + j, 0, :])
            chain.link(ins)
            inverse_roots()
            chain.link(nc.vector.tensor_scalar(rstd, rstd, k_patch, None, ALU.mult))
            for j in range(IT):
                ins = nc.vector.tensor_scalar(h[0:IPAD, BATCH + j, :], h[0:IPAD, BATCH + j, :],
                                              mv[0:IPAD, BATCH + j, 0:1], rstd[0:IPAD, BATCH + j:BATCH + j + 1],
                                              ALU.subtract, ALU.mult)
            chain.link(ins)
            image = h[0:IPAD, BATCH:NT, :]
            chain.link(nc.vector.tensor_tensor(image, image, r_g2[0:IPAD, :].unsqueeze(1).broadcast_to([IPAD, IT, D]),
                                               ALU.mult))
            nc.vector.tensor_tensor(image, image, petab[0:IPAD, :].unsqueeze(1).broadcast_to([IPAD, IT, D]),
                                    ALU.add).then_inc(tok_ready, 1)

            dve.wait_ge(tok_ready, 1)
            for t in range(BATCH, NT):
                ins = nc.vector.bn_stats(stats[:, t, 0, :], h[:, t, :])
            chain.link(ins)
            for t in range(BATCH, NT):
                ins = nc.vector.bn_aggr(mv[:, t, :], stats[:, t, 0, :])
            chain.link(ins)
            inverse_roots()

            def norm(t, rows, slot):
                dve.wait_ge(xn_tr, t + 1)
                nc.vector.tensor_scalar(xn[:, slot, :], h[:, bass.ds(t, 1), :], mv[:, bass.ds(t, 1), 0],
                                        rstd[:, bass.ds(t, 1)], ALU.subtract, ALU.mult).then_inc(xn_ready, 1)
            image_tiles(dve, norm)
            for n in range(9):
                g, c = n // 3, (n % 3) * 2 * SEQ
                dve.wait_ge(bcd_psum, n + 1)
                nc.vector.tensor_scalar(sB[32 * g:32 * g + 32, c:c + 2 * SEQ], PS[0:32, n % 2 + 2, 0:2 * SEQ],
                                        c_bcd[0:32, :], None, ALU.add)
                nc.vector.tensor_scalar(sC[32 * g:32 * g + 32, c:c + 2 * SEQ], PS[32:64, n % 2 + 2, 0:2 * SEQ],
                                        c_bcd[32:64, :], None, ALU.add).then_inc(bc_copied, 1)
            dve.wait_ge(bc_copied, 9)
            dve.wait_ge(sp_ready, 1)
            nc.vector.scalar_tensor_tensor(out=sD[0:96, :], in0=sD[0:96, :], scalar=0.0, in1=sA[0:96, :],
                                           op0=ALU.max, op1=ALU.add).then_inc(delta_ready, 1)
            dve.wait_ge(decay_ready, 1)
            chain.link(nc.vector.memset(sA[0:96, :].rearrange("p (b s) -> p b s", s=SEQ)[:, :, 0:1], 0.0))
            chain.link(nc.vector.tensor_tensor_scan(sS[0:96, :], sA[0:96, :], sB[0:96, :], 0.0, ALU.mult, ALU.add))
            for lo, hi, at_ in ((0, IMG, 0), (IMG, SEQ, SB * IMG)):
                state, cc = (v[0:96, :].rearrange("p (b s) -> p b s", s=SEQ)[:, :, lo:hi] for v in (sS, sC))
                nc.vector.tensor_tensor(sA[0:96, at_:at_ + SB * (hi - lo)].rearrange("p (b s) -> p b s", b=SB),
                                        state, cc, ALU.mult).then_inc(sc_ready, 1)
            dve.wait_ge(y_psum, 1)
            chain.link(nc.vector.memset(yv[:, :], 0.0))
            for t in range(NT):
                g = (t if t < BATCH else (t - BATCH) * PER) // SB
                rows_ = P if t < BATCH else IROWS if t < NT - 1 else LAST * IMG
                ins = nc.vector.tensor_copy(yv[0:rows_, t:t + 1], PS[0:rows_, Y_BANKS[g], t:t + 1])
            chain.link(ins)
            dve.sem_inc(h_added, AHEAD)

            def add_scan(t, rows, slot):
                ht = h[0:rows, bass.ds(t, 1), :]
                dve.wait_ge(o_psum, t + 1)
                nc.vector.scalar_tensor_tensor(out=ht, in0=PS[0:rows, 4 + slot, 0:D].unsqueeze(1),
                                               scalar=yv[0:rows, bass.ds(t, 1)], in1=ht, op0=ALU.mult, op1=ALU.add)\
                    .then_inc(h_added, 1)
                dve.wait_ge(h_added, t + 1 + AHEAD)
                nc.vector.tensor_tensor(ht, ht, r_bout[0:rows, :].unsqueeze(1), ALU.add).then_inc(hb_added, 1)
                dve.wait_ge(hb_added, t + 1)
                nc.vector.bn_stats(stats[:, bass.ds(t, 1), 0, :], h[:, bass.ds(t, 1), :]).then_inc(stats_ready, 1)
            token_tiles(dve, add_scan)
            dve_rest(dve, chain, inverse_roots)


def position_table():
    omega = np.arange(D // 4, dtype=np.float32) / np.float32(D // 4 - 1)
    omega = (np.float32(1.0) / np.float32(10000.0) ** omega).astype(np.float32)
    y, x = np.meshgrid(np.arange(GRID), np.arange(GRID), indexing="ij")
    y = y.reshape(-1)[:, None].astype(np.float32) * omega[None, :]
    x = x.reshape(-1)[:, None].astype(np.float32) * omega[None, :]
    pe = np.concatenate((np.sin(x), np.cos(x), np.sin(y), np.cos(y)), axis=1).astype(np.float32)
    table = np.zeros((IPAD, D), np.float32)
    for b in range(PER):
        table[b * IMG + 1:(b + 1) * IMG] = pe
    return table


def shape_constants():
    c = np.zeros((P, NCST), np.float32)
    c[:, 0:P] = np.eye(P)
    c[:, P:2 * P] = np.triu(np.ones((P, P)), 1)
    at = 2 * P
    valid = np.ones((P, NT))
    valid[IROWS:, BATCH:] = 0
    valid[LAST * IMG:, NT - 1] = 0
    c[:, at:at + NT] = valid; at += NT
    reset = np.ones((4, NT)); reset[:, 0] = 0
    c[:, at:at + 4 * NT] = reset.reshape(-1); at += 4 * NT
    c[:, at:at + 4 * NFULL] = np.tile(np.arange(NFULL) * P, 4); at += 4 * NFULL
    c[:, at:at + SLOT1] = np.arange(SLOT1); at += SLOT1
    c[:, at:at + NT] = (1 - valid) * 2.0 ** 20; at += NT
    c[:, at:at + TOPK * NT] = np.arange(TOPK * NT); at += TOPK * NT
    c[:, at:at + P] = np.arange(P); at += P
    c[:, at] = np.arange(P)
    c[:IROWS, at + 1] = np.arange(IROWS) % IMG != 0
    c[:IROWS, at + 2] = np.arange(IROWS) % IMG == 0
    return c


def chunks(w, parts):
    return w.reshape(parts, P, -1).transpose(1, 0, 2)


def rope_tables():
    freqs = (np.float32(1.0) / np.float32(10000.0) ** (np.arange(0, D, 2, dtype=np.float32) / np.float32(D)))
    ang = freqs.astype(np.float32)[:, None] * np.arange(SEQ, dtype=np.float32)[None, :]
    cos, sin = np.cos(ang).astype(np.float32), np.sin(ang).astype(np.float32)
    query, key = np.arange(P)[:, None], np.arange(SEQ)[None, :]
    mask_a = np.where(key[:, :P] <= query, 0.0, -1e30)
    mask_b = np.where(key <= query + P, 0.0, -1e30)
    return np.concatenate([cos, sin, -sin, mask_a, mask_b], 1).astype(np.float32)


def lay_out(i):
    f = {k: np.asarray(v) for k, v in i.items()}
    x = f["x"].reshape(BATCH, CH, GRID, PATCH, GRID, PATCH).transpose(0, 2, 4, 3, 5, 1).reshape(BATCH, IMG - 1, PDIM)
    pt = np.zeros((PB, IMG, PDIM), np.float32)
    pt[:BATCH, 1:] = x
    patches = np.zeros((IT, IPAD, PDIM), np.float32)
    patches[:, :IROWS] = pt.reshape(IT, IROWS, PDIM)
    w_in, b_in = f["L0_attn_W_in"], f["L0_attn_b_in"]
    cols = np.zeros((P, 20), np.float32)
    cols[:, 0:6] = f["L0_tok_ln1_g"].reshape(PC, P).T
    cols[:, 6:12] = f["L0_tok_ln1_b"].reshape(PC, P).T
    cols[:, 12:14] = b_in[D:2 * D].reshape(KC, P).T
    cols[:, 14:16] = f["L1_attn_bq"].reshape(P, 2)
    cols[:, 16:18] = f["L1_attn_bk"].reshape(P, 2)
    wbcd = np.zeros((D, 96), np.float32)
    for n in range(3):
        wbcd[:, 32 * n:32 * n + NS] = w_in[:, 2 * D + n * NS:2 * D + (n + 1) * NS]
        cols[32 * n:32 * n + NS, 18] = b_in[2 * D + n * NS:2 * D + (n + 1) * NS]
        cols[32 * n:32 * n + NS, 19] = f["L0_attn_A_log"]
    route = np.concatenate([f["L0_ffn_macro_w"], f["L0_ffn_micro_w"].transpose(1, 0, 2).reshape(D, G0 * E0)], 1)
    small = np.concatenate([chunks(w, KC).reshape(P, -1) for w in (wbcd, w_in[:, D:2 * D], f["L0_attn_W_out"], route)], 1)
    w0 = np.concatenate([np.concatenate([chunks(f["L0_ffn_gate_w"][e], KC).reshape(P, -1),
                                         chunks(f["L0_ffn_up_w"][e], KC).reshape(P, -1),
                                         chunks(f["L0_ffn_down_w"][e], F0 // P).reshape(P, -1)], 1)
                         for e in range(G0 * E0)], 1)
    halves = lambda w: np.concatenate([w.T[:, 0::2], w.T[:, 1::2]], 1)
    wattn = np.concatenate([chunks(w, KC).reshape(P, -1) for w in (
        halves(f["L1_attn_Wq"]), halves(f["L1_attn_Wk"]), f["L1_attn_Wv"].T, f["L1_attn_Wf"].T)] + [rope_tables()], 1)
    w1 = np.concatenate([np.concatenate(
        [chunks(f["L1_ffn_w1"][e][:, s * F0:(s + 1) * F0], KC).reshape(P, -1) for s in range(HF)]
        + [chunks(f["L1_ffn_w2"][e], F1 // P).reshape(P, -1)], 1) for e in range(E1)], 1)
    small1 = np.zeros((P, NSM1), np.float32)
    at = 4 * KC
    small1[:, 0:at] = chunks(f["L1_ffn_wr"], KC).reshape(P, -1)
    small1[:, at:at + (F1 // P) * E1] = f["L1_ffn_b1"].reshape(E1, F1 // P, P).transpose(2, 0, 1).reshape(P, -1)
    at += (F1 // P) * E1
    small1[:, at:at + E1] = f["L1_ffn_br"]
    return {
        "wattn": wattn, "rows_f": np.concatenate([f["L1_attn_bv"], f["L1_attn_bf"]])[None], "w1": w1,
        "wsmall1": small1, "b2rows": f["L1_ffn_b2"].reshape(1, -1),
        "txt": f["txt"], "patches": patches, "wtok": chunks(f["L0_tok_W"], PC), "cols": cols,
        "rows_a": np.concatenate([f[k].reshape(-1) for k in (
            "L0_tok_ln2_g", "L0_tok_ln2_b", "L0_tok_bias", "L0_tok_cls_token", "L0_tok_cls_pos_embedding",
            "L0_attn_b_out")])[None],
        "consts": shape_constants(), "pe_table": position_table(), "wsmall": small, "w0": w0,
    }


def kernel(**inputs):
    import concourse.bacc as _bacc
    from concourse.bass_utils import run_bass_kernel_spmd as _run

    nc = _bacc.Bacc("TRN2", target_bir_lowering=False, num_devices=1)
    arrays, args = {}, {}
    for name, a in lay_out(inputs).items():
        a = np.ascontiguousarray(a)
        arrays[f"in_{name}_dram"] = a
        args[name] = nc.dram_tensor(f"in_{name}_dram", a.shape, mybir.dt.from_np(a.dtype), kind="ExternalInput").ap()
    out = nc.dram_tensor("out_0_dram", (BATCH, SEQ, D), F32, kind="ExternalOutput").ap()
    build(nc, out=out, **args)
    r = _run(nc, [arrays], core_ids=[0])
    return r.results[0]["out_0_dram"]
```
